# Optimizing a Trainium2 kernel written in Bass

```python
import numpy as np
import jax
import jax.numpy as jnp

def _softmax(x, axis=-1):
    return jax.nn.softmax(x, axis=axis)

def _gelu(x):
    return jax.nn.gelu(x, approximate=True)

def _silu(x):
    return jax.nn.silu(x)

def _sigmoid(x):
    return jax.nn.sigmoid(x)

def _layernorm(x, axis=-1, eps=1e-05):
    m = jnp.mean(x, axis=axis, keepdims=True)
    v = jnp.var(x, axis=axis, keepdims=True)
    return (x - m) / jnp.sqrt(v + eps)

def _scatter_add(tgt, idx, src, axis=0):
    return tgt.at[idx].add(src)

def _segment_sum(src, seg, n):
    return jax.ops.segment_sum(src, seg, n)
kernel_name = 'mk_perceiver_d2_seqx_r8_f87921'

def setup_inputs(seed: int=0):
    np.random.seed(seed)
    _w = jnp.asarray

    def _rec_inputs():
        import jax
        import jax.numpy as jnp
        _rk = jax.random.key(seed)
        x = -0.0002928 + 1 * jax.random.normal(jax.random.fold_in(_rk, 1), (16, 32, 128), jnp.float32)
        _lenS = 32 - jax.random.randint(jax.random.fold_in(_rk, 7), (16,), 0, max(1, 32 // 4) + 1, jnp.int32)
        _lenS2 = 512 - jax.random.randint(jax.random.fold_in(_rk, 8), (16,), 0, max(1, 512 // 4) + 1, jnp.int32)
        _ctx_1024P = jax.random.normal(jax.random.fold_in(_rk, 11), (16, 16, 128), jnp.float32)
        _ctx_1024c = jax.random.dirichlet(jax.random.fold_in(_rk, 511), 0.3 * jnp.ones((16,), jnp.float32), (16, 512))
        _ctx_1024t = jnp.einsum('bsk,bkd->bsd', _ctx_1024c, _ctx_1024P)
        _ctx_1024t = _ctx_1024t * jax.lax.rsqrt(jnp.mean(jnp.square(_ctx_1024t)) + 1e-12) * 0.953939
        ctx_1024 = 4.13588e-05 + 0.999923 * (_ctx_1024t + 0.3 * jax.random.normal(jax.random.fold_in(_rk, 611), (16, 512, 128), jnp.float32))
        _validS = jnp.arange(32)[None, :] < _lenS[:, None]
        _validS2 = jnp.arange(512)[None, :] < _lenS2[:, None]
        _causal = jnp.tril(jnp.ones((32, 32), dtype=bool))
        mask_Bx1xSxS2_fk0 = jnp.where(jnp.broadcast_to(_validS2[:, None, None, :], (16, 1, 32, 512)), 0.0, 1.0).astype(jnp.float32)
        return (x, ctx_1024, mask_Bx1xSxS2_fk0)
    x, ctx_1024, mask_Bx1xSxS2_fk0 = _rec_inputs()

    def _L0_xattn_setup():
        import jax, jax.numpy as jnp
        import numpy as np
        B, SQ, SK, D, H = (2, 256, 512, 128, 16)
        HD = D // H

        def _local_allowed_mask(num_q, num_k):
            kpq, extra = (num_k // num_q, num_k % num_q)
            i = jnp.arange(num_q)
            start = i * kpq + jnp.minimum(i, extra)
            end = start + kpq + (i < extra)
            j = jnp.arange(num_k)
            return (j[None, :] >= start[:, None]) & (j[None, :] < end[:, None])
        key = jax.random.key(seed)
        ks = jax.random.split(key, 6)
        s = 0.02
        return {'x': jax.random.normal(ks[0], (B, SQ, D), jnp.float32), 'c': jax.random.normal(ks[1], (B, SK, D), jnp.float32), 'Wq': jax.random.normal(ks[2], (D, D), jnp.float32) * s, 'bq': jnp.zeros((D,), jnp.float32), 'Wk': jax.random.normal(ks[3], (D, D), jnp.float32) * s, 'bk': jnp.zeros((D,), jnp.float32), 'Wv': jax.random.normal(ks[4], (D, D), jnp.float32) * s, 'bv': jnp.zeros((D,), jnp.float32), 'Wo': jax.random.normal(ks[5], (D, D), jnp.float32) * s, 'bo': jnp.zeros((D,), jnp.float32)}
    _L0_xattn_all = _L0_xattn_setup()
    _L0_xattn_in = {k: v for k, v in _L0_xattn_all.items() if k in ('Wq', 'bq', 'Wk', 'bk', 'Wv', 'bv', 'Wo', 'bo')}
    del _L0_xattn_all

    def _L0_attn_setup():
        import jax, jax.numpy as jnp
        import numpy as np
        B, T, C = (8, 256, 128)
        NEG = -1e+30

        def wkv(w, u, k, v):
            w_exp = -jnp.exp(w)
            p0 = jnp.zeros(k.shape[::2], k.dtype)
            q0 = jnp.zeros(k.shape[::2], k.dtype)
            o0 = jnp.full(k.shape[::2], NEG, k.dtype)

            def step(carry, kv_t):
                p, q, o = carry
                k_t, v_t = kv_t
                uk = u + k_t
                no = jnp.maximum(o, uk)
                A = jnp.exp(o - no)
                Bc = jnp.exp(uk - no)
                out = (A * p + Bc * v_t) / (A * q + Bc)
                wo = w_exp + o
                no2 = jnp.maximum(wo, k_t)
                A2 = jnp.exp(wo - no2)
                B2 = jnp.exp(k_t - no2)
                return ((A2 * p + B2 * v_t, A2 * q + B2, no2), out)
            kT = jnp.swapaxes(k, 0, 1)
            vT = jnp.swapaxes(v, 0, 1)
            _, outs = jax.lax.scan(step, (p0, q0, o0), (kT, vT))
            return jnp.swapaxes(outs, 0, 1)
        key = jax.random.key(seed)
        ks = jax.random.split(key, 5)
        x = jax.random.normal(ks[0], (B, T, C), dtype=jnp.float32)
        scales = jnp.arange(C, dtype=jnp.float32) / C
        Wk = jax.random.normal(ks[1], (C, C), dtype=jnp.float32) * 0.02
        Wv = jax.random.normal(ks[2], (C, C), dtype=jnp.float32) * 0.02
        Wr = jax.random.normal(ks[3], (C, C), dtype=jnp.float32) * 0.02
        Wo = jax.random.normal(ks[4], (C, C), dtype=jnp.float32) * 0.02
        return {'x': x, 'w': scales, 'u': scales, 'mix_k': scales, 'mix_v': scales, 'mix_r': scales, 'Wk': Wk, 'Wv': Wv, 'Wr': Wr, 'Wo': Wo}
    _L0_attn_all = _L0_attn_setup()
    _L0_attn_in = {k: v for k, v in _L0_attn_all.items() if k in ('w', 'u', 'mix_k', 'mix_v', 'mix_r', 'Wk', 'Wv', 'Wr', 'Wo')}
    del _L0_attn_all

    def _L0_ffn_setup():
        import jax, jax.numpy as jnp
        import numpy as np
        E = 8
        K = 2
        key = jax.random.key(seed)
        ks = jax.random.split(key, 8)
        B, T, d = (4, 256, 128)
        h = 4 * d // E
        s = 0.02
        X = jax.random.normal(ks[0], (B, T, d), jnp.float32)
        routing_W = jax.random.normal(ks[1], (E, d), jnp.float32) * s
        expert_bias = jnp.zeros((E,), jnp.float32)
        sW1 = jax.random.normal(ks[2], (d, h), jnp.float32) * s
        sb1 = jnp.zeros((h,), jnp.float32)
        sW2 = jax.random.normal(ks[3], (h, d), jnp.float32) * s
        sb2 = jnp.zeros((d,), jnp.float32)
        rW1 = jax.random.normal(ks[4], (E, d, h), jnp.float32) * s
        rb1 = jnp.zeros((E, h), jnp.float32)
        rW2 = jax.random.normal(ks[5], (E, h, d), jnp.float32) * s
        rb2 = jnp.zeros((E, d), jnp.float32)
        return dict(X=X, routing_W=routing_W, expert_bias=expert_bias, sW1=sW1, sb1=sb1, sW2=sW2, sb2=sb2, rW1=rW1, rb1=rb1, rW2=rW2, rb2=rb2)
    _L0_ffn_all = _L0_ffn_setup()
    _L0_ffn_in = {k: v for k, v in _L0_ffn_all.items() if k in ('routing_W', 'expert_bias', 'sW1', 'sb1', 'sW2', 'sb2', 'rW1', 'rb1', 'rW2', 'rb2')}
    del _L0_ffn_all

    def _L1_xattn_setup():
        import jax, jax.numpy as jnp
        import numpy as np
        B, L, D, H = (4, 256, 128, 16)
        HD = D // H
        NEG = -1000000000000000.0

        def _split_heads(x):
            b, l, _ = x.shape
            return x.reshape(b, l, H, HD).transpose(0, 2, 1, 3)
        key = jax.random.key(seed)
        ks = jax.random.split(key, 13)
        s = 1.0 / np.sqrt(D)
        inp = {'q': jax.random.normal(ks[0], (B, L, D), jnp.float32), 'k': jax.random.normal(ks[1], (B, L, D), jnp.float32), 'v': jax.random.normal(ks[2], (B, L, D), jnp.float32), 'mask': (jax.random.uniform(ks[3], (B, 1, L, L)) < 0.1).astype(jnp.float32), 'Wq': jax.random.normal(ks[4], (D, D), jnp.float32) * s, 'bq': jnp.zeros((D,), jnp.float32), 'Wk': jax.random.normal(ks[5], (D, D), jnp.float32) * s, 'bk': jnp.zeros((D,), jnp.float32), 'Wv': jax.random.normal(ks[6], (D, D), jnp.float32) * s, 'bv': jnp.zeros((D,), jnp.float32), 'Wo': jax.random.normal(ks[7], (D, D), jnp.float32) * s, 'bo': jnp.zeros((D,), jnp.float32)}
        return inp
    _L1_xattn_all = _L1_xattn_setup()
    _L1_xattn_in = {k: v for k, v in _L1_xattn_all.items() if k in ('Wq', 'bq', 'Wk', 'bk', 'Wv', 'bv', 'Wo', 'bo')}
    del _L1_xattn_all

    def _L1_attn_setup():
        import jax, jax.numpy as jnp
        import numpy as np
        EPS_LN = 1e-06
        STAB = 0.001

        def layer_norm(x, gamma, beta):
            mu = jnp.mean(x, axis=-1, keepdims=True)
            var = jnp.mean(jnp.square(x - mu), axis=-1, keepdims=True)
            return (x - mu) * jax.lax.rsqrt(var + EPS_LN) * gamma + beta
        key = jax.random.key(seed)
        B, L, E, H, F = (8, 256, 128, 16, 512)
        dh = E // H
        ks = jax.random.split(key, 12)
        s_attn = 1.0 / np.sqrt(E)
        s_ffn1 = 1.0 / np.sqrt(E)
        s_ffn2 = 1.0 / np.sqrt(F)
        return {'x': jax.random.normal(ks[0], (B, L, E), jnp.float32), 'gamma1': jnp.ones((E,), jnp.float32), 'beta1': jnp.zeros((E,), jnp.float32), 'wq': jax.random.normal(ks[1], (E, H, dh), jnp.float32) * s_attn, 'wk': jax.random.normal(ks[2], (E, H, dh), jnp.float32) * s_attn, 'wv': jax.random.normal(ks[3], (E, H, dh), jnp.float32) * s_attn, 'wo': jax.random.normal(ks[4], (H, dh, E), jnp.float32) * s_attn, 'w1': jax.random.normal(ks[5], (E, F), jnp.float32) * s_ffn1, 'b1': jnp.zeros((F,), jnp.float32), 'w2': jax.random.normal(ks[6], (F, E), jnp.float32) * s_ffn2, 'b2': jnp.zeros((E,), jnp.float32)}
    _L1_attn_all = _L1_attn_setup()
    _L1_attn_in = {k: v for k, v in _L1_attn_all.items() if k in ('gamma1', 'beta1', 'wq', 'wk', 'wv', 'wo', 'w1', 'b1', 'w2', 'b2')}
    del _L1_attn_all

    def _L1_ffn_setup():
        import jax, jax.numpy as jnp
        import numpy as np
        B, S, D, H, E = (8, 256, 128, 512, 16)
        key = jax.random.key(seed)
        ks = jax.random.split(key, 4)
        sd = 1.0 / np.sqrt(D).astype(np.float32)
        sh = 1.0 / np.sqrt(H).astype(np.float32)
        return {'x': jax.random.normal(ks[0], (B, S, D), jnp.float32), 'Wg': jax.random.normal(ks[1], (D, E), jnp.float32) * sd, 'bg': jnp.zeros((E,), jnp.float32), 'W1': jax.random.normal(ks[2], (E, D, H), jnp.float32) * sd, 'b1': jnp.zeros((E, H), jnp.float32), 'W2': jax.random.normal(ks[3], (E, H, D), jnp.float32) * sh, 'b2': jnp.zeros((E, D), jnp.float32)}
    _L1_ffn_all = _L1_ffn_setup()
    _L1_ffn_in = {k: v for k, v in _L1_ffn_all.items() if k in ('Wg', 'bg', 'W1', 'b1', 'W2', 'b2')}
    del _L1_ffn_all
    return {'x': x, 'ctx_1024': ctx_1024, 'mask_Bx1xSxS2_fk0': mask_Bx1xSxS2_fk0, 'L0_xattn_Wq': _L0_xattn_in['Wq'], 'L0_xattn_bq': _L0_xattn_in['bq'], 'L0_xattn_Wk': _L0_xattn_in['Wk'], 'L0_xattn_bk': _L0_xattn_in['bk'], 'L0_xattn_Wv': _L0_xattn_in['Wv'], 'L0_xattn_bv': _L0_xattn_in['bv'], 'L0_xattn_Wo': _L0_xattn_in['Wo'], 'L0_xattn_bo': _L0_xattn_in['bo'], 'L0_attn_w': _L0_attn_in['w'], 'L0_attn_u': _L0_attn_in['u'], 'L0_attn_mix_k': _L0_attn_in['mix_k'], 'L0_attn_mix_v': _L0_attn_in['mix_v'], 'L0_attn_mix_r': _L0_attn_in['mix_r'], 'L0_attn_Wk': _L0_attn_in['Wk'], 'L0_attn_Wv': _L0_attn_in['Wv'], 'L0_attn_Wr': _L0_attn_in['Wr'], 'L0_attn_Wo': _L0_attn_in['Wo'], 'L0_ffn_routing_W': _L0_ffn_in['routing_W'], 'L0_ffn_expert_bias': _L0_ffn_in['expert_bias'], 'L0_ffn_sW1': _L0_ffn_in['sW1'], 'L0_ffn_sb1': _L0_ffn_in['sb1'], 'L0_ffn_sW2': _L0_ffn_in['sW2'], 'L0_ffn_sb2': _L0_ffn_in['sb2'], 'L0_ffn_rW1': _L0_ffn_in['rW1'], 'L0_ffn_rb1': _L0_ffn_in['rb1'], 'L0_ffn_rW2': _L0_ffn_in['rW2'], 'L0_ffn_rb2': _L0_ffn_in['rb2'], 'L1_xattn_Wq': _L1_xattn_in['Wq'], 'L1_xattn_bq': _L1_xattn_in['bq'], 'L1_xattn_Wk': _L1_xattn_in['Wk'], 'L1_xattn_bk': _L1_xattn_in['bk'], 'L1_xattn_Wv': _L1_xattn_in['Wv'], 'L1_xattn_bv': _L1_xattn_in['bv'], 'L1_xattn_Wo': _L1_xattn_in['Wo'], 'L1_xattn_bo': _L1_xattn_in['bo'], 'L1_attn_gamma1': _L1_attn_in['gamma1'], 'L1_attn_beta1': _L1_attn_in['beta1'], 'L1_attn_wq': _L1_attn_in['wq'], 'L1_attn_wk': _L1_attn_in['wk'], 'L1_attn_wv': _L1_attn_in['wv'], 'L1_attn_wo': _L1_attn_in['wo'], 'L1_attn_w1': _L1_attn_in['w1'], 'L1_attn_b1': _L1_attn_in['b1'], 'L1_attn_w2': _L1_attn_in['w2'], 'L1_attn_b2': _L1_attn_in['b2'], 'L1_ffn_Wg': _L1_ffn_in['Wg'], 'L1_ffn_bg': _L1_ffn_in['bg'], 'L1_ffn_W1': _L1_ffn_in['W1'], 'L1_ffn_b1': _L1_ffn_in['b1'], 'L1_ffn_W2': _L1_ffn_in['W2'], 'L1_ffn_b2': _L1_ffn_in['b2']}

def reference(x, ctx_1024, mask_Bx1xSxS2_fk0, L0_xattn_Wq, L0_xattn_bq, L0_xattn_Wk, L0_xattn_bk, L0_xattn_Wv, L0_xattn_bv, L0_xattn_Wo, L0_xattn_bo, L0_attn_w, L0_attn_u, L0_attn_mix_k, L0_attn_mix_v, L0_attn_mix_r, L0_attn_Wk, L0_attn_Wv, L0_attn_Wr, L0_attn_Wo, L0_ffn_routing_W, L0_ffn_expert_bias, L0_ffn_sW1, L0_ffn_sb1, L0_ffn_sW2, L0_ffn_sb2, L0_ffn_rW1, L0_ffn_rb1, L0_ffn_rW2, L0_ffn_rb2, L1_xattn_Wq, L1_xattn_bq, L1_xattn_Wk, L1_xattn_bk, L1_xattn_Wv, L1_xattn_bv, L1_xattn_Wo, L1_xattn_bo, L1_attn_gamma1, L1_attn_beta1, L1_attn_wq, L1_attn_wk, L1_attn_wv, L1_attn_wo, L1_attn_w1, L1_attn_b1, L1_attn_w2, L1_attn_b2, L1_ffn_Wg, L1_ffn_bg, L1_ffn_W1, L1_ffn_b1, L1_ffn_W2, L1_ffn_b2):
    import jax
    import jax.numpy as jnp

    def _L0_xattn_ref(x, c, Wq, bq, Wk, bk, Wv, bv, Wo, bo):
        import jax, jax.numpy as jnp
        import numpy as np
        B, SQ, SK, D, H = (2, 256, 512, 128, 16)
        HD = D // H

        def _local_allowed_mask(num_q, num_k):
            kpq, extra = (num_k // num_q, num_k % num_q)
            i = jnp.arange(num_q)
            start = i * kpq + jnp.minimum(i, extra)
            end = start + kpq + (i < extra)
            j = jnp.arange(num_k)
            return (j[None, :] >= start[:, None]) & (j[None, :] < end[:, None])
        b, sq, d = x.shape
        sk = c.shape[1]
        scale = 1.0 / jnp.sqrt(jnp.asarray(HD, x.dtype))
        q = (x @ Wq.T + bq).reshape(b, sq, H, HD).transpose(0, 2, 1, 3)
        k = (c @ Wk.T + bk).reshape(b, sk, H, HD).transpose(0, 2, 1, 3)
        v = (c @ Wv.T + bv).reshape(b, sk, H, HD).transpose(0, 2, 1, 3)
        scores = jnp.einsum('bhqd,bhkd->bhqk', q, k) * scale
        allowed = _local_allowed_mask(sq, sk)
        neg = jnp.asarray(jnp.finfo(scores.dtype).min, scores.dtype)
        scores = jnp.where(allowed[None, None], scores, neg)
        attn = jax.nn.softmax(scores, axis=-1)
        out = jnp.einsum('bhqk,bhkd->bhqd', attn, v)
        out = out.transpose(0, 2, 1, 3).reshape(b, sq, d)
        return out @ Wo.T + bo

    def _L0_attn_ref(x, w, u, mix_k, mix_v, mix_r, Wk, Wv, Wr, Wo):
        import jax, jax.numpy as jnp
        import numpy as np
        B, T, C = (8, 256, 128)
        NEG = -1e+30

        def wkv(w, u, k, v):
            w_exp = -jnp.exp(w)
            p0 = jnp.zeros(k.shape[::2], k.dtype)
            q0 = jnp.zeros(k.shape[::2], k.dtype)
            o0 = jnp.full(k.shape[::2], NEG, k.dtype)

            def step(carry, kv_t):
                p, q, o = carry
                k_t, v_t = kv_t
                uk = u + k_t
                no = jnp.maximum(o, uk)
                A = jnp.exp(o - no)
                Bc = jnp.exp(uk - no)
                out = (A * p + Bc * v_t) / (A * q + Bc)
                wo = w_exp + o
                no2 = jnp.maximum(wo, k_t)
                A2 = jnp.exp(wo - no2)
                B2 = jnp.exp(k_t - no2)
                return ((A2 * p + B2 * v_t, A2 * q + B2, no2), out)
            kT = jnp.swapaxes(k, 0, 1)
            vT = jnp.swapaxes(v, 0, 1)
            _, outs = jax.lax.scan(step, (p0, q0, o0), (kT, vT))
            return jnp.swapaxes(outs, 0, 1)
        x_prev = jnp.pad(x, ((0, 0), (1, 0), (0, 0)))[:, :-1]
        xk = x_prev + mix_k * (x - x_prev)
        xv = x_prev + mix_v * (x - x_prev)
        xr = x_prev + mix_r * (x - x_prev)
        k = jnp.einsum('btc,dc->btd', xk, Wk)
        v = jnp.einsum('btc,dc->btd', xv, Wv)
        sr = jax.nn.sigmoid(jnp.einsum('btc,dc->btd', xr, Wr))
        rwkv = sr * wkv(w, u, k, v)
        return jnp.einsum('btc,dc->btd', rwkv, Wo)

    def _L0_ffn_ref(X, routing_W, expert_bias, sW1, sb1, sW2, sb2, rW1, rb1, rW2, rb2):
        import jax, jax.numpy as jnp
        import numpy as np
        E = 8
        K = 2
        B, T, d = X.shape
        shared = jax.nn.silu(X @ sW1 + sb1) @ sW2 + sb2
        logits = jnp.einsum('btd,ed->bte', X, routing_W) + expert_bias
        activation = jnp.sqrt(jax.nn.softplus(logits))
        top_vals, top_idx = jax.lax.top_k(activation, K)
        combine = jnp.sum(jax.nn.one_hot(top_idx, E, dtype=X.dtype) * top_vals[..., None], axis=-2)
        Xf = X.reshape(-1, d)
        cf = combine.reshape(-1, E)
        hdn = jax.nn.silu(jnp.einsum('nd,edh->enh', Xf, rW1) + rb1[:, None, :])
        y = jnp.einsum('enh,ehd->end', hdn, rW2) + rb2[:, None, :]
        routed = jnp.einsum('ne,end->nd', cf, y).reshape(B, T, d)
        return shared + routed

    def _L1_xattn_ref(q, k, v, mask, Wq, bq, Wk, bk, Wv, bv, Wo, bo):
        import jax, jax.numpy as jnp
        import numpy as np
        B, L, D, H = (4, 256, 128, 16)
        HD = D // H
        NEG = -1000000000000000.0

        def _split_heads(x):
            b, l, _ = x.shape
            return x.reshape(b, l, H, HD).transpose(0, 2, 1, 3)
        qw = q @ Wq + bq
        kw = k @ Wk + bk
        vw = v @ Wv + bv
        qh = _split_heads(qw)
        kh = _split_heads(kw)
        vh = _split_heads(vw)
        scale = 1.0 / jnp.sqrt(jnp.float32(HD))
        scores = jnp.einsum('bhqd,bhkd->bhqk', qh, kh) * scale
        scores = scores + mask * NEG
        weights = jax.nn.softmax(scores, axis=-1)
        out = jnp.einsum('bhqk,bhkd->bhqd', weights, vh)
        out = out.transpose(0, 2, 1, 3).reshape(q.shape[0], q.shape[1], D)
        return out @ Wo + bo

    def _L1_attn_ref(x, gamma1, beta1, wq, wk, wv, wo, w1, b1, w2, b2):
        import jax, jax.numpy as jnp
        import numpy as np
        EPS_LN = 1e-06
        STAB = 0.001

        def layer_norm(x, gamma, beta):
            mu = jnp.mean(x, axis=-1, keepdims=True)
            var = jnp.mean(jnp.square(x - mu), axis=-1, keepdims=True)
            return (x - mu) * jax.lax.rsqrt(var + EPS_LN) * gamma + beta
        ln1 = layer_norm(x, gamma1, beta1)
        q = jnp.einsum('ble,ehd->blhd', ln1, wq)
        k = jnp.einsum('ble,ehd->blhd', ln1, wk)
        v = jnp.einsum('ble,ehd->blhd', ln1, wv)
        qp = jax.nn.relu(q) + STAB
        kp = jax.nn.relu(k) + STAB
        kvs = jnp.einsum('blhm,blhd->bhmd', kp, v)
        num = jnp.einsum('blhm,bhmd->blhd', qp, kvs)
        ksum = jnp.sum(kp, axis=1)
        den = jnp.einsum('blhm,bhm->blh', qp, ksum)
        att = num / den[..., None]
        attn_out = jnp.einsum('blhd,hde->ble', att, wo)
        add1 = attn_out + x
        ln2 = layer_norm(add1, gamma1, beta1)
        h = jax.nn.gelu(jnp.einsum('ble,ef->blf', ln2, w1) + b1, approximate=False)
        out2 = jax.nn.gelu(jnp.einsum('blf,fe->ble', h, w2) + b2, approximate=False)
        return out2 + add1

    def _L1_ffn_ref(x, Wg, bg, W1, b1, W2, b2):
        import jax, jax.numpy as jnp
        import numpy as np
        B, S, D, H, E = (8, 256, 128, 512, 16)
        d = x.shape[-1]
        xf = x.reshape(-1, d)
        n_tok = xf.shape[0]
        n_exp = Wg.shape[1]
        cap = -(-n_tok // n_exp)
        score = jax.nn.softmax(xf @ Wg + bg, axis=-1)
        gate = jnp.max(score, axis=-1)
        idx = jnp.argmax(score, axis=-1)
        onehot = jax.nn.one_hot(idx, n_exp, dtype=jnp.int32)
        pos = jnp.sum((jnp.cumsum(onehot, axis=0) - 1) * onehot, axis=-1)
        keep = pos < cap
        safe_pos = jnp.where(keep, pos, cap - 1)
        buf = jnp.zeros((n_exp, cap, d), x.dtype).at[idx, safe_pos].add(jnp.where(keep[:, None], xf, 0.0))
        h = jax.nn.relu(jnp.einsum('ecd,edh->ech', buf, W1) + b1[:, None, :])
        y = jnp.einsum('ech,ehd->ecd', h, W2) + b2[:, None, :]
        out = y[idx, safe_pos] * gate[:, None]
        out = jnp.where(keep[:, None], out, 0.0)
        return out.reshape(x.shape)
    x = x + _L0_xattn_ref(_layernorm(x, axis=-1), ctx_1024, L0_xattn_Wq, L0_xattn_bq, L0_xattn_Wk, L0_xattn_bk, L0_xattn_Wv, L0_xattn_bv, L0_xattn_Wo, L0_xattn_bo)
    x = x + _L0_attn_ref(_layernorm(x, axis=-1), L0_attn_w, L0_attn_u, L0_attn_mix_k, L0_attn_mix_v, L0_attn_mix_r, L0_attn_Wk, L0_attn_Wv, L0_attn_Wr, L0_attn_Wo)
    x = x + _L0_ffn_ref(_layernorm(x, axis=-1), L0_ffn_routing_W, L0_ffn_expert_bias, L0_ffn_sW1, L0_ffn_sb1, L0_ffn_sW2, L0_ffn_sb2, L0_ffn_rW1, L0_ffn_rb1, L0_ffn_rW2, L0_ffn_rb2)
    x = x + _L1_xattn_ref(_layernorm(x, axis=-1), ctx_1024, ctx_1024, mask_Bx1xSxS2_fk0, L1_xattn_Wq, L1_xattn_bq, L1_xattn_Wk, L1_xattn_bk, L1_xattn_Wv, L1_xattn_bv, L1_xattn_Wo, L1_xattn_bo)
    x = x + _L1_attn_ref(_layernorm(x, axis=-1), L1_attn_gamma1, L1_attn_beta1, L1_attn_wq, L1_attn_wk, L1_attn_wv, L1_attn_wo, L1_attn_w1, L1_attn_b1, L1_attn_w2, L1_attn_b2)
    x = x + _L1_ffn_ref(_layernorm(x, axis=-1), L1_ffn_Wg, L1_ffn_bg, L1_ffn_W1, L1_ffn_b1, L1_ffn_W2, L1_ffn_b2)
    return x

_drawn_inputs = setup_inputs


def setup_inputs(seed=0):
    import zlib

    import numpy as np

    out = dict(_drawn_inputs(seed))
    spreads = {'L0_xattn_bq': (0.0, 0.8),
     'L0_xattn_bk': (0.0, 0.8),
     'L0_xattn_bv': (0.0, 0.273),
     'L0_xattn_bo': (0.0, 0.1),
     'L0_ffn_expert_bias': (0.0, 0.1),
     'L0_ffn_sb1': (0.0, 0.8),
     'L0_ffn_sb2': (0.0, 0.1),
     'L0_ffn_rb1': (0.0, 0.74),
     'L0_ffn_rb2': (0.0, 0.1),
     'L1_xattn_bq': (0.0, 0.332),
     'L1_xattn_bk': (0.0, 0.8),
     'L1_xattn_bv': (0.0, 0.1),
     'L1_xattn_bo': (0.0, 0.1),
     'L1_attn_gamma1': (1.0, 0.2),
     'L1_attn_beta1': (0.0, 0.1),
     'L1_attn_b1': (0.0, 0.333),
     'L1_attn_b2': (0.0, 0.1),
     'L1_ffn_bg': (0.0, 0.1),
     'L1_ffn_b1': (0.0, 0.8),
     'L1_ffn_b2': (0.0, 0.8)}
    factors = {'L0_xattn_Wq': 8.0,
     'L0_xattn_Wk': 8.0,
     'L0_attn_w': 8.0,
     'L0_attn_u': 8.0,
     'L0_attn_mix_k': 8.0,
     'L0_attn_mix_v': 4.347,
     'L0_attn_mix_r': 8.0,
     'L0_attn_Wk': 8.0,
     'L0_attn_Wv': 2.74,
     'L0_attn_Wr': 8.0,
     'L0_ffn_sW1': 3.055,
     'L0_ffn_sW2': 2.853}
    for name, (base, spread) in spreads.items():
        noise = np.random.default_rng([zlib.crc32(name.encode()), seed]).standard_normal(out[name].shape)
        drawn = base * np.exp(spread * noise) if base else spread * noise
        out[name] = jnp.asarray(drawn.astype(out[name].dtype))
    for name, factor in factors.items():
        out[name] = (out[name] * factor).astype(out[name].dtype)
    return out
```

```python
from contextlib import ExitStack

import numpy as np
import concourse.bass as bass
from concourse import mybir

F32 = mybir.dt.float32
ALU = mybir.AluOpType
ACT = mybir.ActivationFunctionType
AX_X = mybir.AxisListType.X

P = 128
BATCH, SEQ, D = 16, 32, 128
TOK = BATCH * SEQ
TT = TOK // P
KEYS = 512
CTX = BATCH * KEYS
HEADS, HD = 16, 8
GROUPS = 4
LOCAL = KEYS // SEQ
KT = KEYS // P
E0, H0 = 8, 64
E1, H1 = 16, 512
CAP = TOK // E1
SLOTS = E1 * CAP
FF = 512
QSCALE = float(1.0 / np.sqrt(np.float32(HD)))
MASK_BIG = 1e15
NEG_STATE = -1e30
STAB = 0.001
EPS_OUTER, EPS_INNER = 1e-5, 1e-6

EARLY = [("ident", 128), ("bq0", 1), ("bk0", 1), ("bv0", 1), ("wq0", 128), ("wk0", 128), ("wv0", 128),
         ("wo0", 128), ("headsum", 64), ("headspread", 256), ("bo0", 128)]
LATE = [("rk", 128), ("rv", 128), ("rr", 128), ("ro", 128), ("w", 1), ("u", 1), ("mk", 1), ("mv", 1), ("mr", 1),
        ("route", E0), ("eb", E0), ("sw1", H0), ("sb1", 1), ("rw1", 512), ("rb1", 4), ("rw2", 512), ("sw2", 128),
        ("rb2", 128), ("sb2", 128), ("spread", 512), ("before", E0 * E0),
        ("wq1", 128), ("wk1", 128), ("wv1", 128), ("wo1", 128), ("bq1", 1), ("bk1", 1), ("bv1", 1), ("bo1", 128),
        ("own4", 4), ("rows32", 32), ("heads32", 32),
        ("gamma", 1), ("beta", 1), ("lq", 128), ("lk", 128), ("lv", 128), ("lo", 128), ("w1", FF), ("b1", 4),
        ("w2", FF), ("b2", 128), ("samehead", 128), ("batchof", 4),
        ("wg", E1), ("bg", E1), ("iota_e", E1), ("iota_slot", SLOTS), ("slot_row", 4), ("upto", 128), ("ones", 128)]


def width(pack):
    return sum(n for _, n in pack)


def columns(pack):
    at, out = 0, {}
    for name, n in pack:
        out[name] = (at, at + n)
        at += n
    return out


class Chain:

    def __init__(self, eng, sem):
        self.eng, self.sem, self.n = eng, sem, 0

    def add(self, ins):
        self.n += 1
        ins.then_inc(self.sem, 1)

    def join(self):
        self.eng.wait_ge(self.sem, self.n)

    def link(self, ins):
        self.add(ins)
        self.join()


def program(nc, x_d, early_d, late_d, ctx_d, mask_d, w1_d, w2_d, moeb_d, out_d):
    with ExitStack() as stack:
        def sb(name, cols, rows=P):
            return stack.enter_context(nc.sbuf_tensor(name + "_sb", [rows, cols], F32))

        sems = {}

        def sig(name):
            if name not in sems:
                sems[name] = stack.enter_context(nc.semaphore(name))
            return sems[name]

        bank = [stack.enter_context(nc.psum_tensor(f"bank{i}", [P, 512], F32)) for i in range(8)]

        early, late = sb("early", width(EARLY)), sb("late", width(LATE))
        ce, cl = columns(EARLY), columns(LATE)

        def wt(name, rows=P):
            if name in ce:
                return early[0:rows, ce[name][0]:ce[name][1]]
            return late[0:rows, cl[name][0]:cl[name][1]]

        ctx = sb("ctx", CTX)
        k1 = sb("k1", CTX)
        v1 = sb("v1", CTX)
        mask = sb("mask", CTX)
        x_tok = sb("x_tok", TOK)
        xb_tok = sb("xb_tok", TOK)
        xn_tok = sb("xn_tok", TOK)
        lnT = sb("lnT", TOK)
        work = sb("work", 16 * 512)
        stats, aggr = sb("stats", TT * 6), sb("aggr", TT * 2)
        veps, rstd, minus_half, half = sb("veps", TT), sb("rstd", TT), sb("minus_half", TT), sb("half", TT * E0)
        small = sb("small", 1024)

        def tile(i, n=1, of=work):
            return of[:, 512 * i:512 * (i + n)]

        def tok3(a):
            return a.rearrange("p (t d) -> p t d", t=TT)

        x3, xb3, xn3 = tok3(x_tok[:, :]), tok3(xb_tok[:, :]), tok3(xn_tok[:, :])
        st3, ag3 = stats[:, :].rearrange("p (t k) -> p t k", t=TT), aggr[:, :].rearrange("p (t k) -> p t k", t=TT)

        def over_tiles(row):
            return row.unsqueeze(1).broadcast_to([P, TT, D])

        q0T, v0s, vp = tile(0), [tile(3), tile(4)], [tile(5), tile(6)]
        prod4 = [tile(1), tile(2), tile(10), tile(11)]
        e0 = [tile(7), tile(8)]
        o0T = tile(9)
        mx0, sm0, rs0 = small[:, 0:64], small[:, 64:128], small[:, 128:192]

        S33 = SEQ + 1
        N33 = BATCH * S33

        def m33(i):
            return mask[:, N33 * i:N33 * (i + 1)]

        def b33(a):
            return a.rearrange("p (b s) -> p b s", s=S33)

        def now(a):
            return b33(a)[:, :, 1:S33]

        def prev(a):
            return b33(a)[:, :, 0:SEQ]

        def bs(a):
            return a.rearrange("p (b s) -> p b s", s=SEQ)

        ln33, dec33, k33, o33, A33, B33, Bv33, p33 = [m33(i) for i in range(8)]
        r0 = 8 * N33
        q33 = mask[:, r0:r0 + N33]
        r0 += N33
        dx, xk, xv, xr, ab = [mask[:, r0 + 512 * i:r0 + 512 * (i + 1)] for i in range(4)] + [mask[:, r0 + 2048:r0 + 3072]]
        num, t_bv, den, er, v_sb = tile(10), tile(11), tile(12), tile(13), tile(14)
        rw = tile(15)
        wexp = small[:, 192:193]

        hid = [tile(i) for i in range(5)]
        hsc = [tile(5 + i) for i in range(4)]
        cfT = tile(9)[0:E0, :]
        fr = [small[:, 200 + 32 * i:232 + 32 * i] for i in range(12)]
        fcmp = [tile(10)[:, 0:256], tile(10)[:, 256:512]]

        qbd = tile(0, 4).rearrange("p (b j q) -> p b j q", b=BATCH, j=4)
        NS, NT, NPT = 3, 3, 8
        q1T = tile(15)
        sc = [tile(4 + i) for i in range(NS)]
        pt = [tile(7 + i) for i in range(NPT)]
        rsum, rinv = small[:, 640:704], small[:, 704:768]
        smin = small[:, 768:832]
        oT = q1T
        otmp = lnT
        mg = tile(4, 4)
        vkey = v1[:, :].rearrange("p (b k f) -> p b k f", b=BATCH, k=KT)

        qp, att, qk, nump = tile(0), tile(1), tile(2), tile(3)
        kp_tok, v_tok = tile(4), tile(5)
        ksum = small[:, 832:848]
        kvs = tile(6, 4)
        hT = tile(10, 4)
        add1, res4 = tile(4), tile(5)
        g2 = tile(6)

        w1e = ctx[:, :].rearrange("p (e h) -> p e h", e=E1)
        w2e = k1[:, :].rearrange("p (e k d) -> p e k d", e=E1, k=4)
        moeb = v1[:, 0:2560]
        b1e, b2e = moeb[:, 0:2048], moeb[:, 2048:2560]
        disp = v1[:, 2560:2560 + 2048]
        comb = v1[:, 4608:4608 + 2048]
        slotbc = v1[:, 6656:6656 + 512]
        bufT = mask[:, 0:512]
        hmoe = mask[:, 512:2560]
        hmoeT = mask[:, 2560:4608]
        ymoe = mask[:, 4608:5120]
        outt = mask[:, 5120:5632]
        mr = [small[:, 64 * i:64 * (i + 1)] for i in range(8)]
        m4 = [small[:, 512 + 4 * i:516 + 4 * i] for i in range(8)]

        block = stack.enter_context(nc.Block())

        NCH = 4
        PIECE = CTX // NCH

        @block.sync
        def _(sp):
            sp.dma_start(x3, x_d.rearrange("(t p) d -> p t d", p=P)).then_inc(sig("x_in"), 16)
            sp.dma_start(early[:, :], early_d).then_inc(sig("early_in"), 16)
            for c in range(NCH):
                sp.dma_start(ctx[:, c * PIECE:(c + 1) * PIECE], ctx_d[:, c * PIECE:(c + 1) * PIECE]).then_inc(sig(f"ctx_in{c}"), 16)
            sp.wait_ge(sig("x_new"), 2)
            for j in range(4):
                sp.dma_start(mask[32 * j:32 * j + 32, :], mask_d).then_inc(sig("mask_in"), 16)
            sp.wait_ge(sig("proj_done"), 32)
            sp.dma_start(ctx[:, :], w1_d).then_inc(sig("w1_in"), 16)
            sp.wait_ge(sig("s1_ready"), GROUPS * BATCH)
            sp.dma_start(k1[:, :], w2_d).then_inc(sig("w2_in"), 16)
            sp.wait_ge(sig("o1_ready"), BATCH)
            sp.dma_start(moeb, moeb_d).then_inc(sig("moeb_in"), 16)
            sp.wait_ge(sig("out_ready"), TT)
            sp.dma_start(out_d.rearrange("(t p) d -> p t d", p=P), tok3(outt)).then_inc(sig("stored"), 16)
            sp.wait_ge(sig("stored"), 16)

        @block.gpsimd
        def _(pool):
            pool.memset(minus_half[:, :], -0.5).then_inc(sig("half_ready"), 1)
            pool.memset(half[:, :], 0.5).then_inc(sig("half_ready"), 1)
            for a, v in ((ln33, 0.0), (k33, NEG_STATE), (A33, 0.0), (B33, 0.0), (Bv33, 0.0), (dec33, NEG_STATE)):
                pool.memset(b33(a)[:, :, 0:1], v).then_inc(sig("edges_ready"), 1)
            pool.wait_ge(sig("half_ready"), 2)

            def inverse_std(i):
                pool.wait_ge(sig("ln_var"), i + 1)
                nc.gpsimd.tensor_tensor(rstd[:, :], veps[:, :], minus_half[:, :], ALU.pow).then_inc(sig("ln_rstd"), 1)

            def residual_bias(name, n):
                if n == 0:
                    pool.wait_ge(sig("x_in"), 16)
                    pool.wait_ge(sig("early_in"), 16)
                else:
                    pool.wait_ge(sig("x_new"), n)
                nc.gpsimd.tensor_tensor(xb3, x3, over_tiles(wt(name)), ALU.add).then_inc(sig("xb_ready"), 1)

            inverse_std(0)
            residual_bias("bo0", 0)
            inverse_std(1)
            pool.wait_ge(sig("late_in"), 16)
            pool.wait_ge(sig("ab_exp"), 1)
            pool.wait_ge(sig("v_out"), 1)
            nc.gpsimd.tensor_tensor(t_bv, ab[:, 512:1024], v_sb, ALU.mult).then_inc(sig("bonus_ready"), 1)
            inverse_std(2)
            residual_bias("sb2", 2)
            pool.wait_ge(sig("softplus_ready"), 1)
            nc.gpsimd.tensor_tensor(fr[6], fr[5], half[:, :], ALU.pow).then_inc(sig("act_ready"), 1)
            inverse_std(3)
            residual_bias("bo1", 3)
            inverse_std(4)
            inverse_std(5)
            inverse_std(6)
            nc.gpsimd.tensor_tensor(res4, x_tok[:, :], add1, ALU.add).then_inc(sig("res_ready"), 1)
            inverse_std(7)

        @block.scalar
        def _(act):
            act.dma_start(late[:, :], late_d).then_inc(sig("late_in"), 16)

            def normT(n, dst, **affine):
                act.wait_ge(sig("lnT_ps"), n + 1)
                nc.scalar.activation(dst, bank[6][:, :], ACT.Identity, **affine).then_inc(sig("lnT_ready"), 1)

            act.wait_ge(sig("early_in"), 16)
            normT(0, lnT[:, :])
            for n in range(2):
                act.wait_ge(sig("e0_arg"), n + 1)
                nc.scalar.activation(e0[n], e0[n], ACT.Exp).then_inc(sig("e0_exp"), 1)
            for c in range(BATCH):
                act.wait_ge(sig("v0_ps"), c + 1)
                if c >= 2:
                    act.wait_ge(sig("vp_ready"), c - 1)
                nc.scalar.activation(v0s[c % 2], bank[6 + c % 2][:, :], ACT.Identity, bias=wt("bv0")).then_inc(sig("v0_ready"), 1)
            act.wait_ge(sig("late_in"), 16)

            nproj = [0]

            def evacuate(n):
                for _ in range(n):
                    i = nproj[0]
                    nproj[0] += 1
                    act.wait_ge(sig("proj_done"), i + 1)
                    src = bank[4 + i % 2][:, :]
                    if i < BATCH:
                        nc.scalar.activation(k1[:, 512 * i:512 * (i + 1)], src, ACT.Identity, bias=wt("bk1")).then_inc(sig("proj_out"), 1)
                    else:
                        i -= BATCH
                        nc.scalar.copy(v1[:, 512 * i:512 * (i + 1)], src).then_inc(sig("proj_out"), 1)

            nc.scalar.activation(wexp, wt("w"), ACT.Exp).then_inc(sig("wexp_raw"), 1)
            evacuate(2)
            act.wait_ge(sig("edges_ready"), 6)
            act.wait_ge(sig("lnT_ps"), 2)
            nc.scalar.activation(now(ln33), bs(bank[6][:, :]), ACT.Identity).then_inc(sig("lnT_ready"), 1)
            evacuate(2)
            act.wait_ge(sig("rkvr_ps"), 1)
            nc.scalar.activation(now(k33), bs(bank[0][:, :]), ACT.Identity).then_inc(sig("k_out"), 1)
            act.wait_ge(sig("rkvr_ps"), 2)
            nc.scalar.copy(v_sb, bank[1][:, :]).then_inc(sig("v_out"), 1)
            act.wait_ge(sig("rkvr_ps"), 3)
            nc.scalar.activation(er, bank[2][:, :], ACT.Exp, scale=-1.0).then_inc(sig("er_ready"), 1)
            evacuate(1)
            act.wait_ge(sig("ab_arg"), 2)
            nc.scalar.activation(ab, ab, ACT.Exp).then_inc(sig("ab_exp"), 1)
            act.wait_ge(sig("AB_arg"), 1)
            nc.scalar.activation(now(A33), now(A33), ACT.Exp).then_inc(sig("AB_exp"), 1)
            act.wait_ge(sig("AB_arg"), 2)
            nc.scalar.activation(now(B33), now(B33), ACT.Exp).then_inc(sig("AB_exp"), 1)
            evacuate(11)
            normT(2, lnT[:, :])
            act.wait_ge(sig("abs_ready"), 1)
            nc.scalar.activation(fr[2], fr[1], ACT.Exp, scale=-1.0).then_inc(sig("e_ready"), 1)
            act.wait_ge(sig("w_ready"), 1)
            nc.scalar.activation(fr[4], fr[3], ACT.Ln).then_inc(sig("ln_ready"), 1)
            for n in range(5):
                act.wait_ge(sig("hid_ps"), n + 1)
                rows = P if n < 4 else H0
                bias = wt("rb1")[:, n:n + 1] if n < 4 else wt("sb1", H0)
                nc.scalar.activation(hid[n][0:rows, :], bank[n if n < 4 else 7][0:rows, :], ACT.Silu,
                                     bias=bias).then_inc(sig("hid_ready"), 1)
            evacuate(16)
            normT(3, lnT[:, :])
            for i in range(GROUPS * BATCH + 2):
                if i < GROUPS * BATCH:
                    act.wait_ge(sig("s1_min"), i + 1)
                    nc.scalar.activation(sc[i % NS], sc[i % NS], ACT.Exp, bias=smin[:, i:i + 1], scale=-1.0,
                                         accum_out=rsum[:, i:i + 1]).then_inc(sig("p1_ready"), 1)
                j = i - 2
                if j >= 0 and j % 2 == 0:
                    act.wait_ge(sig("pT_ps"), j + 1)
                    if j >= NPT:
                        act.wait_ge(sig("o1_ready"), (j - NPT) // GROUPS + 1)
                    nc.scalar.copy(pt[j % NPT], bank[3 + j % NT][:, :]).then_inc(sig("pT_even"), 1)
            normT(4, lnT[:, :], scale=wt("gamma"), bias=wt("beta"))
            act.wait_ge(sig("vtok_ps"), 1)
            nc.scalar.copy(v_tok, bank[2][:, :]).then_inc(sig("vtok_ready"), 1)
            normT(5, lnT[:, :], scale=wt("gamma"), bias=wt("beta"))
            for n in range(4):
                act.wait_ge(sig("ffh_ps"), n + 1)
                nc.scalar.activation(hT[:, 512 * n:512 * (n + 1)], bank[n][:, :], ACT.Gelu, bias=wt("b1")[:, n:n + 1]).then_inc(sig("ffh_ready"), 1)
            act.wait_ge(sig("ffo_ready"), 1)
            nc.scalar.activation(g2, g2, ACT.Gelu).then_inc(sig("g2_ready"), 1)
            normT(6, lnT[:, :])
            act.wait_ge(sig("gate_arg"), 1)
            nc.scalar.activation(mr[2], mr[1], ACT.Exp).then_inc(sig("gate_exp"), 1)
            for g in range(4):
                act.wait_ge(sig("hmT_ps"), g + 1)
                nc.scalar.activation(hmoeT[:, 512 * g:512 * (g + 1)], bank[g][:, :], ACT.Relu).then_inc(sig("hmT_ready"), 1)

        @block.vector
        def _(dve):
            v = nc.vector
            ch = Chain(dve, sig("dve_step"))
            norms = [0]

            def norm(src, eps):
                s3 = tok3(src)
                i = norms[0]
                norms[0] += 1
                for t in range(TT):
                    ch.add(v.bn_stats(st3[:, t, :], s3[:, t, :]))
                ch.join()
                for t in range(TT):
                    ch.add(v.bn_aggr(ag3[:, t, :], st3[:, t, :]))
                ch.join()
                v.tensor_scalar(veps[:, :], ag3[:, :, 1], eps, None, ALU.add).then_inc(sig("ln_var"), 1)
                dve.wait_ge(sig("ln_rstd"), i + 1)
                for t in range(TT):
                    v.tensor_scalar(xn3[:, t, :], s3[:, t, :], ag3[:, t, 0:1], rstd[:, t:t + 1],
                                    ALU.subtract, ALU.mult).then_inc(sig("xn_ready"), 1)
                dve.wait_ge(sig("xn_ready"), TT * (i + 1))

            dve.wait_ge(sig("x_in"), 16)
            norm(x_tok[:, :], EPS_OUTER)
            dve.wait_ge(sig("early_in"), 16)
            dve.wait_ge(sig("q0_ps"), 1)
            ch.link(v.tensor_scalar(q0T, bank[7][:, :], wt("bq0"), QSCALE, ALU.add, ALU.mult))

            def products(c):
                dve.wait_ge(sig("k0_ps"), c + 1)
                if c >= 4:
                    dve.wait_ge(sig("s0_ps"), c // 4)
                qb = q0T[:, SEQ * c:SEQ * (c + 1)].unsqueeze(2).broadcast_to([P, SEQ, LOCAL])
                v.scalar_tensor_tensor(prod4[c % 4].rearrange("p (q j) -> p q j", j=LOCAL),
                                       bank[c % 2][:, :].rearrange("p (q j) -> p q j", j=LOCAL), wt("bk0"), qb,
                                       ALU.add, ALU.mult).then_inc(sig("prod_ready"), 1)

            def softmax0(n):
                dve.wait_ge(sig("s0_ps"), 2 * (n + 1))
                s = bank[2 + n][:, :].rearrange("p (q j) -> p q j", j=LOCAL)
                e = e0[n].rearrange("p (q j) -> p q j", j=LOCAL)
                m, z, r = [a[:, SEQ * n:SEQ * (n + 1)] for a in (mx0, sm0, rs0)]
                wide = lambda a: a.unsqueeze(2).broadcast_to([P, SEQ, LOCAL])
                ch.link(v.tensor_reduce(m, s, AX_X, ALU.max))
                v.tensor_tensor(e, s, wide(m), ALU.subtract).then_inc(sig("e0_arg"), 1)
                dve.wait_ge(sig("e0_exp"), n + 1)
                ch.link(v.tensor_reduce(z, e, AX_X, ALU.add))
                ch.link(v.reciprocal(r, z))
                v.tensor_tensor(e, e, wide(r), ALU.mult).then_inc(sig("p0_ready"), 1)

            def weighted(c):
                dve.wait_ge(sig("p0_spread"), c + 1)
                dve.wait_ge(sig("v0_ready"), c + 1)
                v.tensor_tensor(vp[c % 2], bank[4 + c % 2][:, :], v0s[c % 2], ALU.mult).then_inc(sig("vp_ready"), 1)
                dve.wait_ge(sig("vp_ready"), c + 1)
                v.tensor_reduce(o0T[:, SEQ * c:SEQ * (c + 1)], vp[c % 2].rearrange("p (q j) -> p q j", j=LOCAL),
                                AX_X, ALU.add).then_inc(sig("o0_ready"), 1)

            for c in range(BATCH // 2):
                products(c)
            products(8)
            softmax0(0)
            for c in range(9, BATCH):
                products(c)
            softmax0(1)
            for c in range(BATCH):
                weighted(c)

            xver = [0]

            def residual(src, base):
                v.tensor_tensor(x_tok[:, :], src, base, ALU.add).then_inc(sig("x_new"), 1)
                xver[0] += 1
                dve.wait_ge(sig("x_new"), xver[0])

            dve.wait_ge(sig("xo_ps"), 1)
            dve.wait_ge(sig("xb_ready"), 1)
            residual(bank[0][:, :], xb_tok[:, :])

            norm(x_tok[:, :], EPS_OUTER)
            dve.wait_ge(sig("late_in"), 16)
            dve.wait_ge(sig("wexp_raw"), 1)
            dve.wait_ge(sig("edges_ready"), 6)
            ch.link(v.tensor_scalar(wexp, wexp, -1.0, None, ALU.mult))
            ch.link(v.memset(now(dec33), 0.0))
            ch.add(v.tensor_scalar(now(dec33), now(dec33), wexp, None, ALU.add))
            dve.wait_ge(sig("lnT_ready"), 2)
            ch.link(v.tensor_tensor(bs(dx), now(ln33), prev(ln33), ALU.subtract))
            for dst, mix in ((xk, "mk"), (xv, "mv"), (xr, "mr")):
                v.scalar_tensor_tensor(bs(dst), bs(dx), wt(mix), prev(ln33), ALU.mult, ALU.add).then_inc(sig("mix_ready"), 1)
            dve.wait_ge(sig("k_out"), 1)
            ch.link(v.tensor_tensor_scan(o33, dec33, k33, NEG_STATE, ALU.add, ALU.max))
            dve.wait_ge(sig("mix_ready"), 3)
            dve.wait_ge(sig("rkvr_ps"), 3)
            top = xk
            ch.link(v.scalar_tensor_tensor(bs(top), now(k33), wt("u"), prev(o33), ALU.add, ALU.max))
            v.tensor_tensor(bs(ab[:, 0:512]), prev(o33), bs(top), ALU.subtract).then_inc(sig("ab_arg"), 1)
            v.scalar_tensor_tensor(bs(ab[:, 512:1024]), now(k33), wt("u"), bs(top), ALU.add, ALU.subtract).then_inc(sig("ab_arg"), 1)
            v.scalar_tensor_tensor(now(A33), prev(o33), wexp, now(o33), ALU.add, ALU.subtract).then_inc(sig("AB_arg"), 1)
            v.tensor_tensor(now(B33), now(k33), now(o33), ALU.subtract).then_inc(sig("AB_arg"), 1)
            dve.wait_ge(sig("AB_exp"), 2)
            ch.add(v.tensor_tensor(now(Bv33), now(B33), bs(bank[1][:, :]), ALU.mult))
            ch.link(v.tensor_tensor_scan(q33, A33, B33, 0.0, ALU.mult, ALU.add))
            dve.wait_ge(sig("ab_exp"), 1)
            ch.add(v.tensor_tensor(bs(den), bs(ab[:, 0:512]), prev(q33), ALU.mult))
            ch.link(v.tensor_tensor_scan(p33, A33, Bv33, 0.0, ALU.mult, ALU.add))
            ch.add(v.tensor_tensor(den, den, ab[:, 512:1024], ALU.add))
            ch.link(v.tensor_tensor(bs(num), bs(ab[:, 0:512]), prev(p33), ALU.mult))
            dve.wait_ge(sig("er_ready"), 1)
            dve.wait_ge(sig("bonus_ready"), 1)
            ch.add(v.scalar_tensor_tensor(den, er, 1.0, den, ALU.add, ALU.mult))
            ch.link(v.tensor_tensor(num, num, t_bv, ALU.add))
            ch.link(v.reciprocal(den, den))
            v.tensor_tensor(rw, num, den, ALU.mult).then_inc(sig("rw_ready"), 1)
            dve.wait_ge(sig("xo_ps"), 2)
            residual(bank[0][:, :], x_tok[:, :])

            norm(x_tok[:, :], EPS_OUTER)
            e3 = lambda a: a.rearrange("p (t e) -> p t e", e=E0)
            dve.wait_ge(sig("route_ps"), 1)
            logit, mag, ex, wl, lw, sp, av, t0, t1, cf = [fr[i] for i in range(10)]
            eb = wt("eb").unsqueeze(1).broadcast_to([P, TT, E0])
            ch.link(v.tensor_tensor(e3(logit), e3(bank[6][:, 0:32]), eb, ALU.add))
            v.scalar_tensor_tensor(mag, logit, -1.0, logit, ALU.mult, ALU.max).then_inc(sig("abs_ready"), 1)
            dve.wait_ge(sig("e_ready"), 1)
            v.tensor_scalar(wl, ex, 1.0, None, ALU.add).then_inc(sig("w_ready"), 1)
            dve.wait_ge(sig("w_ready"), 1)
            ch.link(v.tensor_scalar(t0, wl, -1.0, 1e-30, ALU.add, ALU.max))
            ch.link(v.reciprocal(t0, t0))
            ch.add(v.scalar_tensor_tensor(t1, wl, 1.0, ex, ALU.is_equal, ALU.mult))
            ch.link(v.tensor_tensor(t0, t0, ex, ALU.mult))
            dve.wait_ge(sig("ln_ready"), 1)
            ch.link(v.tensor_tensor(t0, t0, lw, ALU.mult))
            ch.link(v.tensor_tensor(t0, t0, t1, ALU.add))
            v.scalar_tensor_tensor(sp, logit, 0.0, t0, ALU.max, ALU.add).then_inc(sig("softplus_ready"), 1)
            dve.wait_ge(sig("act_ready"), 1)
            pair = [P, TT, E0, E0]
            f4 = [a.rearrange("p (t e j) -> p t e j", t=TT, e=E0) for a in fcmp]
            a_j, a_e = e3(av).unsqueeze(2).broadcast_to(pair), e3(av).unsqueeze(3).broadcast_to(pair)
            ch.add(v.tensor_tensor(f4[0], a_j, a_e, ALU.is_gt))
            ch.link(v.tensor_tensor(f4[1], a_j, a_e, ALU.is_equal))
            before = wt("before").unsqueeze(1).broadcast_to([P, TT, E0 * E0])
            ch.link(v.tensor_tensor(fcmp[1].rearrange("p (t k) -> p t k", t=TT), fcmp[1].rearrange("p (t k) -> p t k", t=TT), before, ALU.mult))
            ch.link(v.tensor_tensor(fcmp[0], fcmp[0], fcmp[1], ALU.add))
            ch.link(v.tensor_reduce(t1, fcmp[0].rearrange("p (k j) -> p k j", j=E0), AX_X, ALU.add))
            v.scalar_tensor_tensor(cf, t1, 1.5, av, ALU.is_lt, ALU.mult).then_inc(sig("cf_ready"), 1)
            dve.wait_ge(sig("cfT_ps"), 1)
            v.tensor_copy(cfT, bank[6][0:E0, :]).then_inc(sig("cfT_ready"), 1)
            for n in range(4):
                dve.wait_ge(sig("spread_ps"), n + 1)
                dve.wait_ge(sig("hid_ready"), n + 1)
                v.tensor_tensor(hsc[n], hid[n], bank[n][:, :], ALU.mult).then_inc(sig("hsc_ready"), 1)
            dve.wait_ge(sig("xo_ps"), 3)
            dve.wait_ge(sig("xb_ready"), 2)
            residual(bank[6][:, :], xb_tok[:, :])

            norm(x_tok[:, :], EPS_OUTER)
            dve.wait_ge(sig("q1_ps"), 1)
            ch.link(v.tensor_scalar(q1T, bank[7][:, :], wt("bq1"), -QSCALE, ALU.add, ALU.mult))
            ch.link(v.tensor_scalar(q1T, q1T, 1.0 / MASK_BIG, None, ALU.mult))
            own = wt("own4").unsqueeze(2).broadcast_to([P, 4, SEQ])
            for b in range(BATCH):
                qv = q1T[:, SEQ * b:SEQ * (b + 1)].unsqueeze(1).broadcast_to([P, 4, SEQ])
                v.tensor_tensor(qbd[:, b, :, :], qv, own, ALU.mult).then_inc(sig("qbd_ready"), 1)
            dve.wait_ge(sig("qbd_ready"), BATCH)
            dve.wait_ge(sig("mask_in"), 64)

            def take_heads(n):
                dve.wait_ge(sig("o1_ready"), 4 * n + 4)
                o = bank[6 + n % 2][:, :].rearrange("p (b j q) -> p b j q", b=4, j=4)
                t = otmp[:, :].rearrange("p (b j q) -> p b j q", b=4, j=4)
                own_b = wt("own4").unsqueeze(1).unsqueeze(3).broadcast_to([P, 4, 4, SEQ])
                v.tensor_tensor(t, o, own_b, ALU.mult).then_inc(sig("o1_taken"), 1)
                dve.wait_ge(sig("o1_taken"), n + 1)
                ch.link(v.tensor_reduce(oT[:, P * n:P * (n + 1)].rearrange("p (b q) -> p b q", b=4),
                                        t.rearrange("p b j q -> p b q j"), AX_X, ALU.add))

            for i in range(GROUPS * BATCH + 2):
                if i < GROUPS * BATCH:
                    dve.wait_ge(sig("s1_ready"), i + 1)
                    if i >= NS:
                        dve.wait_ge(sig("pT_ps"), i - NS + 1)
                    b = i // GROUPS
                    v.tensor_tensor_reduce(sc[i % NS], bank[i % NS][:, :], mask[:, KEYS * b:KEYS * (b + 1)], MASK_BIG, 3e38,
                                           ALU.add, ALU.min, smin[:, i:i + 1]).then_inc(sig("s1_min"), 1)
                j = i - 2
                if j >= 0 and j % 2 == 1:
                    dve.wait_ge(sig("pT_ps"), j + 1)
                    if j >= NPT:
                        dve.wait_ge(sig("o1_ready"), (j - NPT) // GROUPS + 1)
                    v.tensor_copy(pt[j % NPT], bank[3 + j % NT][:, :]).then_inc(sig("pT_odd"), 1)
                if i >= 24 and (i - 24) % 16 == 0:
                    take_heads((i - 24) // 16)
            take_heads(3)
            dve.wait_ge(sig("p1_ready"), GROUPS * BATCH)
            ch.link(v.reciprocal(rinv, rsum))
            mg4 = mg.rearrange("p (g b q) -> p g b q", g=4, b=BATCH)
            ri = rinv.rearrange("p (b g) -> p g b", g=GROUPS)
            rows = wt("rows32").unsqueeze(1).broadcast_to([P, BATCH, SEQ])
            dve.wait_ge(sig("o1_ready"), BATCH)
            for g in range(GROUPS):
                v.tensor_tensor(mg4[:, g, :, :], rows, ri[:, g, :].unsqueeze(2).broadcast_to([P, BATCH, SEQ]),
                                ALU.mult).then_inc(sig("mg_ready"), 1)
            dve.wait_ge(sig("rinv_ps"), 1)
            ch.link(v.tensor_tensor(oT, oT, bank[0][:, :], ALU.mult))
            v.tensor_scalar(oT, oT, wt("bv1"), None, ALU.add).then_inc(sig("o1T_ready"), 1)
            dve.wait_ge(sig("xo_ps"), 4)
            dve.wait_ge(sig("xb_ready"), 3)
            residual(bank[1][:, :], xb_tok[:, :])

            norm(x_tok[:, :], EPS_OUTER)
            ch.link(v.tensor_copy(xb_tok[:, :], xn_tok[:, :]))
            norm(xb_tok[:, :], EPS_INNER)
            dve.wait_ge(sig("qk_ps"), 1)
            ch.add(v.tensor_scalar(qp, bank[0][:, :], 0.0, STAB, ALU.max, ALU.add))
            dve.wait_ge(sig("qk_ps"), 2)
            v.tensor_scalar(kp_tok, bank[1][:, :], 0.0, STAB, ALU.max, ALU.add).then_inc(sig("kp_ready"), 1)
            ch.join()
            dve.wait_ge(sig("ksum_ps"), 1)
            ch.link(v.tensor_copy(ksum, bank[3][:, 0:BATCH]))
            v.tensor_tensor(bs(qk), bs(qp), ksum.unsqueeze(2).broadcast_to([P, BATCH, SEQ]), ALU.mult).then_inc(sig("qksum_ready"), 1)
            same4 = wt("samehead").unsqueeze(1).broadcast_to([P, 4, D])
            for n in range(4):
                dve.wait_ge(sig("kvs_ps"), 1)
                v.tensor_tensor(kvs[:, 512 * n:512 * (n + 1)].rearrange("p (t d) -> p t d", t=4),
                                bank[4 + n][:, :].rearrange("p (t d) -> p t d", t=4), same4, ALU.mult).then_inc(sig("kvs_ready"), 1)
            dve.wait_ge(sig("den_ps"), 1)
            ch.link(v.reciprocal(nump, bank[3][:, :]))
            dve.wait_ge(sig("num_ps"), 1)
            v.tensor_tensor(att, nump, bank[2][:, :], ALU.mult).then_inc(sig("att_ready"), 1)
            dve.wait_ge(sig("ao_ps"), 1)
            v.tensor_tensor(add1, bank[0][:, :], xb_tok[:, :], ALU.add).then_inc(sig("add1_ready"), 1)
            dve.wait_ge(sig("add1_ready"), 1)
            norm(add1, EPS_INNER)
            dve.wait_ge(sig("ffo_ps"), 1)
            v.tensor_tensor(tok3(g2), tok3(bank[4][:, :]), over_tiles(wt("b2")), ALU.add).then_inc(sig("ffo_ready"), 1)
            dve.wait_ge(sig("g2_ready"), 1)
            dve.wait_ge(sig("res_ready"), 1)
            residual(g2, res4)

            norm(x_tok[:, :], EPS_OUTER)
            ge = lambda a: a.rearrange("p (t e) -> p t e", e=E1)
            wide = lambda a: a.unsqueeze(2).broadcast_to([P, TT, E1])
            flat = lambda name: wt(name).unsqueeze(1).broadcast_to([P, TT, E1])
            dve.wait_ge(sig("gate_ps"), 1)
            ch.link(v.tensor_tensor(ge(mr[0]), ge(bank[7][:, 0:64]), flat("bg"), ALU.add))
            ch.link(v.tensor_reduce(m4[0], ge(mr[0]), AX_X, ALU.max))
            v.tensor_tensor(ge(mr[1]), ge(mr[0]), wide(m4[0]), ALU.subtract).then_inc(sig("gate_arg"), 1)
            dve.wait_ge(sig("gate_exp"), 1)
            ch.link(v.tensor_reduce(m4[1], ge(mr[2]), AX_X, ALU.add))
            ch.link(v.reciprocal(m4[2], m4[1]))
            ch.link(v.tensor_tensor(ge(mr[3]), ge(mr[2]), wide(m4[2]), ALU.mult))
            ch.link(v.tensor_reduce(m4[3], ge(mr[3]), AX_X, ALU.max))
            ch.link(v.tensor_tensor(ge(mr[4]), ge(mr[3]), wide(m4[3]), ALU.not_equal))
            ch.link(v.scalar_tensor_tensor(ge(mr[4]), ge(mr[4]), float(E1), flat("iota_e"), ALU.mult, ALU.add))
            ch.link(v.tensor_reduce(m4[4], ge(mr[4]), AX_X, ALU.min))
            v.tensor_tensor(ge(mr[5]), flat("iota_e"), wide(m4[4]), ALU.is_equal).then_inc(sig("onehot_ready"), 1)
            dve.wait_ge(sig("onehot_ready"), 1)
            dve.wait_ge(sig("count_ps"), 1)
            ch.link(v.scalar_tensor_tensor(ge(mr[6]), ge(bank[7][:, 64:128]), -1.0, ge(mr[5]), ALU.add, ALU.mult))
            ch.link(v.tensor_reduce(m4[5], ge(mr[6]), AX_X, ALU.add))
            ch.add(v.tensor_scalar(m4[6], m4[5], CAP - 0.5, float(4 * SLOTS), ALU.is_gt, ALU.mult))
            ch.link(v.scalar_tensor_tensor(m4[7], m4[4], float(CAP), m4[5], ALU.mult, ALU.add))
            ch.link(v.tensor_tensor(m4[7], m4[7], m4[6], ALU.add))
            for t in range(TT):
                v.tensor_scalar(disp[:, 512 * t:512 * (t + 1)], wt("iota_slot"), m4[7][:, t:t + 1], None,
                                ALU.is_equal).then_inc(sig("disp_ready"), 1)
            v.tensor_copy(tok3(slotbc), m4[7].unsqueeze(2).broadcast_to([P, TT, P])).then_inc(sig("slotbc_ready"), 1)
            dve.wait_ge(sig("buf_ps"), 1)
            v.tensor_copy(bufT, bank[4][:, :]).then_inc(sig("buf_ready"), 1)
            dve.wait_ge(sig("slotT_ps"), 1)
            for g in range(4):
                v.tensor_scalar(comb[:, 512 * g:512 * (g + 1)], bank[5][:, :], wt("slot_row")[:, g:g + 1], None,
                                ALU.is_equal).then_inc(sig("comb_ready"), 1)
            dve.wait_ge(sig("moeb_in"), 16)
            for g in range(4):
                dve.wait_ge(sig("hm_ps"), g + 1)
                v.tensor_tensor(hmoe[:, 512 * g:512 * (g + 1)], bank[g][:, :], b1e[:, 512 * g:512 * (g + 1)],
                                ALU.add).then_inc(sig("hm_ready"), 1)
            dve.wait_ge(sig("y_ps"), 4)
            v.tensor_tensor(ymoe, bank[6][:, :], b2e, ALU.add).then_inc(sig("y_ready"), 1)
            for t in range(TT):
                dve.wait_ge(sig("comb_ps"), t + 1)
                v.scalar_tensor_tensor(tok3(outt)[:, t, :], bank[t][:, 0:P], m4[3][:, t:t + 1], x3[:, t, :],
                                       ALU.mult, ALU.add).then_inc(sig("out_ready"), 1)

        @block.tensor
        def _(pe):
            mm = nc.tensor.matmul
            norms = [0]
            turned = [0]

            def turn_norm(*waits):
                i = norms[0]
                norms[0] += 1
                for name, n in waits:
                    pe.wait_ge(sig(name), n)
                for t in range(TT):
                    pe.wait_ge(sig("xn_ready"), TT * i + t + 1)
                    last = nc.tensor.transpose(bank[6][:, P * t:P * (t + 1)], xn3[:, t, :], wt("ident"))
                last.then_inc(sig("lnT_ps"), 1)
                turned[0] += 1

            def wait_norm():
                pe.wait_ge(sig("lnT_ready"), turned[0])

            def project_tokens(dst, srcT, w):
                for t in range(TT):
                    last = mm(dst[:, P * t:P * (t + 1)], srcT[:, P * t:P * (t + 1)], w, start=True, stop=True)
                return last

            pe.wait_ge(sig("early_in"), 16)
            turn_norm()
            wait_norm()
            mm(bank[7][:, :], wt("wq0"), lnT[:, :], start=True, stop=True).then_inc(sig("q0_ps"), 1)

            def keys0(c):
                pe.wait_ge(sig(f"ctx_in{c // 4}"), 16)
                if c >= 2:
                    pe.wait_ge(sig("prod_ready"), c - 1)
                mm(bank[c % 2][:, :], wt("wk0"), ctx[:, KEYS * c:KEYS * (c + 1)], start=True, stop=True).then_inc(sig("k0_ps"), 1)

            def headsum(n):
                for c in range(4 * n, 4 * n + 4):
                    pe.wait_ge(sig("prod_ready"), c + 1)
                    r = 32 * (c % 4)
                    last = mm(bank[2 + n // 2][r:r + 32, :], wt("headsum")[:, 32 * (n % 2):32 * (n % 2) + 32], prod4[c % 4],
                              start=(n % 2 == 0), stop=(n % 2 == 1), skip_group_check=True)
                last.then_inc(sig("s0_ps"), 1)

            for n in range(4):
                for c in range(4 * n, 4 * n + 4):
                    keys0(c)
                headsum(n)

            def values0(c):
                if c < 2:
                    pe.wait_ge(sig("prod_ready"), 1)
                else:
                    pe.wait_ge(sig("v0_ready"), c - 1)
                mm(bank[6 + c % 2][:, :], wt("wv0"), ctx[:, KEYS * c:KEYS * (c + 1)], start=True, stop=True).then_inc(sig("v0_ps"), 1)

            def spread0(c):
                pe.wait_ge(sig("p0_ready"), c // 8 + 1)
                if c >= 2:
                    pe.wait_ge(sig("vp_ready"), c - 1)
                r, h = 32 * (c % 4), (c // 4) % 2
                mm(bank[4 + c % 2][:, :], wt("headspread")[r:r + 32, P * h:P * (h + 1)], e0[c // 8][r:r + 32, :],
                   start=True, stop=True).then_inc(sig("p0_spread"), 1)

            values0(0)
            values0(1)
            for c in range(BATCH):
                spread0(c)
                if c + 2 < BATCH:
                    values0(c + 2)

            nproj = [0]

            def context(n):
                for _ in range(n):
                    i = nproj[0]
                    nproj[0] += 1
                    if i == 0:
                        pe.wait_ge(sig("late_in"), 16)
                    if i < 2:
                        pe.wait_ge(sig("vp_ready"), BATCH)
                    else:
                        pe.wait_ge(sig("proj_out"), i - 1)
                    dst = bank[4 + i % 2]
                    if i < BATCH:
                        last = mm(dst[:, :], wt("wk1"), ctx[:, KEYS * i:KEYS * (i + 1)], start=True, stop=True)
                    else:
                        b = i - BATCH
                        for k in range(KT):
                            at = KEYS * b + P * k
                            last = mm(dst[:, P * k:P * (k + 1)], ctx[:, at:at + P], wt("wv1"), start=True, stop=True)
                    last.then_inc(sig("proj_done"), 1)

            pe.wait_ge(sig("o0_ready"), BATCH)
            project_tokens(bank[0], o0T, wt("wo0")).then_inc(sig("xo_ps"), 1)

            context(2)
            turn_norm(("v0_ready", BATCH))
            wait_norm()
            context(2)
            for n, src in enumerate((xk, xv, xr)):
                pe.wait_ge(sig("mix_ready"), n + 1)
                mm(bank[n][:, :], wt(("rk", "rv", "rr")[n]), src, start=True, stop=True).then_inc(sig("rkvr_ps"), 1)
            context(12)
            pe.wait_ge(sig("rw_ready"), 1)
            project_tokens(bank[0], rw, wt("ro")).then_inc(sig("xo_ps"), 1)

            turn_norm(("lnT_ready", 2))
            wait_norm()
            for t in range(TT):
                last = mm(bank[6][:, E0 * t:E0 * (t + 1)], lnT[:, P * t:P * (t + 1)], wt("route"), start=True, stop=True)
            last.then_inc(sig("route_ps"), 1)
            for n in range(5):
                dst, w, rows = (bank[n], wt("rw1")[:, P * n:P * (n + 1)], P) if n < 4 else (bank[7], wt("sw1"), H0)
                if n == 4:
                    pe.wait_ge(sig("v0_ready"), BATCH)
                mm(dst[0:rows, :], w, lnT[:, :], start=True, stop=True).then_inc(sig("hid_ps"), 1)
            pe.wait_ge(sig("cf_ready"), 1)
            cf3 = fr[9].rearrange("p (t e) -> p t e", e=E0)
            for t in range(TT):
                last = nc.tensor.transpose(bank[6][0:E0, P * t:P * (t + 1)], cf3[:, t, :], wt("ident"))
            last.then_inc(sig("cfT_ps"), 1)
            pe.wait_ge(sig("cfT_ready"), 1)
            for n in range(4):
                pe.wait_ge(sig("hid_ready"), n + 1)
                mm(bank[n][:, :], wt("spread", E0)[:, P * n:P * (n + 1)], cfT, start=True, stop=True).then_inc(sig("spread_ps"), 1)
            pe.wait_ge(sig("hid_ready"), 5)
            pe.wait_ge(sig("hsc_ready"), 4)
            for t in range(TT):
                cols = slice(P * t, P * (t + 1))
                mm(bank[6][:, cols], cfT[:, cols], wt("rb2", E0), start=True, stop=False)
                mm(bank[6][:, cols], hid[4][0:H0, cols], wt("sw2", H0), start=False, stop=False)
                for n in range(4):
                    last = mm(bank[6][:, cols], hsc[n][:, cols], wt("rw2")[:, P * n:P * (n + 1)], start=False, stop=(n == 3))
            last.then_inc(sig("xo_ps"), 1)
            context(16)

            turn_norm(("x_new", 3))
            wait_norm()
            mm(bank[7][:, :], wt("wq1"), lnT[:, :], start=True, stop=True).then_inc(sig("q1_ps"), 1)
            pe.wait_ge(sig("proj_out"), 2 * BATCH)

            def scores(i):
                b, g = divmod(i, GROUPS)
                if i < NS:
                    pe.wait_ge(sig("qbd_ready"), BATCH)
                else:
                    pe.wait_ge(sig("s1_min"), i - NS + 1)
                r = slice(32 * g, 32 * g + 32)
                mm(bank[i % NS][:, :], qbd[r, b, :, :].rearrange("p j q -> p (j q)"), k1[r, KEYS * b:KEYS * (b + 1)],
                   start=True, stop=True).then_inc(sig("s1_ready"), 1)

            def turn(i):
                pe.wait_ge(sig("p1_ready"), i + 1)
                if i >= NT:
                    j = i - NT
                    pe.wait_ge(sig("pT_odd" if j % 2 else "pT_even"), j // 2 + 1)
                for k in range(KT):
                    last = nc.tensor.transpose(bank[3 + i % NT][:, P * k:P * (k + 1)], sc[i % NS][:, P * k:P * (k + 1)], wt("ident"))
                last.then_inc(sig("pT_ps"), 1)

            def outputs(b):
                pe.wait_ge(sig("pT_even"), 2 * b + 2)
                pe.wait_ge(sig("pT_odd"), 2 * b + 2)
                if b % 4 == 0 and b >= 8:
                    pe.wait_ge(sig("o1_taken"), b // 4 - 1)
                for k in range(KT):
                    for g in range(GROUPS):
                        r = slice(32 * g, 32 * g + 32)
                        last = mm(bank[6 + (b // 4) % 2][r, P * (b % 4):P * (b % 4 + 1)], vkey[:, b, k, r],
                                  pt[(GROUPS * b + g) % NPT][:, P * k:P * (k + 1)], start=(k == 0), stop=(k == KT - 1),
                                  skip_group_check=True)
                last.then_inc(sig("o1_ready"), 1)

            for i in range(GROUPS * BATCH + 6):
                if i < GROUPS * BATCH:
                    scores(i)
                if 2 <= i < GROUPS * BATCH + 2:
                    turn(i - 2)
                if i >= 7 and (i - 7) % GROUPS == 0:
                    outputs((i - 7) // GROUPS)
            for g in range(GROUPS):
                pe.wait_ge(sig("mg_ready"), g + 1)
                last = mm(bank[0][32 * g:32 * g + 32, :], wt("heads32"), mg[:, 512 * g:512 * (g + 1)], start=True, stop=True,
                          skip_group_check=True)
            last.then_inc(sig("rinv_ps"), 1)
            pe.wait_ge(sig("o1T_ready"), 1)
            project_tokens(bank[1], oT, wt("wo1")).then_inc(sig("xo_ps"), 1)

            norms[0] += 1
            turn_norm(("o1_taken", 4))
            wait_norm()
            mm(bank[0][:, :], wt("lq"), lnT[:, :], start=True, stop=True).then_inc(sig("qk_ps"), 1)
            project_tokens(bank[1], lnT, wt("lk")).then_inc(sig("qk_ps"), 1)
            project_tokens(bank[2], lnT, wt("lv")).then_inc(sig("vtok_ps"), 1)
            pe.wait_ge(sig("kp_ready"), 1)
            for t in range(TT):
                last = mm(bank[3][:, 4 * t:4 * t + 4], kp_tok[:, P * t:P * (t + 1)], wt("batchof"), start=True, stop=True)
            last.then_inc(sig("ksum_ps"), 1)
            pe.wait_ge(sig("vtok_ready"), 1)
            for t in range(TT):
                for b in range(4):
                    r = slice(32 * b, 32 * b + 32)
                    last = mm(bank[4 + b][:, P * t:P * (t + 1)], kp_tok[r, P * t:P * (t + 1)], v_tok[r, P * t:P * (t + 1)],
                              start=True, stop=True)
            last.then_inc(sig("kvs_ps"), 1)
            pe.wait_ge(sig("qksum_ready"), 1)
            mm(bank[3][:, :], wt("samehead"), qk, start=True, stop=True).then_inc(sig("den_ps"), 1)
            for n in range(4):
                pe.wait_ge(sig("kvs_ready"), n + 1)
                for t in range(TT):
                    b, at = 4 * t + n, 512 * n + P * t
                    last = mm(bank[2][:, SEQ * b:SEQ * (b + 1)], kvs[:, at:at + P], qp[:, SEQ * b:SEQ * (b + 1)],
                              start=True, stop=True)
            last.then_inc(sig("num_ps"), 1)
            pe.wait_ge(sig("att_ready"), 1)
            project_tokens(bank[0], att, wt("lo")).then_inc(sig("ao_ps"), 1)
            turn_norm()
            wait_norm()
            for n in range(4):
                mm(bank[n][:, :], wt("w1")[:, P * n:P * (n + 1)], lnT[:, :], start=True, stop=True).then_inc(sig("ffh_ps"), 1)
            pe.wait_ge(sig("ffh_ready"), 4)
            for t in range(TT):
                for n in range(4):
                    last = mm(bank[4][:, P * t:P * (t + 1)], hT[:, 512 * n + P * t:512 * n + P * (t + 1)],
                              wt("w2")[:, P * n:P * (n + 1)], start=(n == 0), stop=(n == 3))
            last.then_inc(sig("ffo_ps"), 1)

            turn_norm()
            wait_norm()
            for t in range(TT):
                last = mm(bank[7][:, E1 * t:E1 * (t + 1)], lnT[:, P * t:P * (t + 1)], wt("wg"), start=True, stop=True)
            last.then_inc(sig("gate_ps"), 1)
            pe.wait_ge(sig("onehot_ready"), 1)
            oh = mr[5].rearrange("p (t e) -> p t e", e=E1)
            for t in range(TT):
                dst = bank[7][:, 64 + E1 * t:64 + E1 * (t + 1)]
                for s in range(t):
                    mm(dst, wt("ones"), oh[:, s, :], start=(s == 0), stop=False)
                last = mm(dst, wt("upto"), oh[:, t, :], start=(t == 0), stop=True)
            last.then_inc(sig("count_ps"), 1)
            for t in range(TT):
                pe.wait_ge(sig("disp_ready"), t + 1)
                last = mm(bank[4][:, :], xn3[:, t, :], disp[:, 512 * t:512 * (t + 1)], start=(t == 0), stop=(t == TT - 1))
            last.then_inc(sig("buf_ps"), 1)
            pe.wait_ge(sig("slotbc_ready"), 1)
            for t in range(TT):
                last = nc.tensor.transpose(bank[5][:, P * t:P * (t + 1)], tok3(slotbc)[:, t, :], wt("ident"))
            last.then_inc(sig("slotT_ps"), 1)
            pe.wait_ge(sig("w1_in"), 16)
            pe.wait_ge(sig("buf_ready"), 1)
            for g in range(4):
                for j in range(4):
                    e = 4 * g + j
                    last = mm(bank[g][32 * j:32 * j + 32, :], bufT[:, CAP * e:CAP * (e + 1)], w1e[:, e, :], start=True, stop=True,
                              skip_group_check=True)
                last.then_inc(sig("hm_ps"), 1)
            for g in range(4):
                pe.wait_ge(sig("hm_ready"), g + 1)
                for k in range(4):
                    last = nc.tensor.transpose(bank[g][:, P * k:P * (k + 1)], hmoe[:, 512 * g + P * k:512 * g + P * (k + 1)], wt("ident"))
                last.then_inc(sig("hmT_ps"), 1)
            pe.wait_ge(sig("w2_in"), 16)
            for g in range(4):
                pe.wait_ge(sig("hmT_ready"), g + 1)
                for k in range(4):
                    for j in range(4):
                        at = 512 * g + P * k + CAP * j
                        last = mm(bank[6][32 * j:32 * j + 32, P * g:P * (g + 1)], hmoeT[:, at:at + CAP], w2e[:, 4 * g + j, k, :],
                                  start=(k == 0), stop=(k == 3), skip_group_check=True)
                last.then_inc(sig("y_ps"), 1)
            pe.wait_ge(sig("y_ready"), 1)
            pe.wait_ge(sig("comb_ready"), 4)
            for t in range(TT):
                for g in range(4):
                    last = mm(bank[t][:, 0:P], comb[:, 512 * g + P * t:512 * g + P * (t + 1)], ymoe[:, P * g:P * (g + 1)],
                              start=(g == 0), stop=(g == 3))
                last.then_inc(sig("comb_ps"), 1)


def constants():
    p, one = np.arange(P), np.float32
    r = p[:, None]
    f = np.arange(P)[None, :]
    out = {
        "ident": r == f,
        "headsum": np.concatenate([(np.arange(32) // 16 == h) & (np.arange(32) % 16 == r // HD) for h in range(2)], 1),
        "headspread": np.concatenate([(r % 32 // 16 == h) & (r % 16 == f // HD) for h in range(2)], 1),
        "spread": np.concatenate([r == 2 * n + f // H0 for n in range(4)], 1),
        "before": np.broadcast_to(np.tril(np.ones((E0, E0)), -1).reshape(1, -1), (P, E0 * E0)),
        "own4": r // HD % 4 == np.arange(4)[None, :],
        "rows32": r % 32 == np.arange(32)[None, :],
        "heads32": r // 32 == np.arange(32)[None, :] // HD,
        "samehead": r // HD == f // HD,
        "batchof": r // SEQ == np.arange(4)[None, :],
        "iota_e": np.broadcast_to(np.arange(E1)[None, :], (P, E1)),
        "iota_slot": np.broadcast_to(np.arange(SLOTS)[None, :], (P, SLOTS)),
        "slot_row": P * np.arange(4)[None, :] + r,
        "upto": r <= f,
        "ones": np.ones((P, P)),
    }
    return {k: np.ascontiguousarray(v).astype(one) for k, v in out.items()}


def kernel(**inputs):
    import concourse.bacc as bacc
    from concourse.bass_utils import run_bass_kernel_spmd

    a = {k: np.asarray(v) for k, v in inputs.items()}

    def col(name):
        return a[name].reshape(-1, 1)

    def rows(name):
        return np.broadcast_to(a[name].reshape(1, -1), (P, a[name].size))

    def tiles(m):
        return m.reshape(-1, P, m.shape[-1]).transpose(1, 0, 2).reshape(P, -1)

    parts = dict(constants())
    parts.update(
        wq0=a["L0_xattn_Wq"].T, wk0=a["L0_xattn_Wk"].T, wv0=a["L0_xattn_Wv"].T, wo0=a["L0_xattn_Wo"].T,
        bq0=col("L0_xattn_bq"), bk0=col("L0_xattn_bk"), bv0=col("L0_xattn_bv"), bo0=rows("L0_xattn_bo"),
        rk=a["L0_attn_Wk"].T, rv=a["L0_attn_Wv"].T, rr=a["L0_attn_Wr"].T, ro=a["L0_attn_Wo"].T,
        w=col("L0_attn_w"), u=col("L0_attn_u"), mk=col("L0_attn_mix_k"), mv=col("L0_attn_mix_v"), mr=col("L0_attn_mix_r"),
        route=a["L0_ffn_routing_W"].T, eb=rows("L0_ffn_expert_bias"), sw1=a["L0_ffn_sW1"], sb1=col("L0_ffn_sb1"),
        rw1=a["L0_ffn_rW1"].transpose(1, 0, 2).reshape(P, -1), rb1=a["L0_ffn_rb1"].reshape(4, P).T,
        rw2=tiles(a["L0_ffn_rW2"].reshape(E0 * H0, D)), sw2=a["L0_ffn_sW2"], rb2=a["L0_ffn_rb2"], sb2=rows("L0_ffn_sb2"),
        wq1=a["L1_xattn_Wq"], wk1=a["L1_xattn_Wk"], wv1=a["L1_xattn_Wv"], wo1=a["L1_xattn_Wo"],
        bq1=col("L1_xattn_bq"), bk1=col("L1_xattn_bk"), bv1=col("L1_xattn_bv"), bo1=rows("L1_xattn_bo"),
        gamma=col("L1_attn_gamma1"), beta=col("L1_attn_beta1"), lq=a["L1_attn_wq"].reshape(D, D), lk=a["L1_attn_wk"].reshape(D, D),
        lv=a["L1_attn_wv"].reshape(D, D), lo=a["L1_attn_wo"].reshape(D, D), w1=a["L1_attn_w1"],
        b1=a["L1_attn_b1"].reshape(4, P).T, w2=tiles(a["L1_attn_w2"]), b2=rows("L1_attn_b2"),
        wg=a["L1_ffn_Wg"], bg=rows("L1_ffn_bg"),
    )

    def pack(layout):
        out = np.zeros((P, width(layout)), np.float32)
        for name, (lo, hi) in columns(layout).items():
            out[:parts[name].shape[0], lo:hi] = parts[name]
        return out

    def slots(b):
        n = b.shape[1]
        return np.broadcast_to(b.reshape(4, 4, 1, n).transpose(1, 2, 0, 3), (4, CAP, 4, n)).reshape(P, 4 * n)

    arrays = {
        "x": a["x"].reshape(TOK, D),
        "early": pack(EARLY),
        "late": pack(LATE),
        "ctx": a["ctx_1024"].reshape(CTX, D).T,
        "mask": a["mask_Bx1xSxS2_fk0"].transpose(2, 0, 1, 3).reshape(SEQ, CTX),
        "moe_w1": a["L1_ffn_W1"].transpose(1, 0, 2).reshape(D, E1 * H1),
        "moe_w2": a["L1_ffn_W2"].reshape(E1, 4, P, D).transpose(2, 0, 1, 3).reshape(P, E1 * H1),
        "moe_b": np.concatenate([slots(a["L1_ffn_b1"]), slots(a["L1_ffn_b2"])], axis=1),
    }
    arrays = {k: np.ascontiguousarray(v) for k, v in arrays.items()}
    nc = bacc.Bacc("TRN2", target_bir_lowering=False, num_devices=1)
    args = [nc.dram_tensor(k, v.shape, F32, kind="ExternalInput").ap() for k, v in arrays.items()]
    args.append(nc.dram_tensor("out", (TOK, D), F32, kind="ExternalOutput").ap())
    program(nc, *args)
    done = run_bass_kernel_spmd(nc, [arrays], core_ids=[0])
    return done.results[0]["out"].reshape(BATCH, SEQ, D)
```

```python
from contextlib import ExitStack

import numpy as np
import concourse.bass as bass
from concourse import mybir

F32 = mybir.dt.float32
ALU = mybir.AluOpType
ACT = mybir.ActivationFunctionType
AX_X = mybir.AxisListType.X

P = 128
BATCH, SEQ, D = 16, 32, 128
TOK = BATCH * SEQ
TT = TOK // P
KEYS = 512
CTX = BATCH * KEYS
HEADS, HD = 16, 8
GROUPS = 4
LOCAL = KEYS // SEQ
KT = KEYS // P
HB, HT, HTOK = BATCH // 2, TT // 2, TOK // 2
UNITS = HB * GROUPS
E0, H0 = 8, 64
E1, H1 = 16, 512
CAP = TOK // E1
SLOTS = E1 * CAP
FF = 512
QSCALE = float(1.0 / np.sqrt(np.float32(HD)))
MASK_BIG = 1e15
NEG_STATE = -1e30
STAB = 0.001
EPS_OUTER, EPS_INNER = 1e-5, 1e-6

EARLY = [("ident", 128), ("bq0", 1), ("bk0", 1), ("bv0", 1), ("wq0", 128), ("wk0", 128), ("wv0", 128),
         ("wo0", 128), ("headsum", 64), ("headspread", 256), ("rowblock", 4), ("bo0", 128)]
LATE = [("rk", 128), ("rv", 128), ("rr", 128), ("ro", 128), ("w", 1), ("u", 1), ("mk", 1), ("mv", 1), ("mr", 1),
        ("route", E0), ("eb", E0), ("sw1", H0), ("sb1", 1), ("rw1", 512), ("rb1", 4), ("rw2", 512), ("sw2", 128),
        ("rb2", 128), ("sb2", 128), ("spread", 512), ("before", E0 * E0),
        ("wq1", 128), ("wk1", 128), ("wv1", 128), ("wo1", 128), ("bq1", 1), ("bk1", 1), ("bv1", 1), ("bo1", 128),
        ("own4", 4), ("own16", HEADS), ("rows32", 32), ("heads32", 32),
        ("gamma", 1), ("beta", 1), ("lq", 128), ("lk", 128), ("lv", 128), ("lo", 128), ("w1", FF), ("b1", 4),
        ("w2", FF), ("b2", 128), ("samehead", 128), ("batchof", 4),
        ("wg", E1), ("bg", E1), ("iota_e", E1), ("iota_slot", SLOTS), ("slot_row", 4), ("upto", 128), ("ones", 128)]


def width(pack):
    return sum(n for _, n in pack)


def columns(pack):
    at, out = 0, {}
    for name, n in pack:
        out[name] = (at, at + n)
        at += n
    return out


OUT = 7
TAKE = 4 * GROUPS + OUT - GROUPS + 2


class Shifted:

    def __init__(self, tiles):
        self.tiles = tiles

    def __getitem__(self, at):
        return self.tiles[at[1]]


class Chain:

    def __init__(self, eng, sem):
        self.eng, self.sem, self.n = eng, sem, 0

    def add(self, ins):
        self.n += 1
        ins.then_inc(self.sem, 1)

    def join(self):
        self.eng.wait_ge(self.sem, self.n)

    def link(self, ins):
        self.add(ins)
        self.join()


def program(nc, x_d, early_d, late_d, ctx_d, mask_d, w1_d, w2_d, moeb_d, out_d):
    with ExitStack() as stack:
        def sb(name, cols, rows=P):
            return stack.enter_context(nc.sbuf_tensor(name + "_sb", [rows, cols], F32))

        sems = {}

        def sig(name):
            if name not in sems:
                sems[name] = stack.enter_context(nc.semaphore(name))
            return sems[name]

        bank = [stack.enter_context(nc.psum_tensor(f"bank{i}", [P, 512], F32)) for i in range(8)]

        early, late = sb("early", width(EARLY)), sb("late", width(LATE))
        ce, cl = columns(EARLY), columns(LATE)

        def wt(name, rows=P):
            if name in ce:
                return early[0:rows, ce[name][0]:ce[name][1]]
            return late[0:rows, cl[name][0]:cl[name][1]]

        ctx = sb("ctx", CTX)
        k1 = sb("k1", CTX)
        v1 = sb("v1", CTX)
        mask = sb("mask", CTX)
        x_tok = sb("x_tok", TOK)
        xb_tok = sb("xb_tok", TOK)
        xn_tok = sb("xn_tok", TOK)
        lnT = sb("lnT", TOK)
        work = sb("work", 16 * 512)
        otmp = sb("otmp", 512)
        o0 = sb("o0", TOK)
        stats, aggr = sb("stats", TT * 6), sb("aggr", TT * 2)
        veps, rstd, minus_half, half = sb("veps", 2 * TT), sb("rstd", 2 * TT), sb("minus_half", 2 * TT), sb("half", TT * E0)
        small = sb("small", 1024)

        def tile(i, n=1, of=work):
            return of[:, 512 * i:512 * (i + n)]

        def tok3(a):
            return a.rearrange("p (t d) -> p t d", t=TT)

        x3, xb3, xn3 = tok3(x_tok[:, :]), tok3(xb_tok[:, :]), tok3(xn_tok[:, :])
        st3, ag3 = stats[:, :].rearrange("p (t k) -> p t k", t=TT), aggr[:, :].rearrange("p (t k) -> p t k", t=TT)

        def over_tiles(row):
            return row.unsqueeze(1).broadcast_to([P, TT, D])


        def cols(h):
            return slice(HTOK * h, HTOK * (h + 1))

        def tiles_of(h):
            return range(HT * h, HT * (h + 1))

        def part(region, sizes, at):
            out = []
            for n in sizes:
                out.append(region[:, at:at + n])
                at += n
            return out, at

        X, Y, Z = bank[5], bank[6], bank[7]

        q0T, e0 = tile(0), tile(2)
        o0T = o0[:, :]
        v0s, vp = [tile(3), tile(4)], [tile(5), tile(6)]
        prod = [tile(7 + i) for i in range(HB)]
        mx0, sm0, rs0 = small[:, 0:32], small[:, 32:64], small[:, 64:96]
        wexp = small[:, 96:97]
        hspread = [tile(1)[:, 0:256], tile(1)[:, 256:512], otmp[:, 0:256], otmp[:, 256:512]]

        S33 = SEQ + 1
        N33 = HB * S33

        def b33(a):
            return a.rearrange("p (b s) -> p b s", s=S33)

        def now(a):
            return b33(a)[:, :, 1:S33]

        def prev(a):
            return b33(a)[:, :, 0:SEQ]

        def bs(a):
            return a.rearrange("p (b s) -> p b s", s=SEQ)

        MH = CTX // 2
        (ln33, dec33, k33, o33, A33, B33, Bv33), at = part(mask, [N33] * 7, MH)
        q33, p33 = o33, B33
        (dx, xk, xv, xr, ab, er, v_sb), at = part(mask, [HTOK] * 4 + [2 * HTOK] + [HTOK] * 2, at)
        top, t_bv, num, den = xk, dx, xv, xr
        assert at <= CTX

        hid, at = part(mask, [HTOK] * 5, MH)
        (cfT, fc0, fc1), at = part(mask, [HTOK, HT * E0 * E0, HT * E0 * E0], at)
        cfT = cfT[0:E0, :]
        fr = [small[:, 100 + HT * E0 * i:100 + HT * E0 * (i + 1)] for i in range(10)]

        NQ = 4
        qbd = [tile(i) for i in range(NQ)]
        NS, NT, NSC, NPT = 2, 2, 3, 8
        q1T = tile(15)
        sc = [tile(4 + i) for i in range(NSC)]
        pt = [tile(7 + i) for i in range(NPT)]
        rsum, rinv, smin = small[:, 640:704], small[:, 704:768], small[:, 768:832]
        oT = q1T
        vkey = v1[:, :].rearrange("p (b k f) -> p b k f", b=BATCH, k=KT)

        (qp, att, qk, rden, kp_tok, add1, res4, g2), at = part(mask, [HTOK] * 8, 0)
        (vb, kvs), at = part(mask, [2 * HT * 256, 2 * HT * 256], at)
        assert at <= MH
        hT, mg = kvs, kvs
        ksum = small[:, 832:832 + HB]

        w1e = ctx[:, :].rearrange("p (e h) -> p e h", e=E1)
        w2e = k1[:, :].rearrange("p (e k d) -> p e k d", e=E1, k=4)
        moeb = v1[:, 0:2560]
        b1e, b2e = moeb[:, 0:2048], moeb[:, 2048:2560]
        (disp, comb, slotbc), at = part(v1, [2048, 2048, 512], 2560)
        (bufT, hmoe, hmoeT, ymoe, outt), at = part(mask, [512, 2048, 2048, 512, 512], 0)
        mr = [small[:, 64 * i:64 * (i + 1)] for i in range(8)]
        m4 = [small[:, 512 + 4 * i:516 + 4 * i] for i in range(8)]

        NCH = 4
        PIECE = CTX // NCH
        PROJ = [(kind, b) for h in range(2) for kind in "kv" for b in range(HB * h, HB * (h + 1))]
        GAP = 3

        def pace_local(step):
            return 1 if step <= 2 * HB or step % 2 == 0 else 0

        def pace_full(step):
            return 1 if step % 8 != 7 else 0

        def pace_last(step):
            return 1 if step % 2 == 0 else 0

        def advance(stages, n):
            for _ in range(n):
                next(stages, None)

        def finish(stages):
            for _ in stages:
                pass

        block = stack.enter_context(nc.Block())

        @block.sync
        def _(sp):
            sp.dma_start(x3, x_d.rearrange("(t p) d -> p t d", p=P)).then_inc(sig("x_in"), 16)
            sp.dma_start(early[:, :], early_d).then_inc(sig("early_in"), 16)
            for c in range(NCH):
                sp.dma_start(ctx[:, c * PIECE:(c + 1) * PIECE], ctx_d[:, c * PIECE:(c + 1) * PIECE]).then_inc(sig(f"ctx_in{c}"), 16)
                if c == 1:
                    sp.dma_start(late[:, :], late_d).then_inc(sig("late_in"), 16)
            for j in range(4):
                sp.dma_start(mask[32 * j:32 * j + 32, 0:MH], mask_d[:, 0:MH]).then_inc(sig("mask_in0"), 16)
            sp.wait_ge(sig("proj_done"), len(PROJ))
            sp.dma_start(ctx[:, :], w1_d).then_inc(sig("w1_in"), 16)
            sp.wait_ge(sig("x_new"), 6)
            for j in range(4):
                sp.dma_start(mask[32 * j:32 * j + 32, MH:CTX], mask_d[:, MH:CTX]).then_inc(sig("mask_in1"), 16)
            sp.wait_ge(sig("s1_ready"), 2 * UNITS)
            sp.dma_start(k1[:, :], w2_d).then_inc(sig("w2_in"), 16)
            sp.wait_ge(sig("o1_ready"), BATCH)
            sp.dma_start(moeb, moeb_d).then_inc(sig("moeb_in"), 16)
            sp.wait_ge(sig("out_ready"), TT)
            sp.dma_start(out_d.rearrange("(t p) d -> p t d", p=P), tok3(outt)).then_inc(sig("stored"), 16)
            sp.wait_ge(sig("stored"), 16)

        @block.gpsimd
        def _(pool):
            g = nc.gpsimd
            pool.memset(minus_half[:, :], -0.5).then_inc(sig("half_ready"), 1)
            pool.memset(half[:, :], 0.5).then_inc(sig("half_ready"), 1)
            pool.wait_ge(sig("half_ready"), 2)
            norms = [0]

            def inverse_std(tiles, extra=False):
                norms[0] += 1
                pool.wait_ge(sig("ln_var"), norms[0])
                views = [a[:, :].rearrange("p (k t) -> p k t", k=2)[:, 0:2 if extra else 1, tiles.start:tiles.stop]
                         for a in (rstd, veps, minus_half)]
                g.tensor_tensor(*views, ALU.pow).then_inc(sig("ln_rstd"), 1)

            def residual_bias(name, tiles, count):
                if count:
                    pool.wait_ge(sig("x_new"), count)
                t = slice(tiles.start, tiles.stop)
                g.tensor_tensor(xb3[:, t, :], x3[:, t, :], over_tiles(wt(name))[:, 0:len(tiles), :],
                                ALU.add).then_inc(sig("xb_ready"), 1)

            def edges():
                for a, v in ((ln33, 0.0), (k33, NEG_STATE), (A33, 0.0), (B33, 0.0), (Bv33, 0.0), (dec33, NEG_STATE)):
                    pool.memset(b33(a)[:, :, 0:1], v).then_inc(sig("edges_ready"), 1)

            def queries(h, lo, hi):
                own = wt("own16").unsqueeze(2).broadcast_to([P, HEADS, SEQ])
                if lo == 0:
                    pool.wait_ge(sig("q1_ready"), h + 1)
                    pool.wait_ge(sig("p0_spread"), BATCH)
                    pool.wait_ge(sig("vp_ready"), BATCH)
                    pool.wait_ge(sig("prod_ready"), BATCH)
                for b in range(HB * h + lo, HB * h + hi):
                    if b >= NQ:
                        pool.wait_ge(sig("s1_ready"), GROUPS * (b - NQ + 1))
                    qv = q1T[:, SEQ * b:SEQ * (b + 1)].unsqueeze(1).broadcast_to([P, HEADS, SEQ])
                    g.tensor_tensor(qbd[b % NQ].rearrange("p (j q) -> p j q", j=HEADS), qv, own, ALU.mult)\
                        .then_inc(sig("qbd_ready"), 1)

            def full(h, stages, pace):
                for i in range(UNITS + 2):
                    b = i // GROUPS + NQ - 1
                    if i % GROUPS == 0 and NQ <= b < HB:
                        queries(h, b, b + 1)
                    advance(stages, pace(i))
                finish(stages)

            def small_stages(h):
                tiles = tiles_of(h)
                yield
                if h:
                    pool.wait_ge(sig("x_new"), 3)
                edges()
                inverse_std(tiles)
                yield
                yield
                yield
                yield
                yield
                pool.wait_ge(sig("ab_exp"), h + 1)
                pool.wait_ge(sig("v_out"), h + 1)
                g.tensor_tensor(t_bv, ab[:, HTOK:2 * HTOK], v_sb, ALU.mult).then_inc(sig("bonus_ready"), 1)
                yield
                yield
                yield
                yield
                yield
                yield
                inverse_std(tiles)
                residual_bias("sb2", tiles, 3 * h + 2)
                yield
                yield
                yield
                yield
                pool.wait_ge(sig("softplus_ready"), h + 1)
                g.tensor_tensor(fr[6], fr[5], half[:, 0:HT * E0], ALU.pow).then_inc(sig("act_ready"), 1)
                yield
                yield
                yield
                yield
                yield
                yield
                inverse_std(tiles)
                residual_bias("bo1", tiles, 3 * h + 3)
                yield
                yield
                yield

            def linear_stages(h):
                yield
                yield
                yield
                inverse_std(tiles_of(h), extra=True)
                yield
                for _ in range(6):
                    yield
                inverse_std(tiles_of(h))
                g.tensor_tensor(res4, x_tok[:, cols(h)], add1, ALU.add).then_inc(sig("res_ready"), 1)
                yield

            inverse_std(range(TT))
            pool.wait_ge(sig("x_in"), 16)
            pool.wait_ge(sig("early_in"), 16)
            for j in range(4):
                g.tensor_tensor(hspread[j], wt("headspread"), wt("rowblock")[:, j:j + 1].broadcast_to([P, 256]),
                                ALU.mult).then_inc(sig("hspread_ready"), 1)
            residual_bias("bo0", range(TT), 0)
            finish(small_stages(0))
            queries(0, 0, NQ)
            full(0, small_stages(1), pace_full)
            queries(1, 0, NQ)
            full(1, linear_stages(0), pace_last)
            finish(linear_stages(1))
            inverse_std(range(TT))

        @block.scalar
        def _(act):
            s = nc.scalar
            turned = [0]

            def normT(dst, src, **affine):
                turned[0] += 1
                act.wait_ge(sig("lnT_ps"), turned[0])
                s.activation(dst, src, ACT.Identity, **affine).then_inc(sig("lnT_ready"), 1)

            nproj = [0]

            def projection():
                i = nproj[0]
                nproj[0] += 1
                kind, b = PROJ[i]
                act.wait_ge(sig("proj_done"), i + 1)
                src = bank[3 + i % 2][:, :]
                dst = (k1 if kind == "k" else v1)[:, KEYS * b:KEYS * (b + 1)]
                if kind == "k":
                    s.activation(dst, src, ACT.Identity, bias=wt("bk1")).then_inc(sig("proj_out"), 1)
                else:
                    s.copy(dst, src).then_inc(sig("proj_out"), 1)

            def local(h, stages, pace):
                step = 0
                for c in range(HB):
                    advance(stages, pace(step))
                    step += 1
                act.wait_ge(sig("e0_arg"), h + 1)
                s.activation(e0, e0, ACT.Exp).then_inc(sig("e0_exp"), 1)

                def values(c):
                    act.wait_ge(sig("v0_ps"), c + 1)
                    if c >= 2:
                        act.wait_ge(sig("vp_ready"), c - 1)
                    s.activation(v0s[c % 2], bank[c % 2][:, :], ACT.Identity, bias=wt("bv0")).then_inc(sig("v0_ready"), 1)

                values(HB * h)
                values(HB * h + 1)
                if h == 0:
                    act.wait_ge(sig("late_in"), 16)
                for _ in range(GAP):
                    projection()
                advance(stages, pace(step))
                step += 1
                for c in range(HB * h, HB * (h + 1)):
                    if c + 2 < HB * (h + 1):
                        values(c + 2)
                    advance(stages, pace(step))
                    step += 1
                if h:
                    while nproj[0] < len(PROJ):
                        projection()
                        advance(stages, pace(step))
                        step += 1

            def small_stages(h):
                yield
                yield
                yield
                if h == 0:
                    s.activation(wexp, wt("w"), ACT.Exp).then_inc(sig("wexp_raw"), 1)
                act.wait_ge(sig("edges_ready"), 6 * h + 6)
                normT(now(ln33), bs(X[:, 0:HTOK]))
                yield
                yield
                act.wait_ge(sig("rkvr_ps"), 3 * h + 2)
                s.copy(now(k33), bs(X[:, 0:HTOK])).then_inc(sig("k_out"), 1)
                s.copy(v_sb, X[:, HTOK:2 * HTOK]).then_inc(sig("v_out"), 1)
                act.wait_ge(sig("rkvr_ps"), 3 * h + 3)
                s.activation(er, Y[:, 0:HTOK], ACT.Exp, scale=-1.0).then_inc(sig("er_ready"), 1)
                yield
                act.wait_ge(sig("ab_arg"), 2 * h + 2)
                s.activation(ab, ab, ACT.Exp).then_inc(sig("ab_exp"), 1)
                for n, a in enumerate((A33, B33)):
                    act.wait_ge(sig("AB_arg"), 2 * h + n + 1)
                    s.activation(now(a), now(a), ACT.Exp).then_inc(sig("AB_exp"), 1)
                yield
                yield
                yield
                yield
                yield
                yield
                yield
                yield
                normT(lnT[:, cols(h)], X[:, 0:HTOK])
                yield
                act.wait_ge(sig("abs_ready"), h + 1)
                s.activation(fr[2], fr[1], ACT.Exp, scale=-1.0).then_inc(sig("e_ready"), 1)
                act.wait_ge(sig("w_ready"), h + 1)
                s.activation(fr[4], fr[3], ACT.Ln).then_inc(sig("ln_ready"), 1)
                yield
                for n in range(5):
                    act.wait_ge(sig("hid_ps"), 3 * h + (1, 1, 2, 2, 3)[n])
                    rows = P if n < 4 else H0
                    src = (X[:, 0:HTOK], X[:, HTOK:], Y[:, 0:HTOK], Y[:, HTOK:], Z[0:H0, 0:HTOK])[n]
                    bias = wt("rb1")[:, n:n + 1] if n < 4 else wt("sb1", H0)
                    s.activation(hid[n][0:rows, :], src, ACT.Silu, bias=bias).then_inc(sig("hid_ready"), 1)
                yield
                yield
                yield
                yield
                yield
                yield
                yield
                yield
                normT(lnT[:, cols(h)], X[:, 0:HTOK])
                yield
                yield

            def full(h, stages, pace):
                for i in range(UNITS + 2):
                    u = UNITS * h + i
                    if i < UNITS:
                        act.wait_ge(sig("s1_min"), u + 1)
                        s.activation(sc[u % NSC], sc[u % NSC], ACT.Exp, bias=smin[:, u:u + 1], scale=-1.0,
                                     accum_out=rsum[:, u:u + 1]).then_inc(sig("p1_ready"), 1)
                    j = u - 2
                    if i >= 2 and j % 2 == 0:
                        act.wait_ge(sig("pT_ps"), j + 1)
                        if j >= NPT:
                            act.wait_ge(sig("o1_ready"), (j - NPT) // GROUPS + 1)
                        s.copy(pt[j % NPT], bank[2 + j % NT][:, :]).then_inc(sig("pT_even"), 1)
                    advance(stages, pace(i))

            def linear_stages(h):
                yield
                yield
                yield
                yield
                yield
                normT(lnT[:, cols(h)], X[:, 0:HTOK], scale=wt("gamma"), bias=wt("beta"))
                yield
                yield
                yield
                yield
                yield
                yield
                yield
                normT(lnT[:, cols(h)], X[:, 0:HTOK], scale=wt("gamma"), bias=wt("beta"))
                yield
                for n in range(4):
                    act.wait_ge(sig("ffh_ps"), 2 * h + n // 2 + 1)
                    s.activation(hT[:, HTOK * n:HTOK * (n + 1)], (Y, Z)[n // 2][:, HTOK * (n % 2):HTOK * (n % 2 + 1)], ACT.Gelu,
                                 bias=wt("b1")[:, n:n + 1]).then_inc(sig("ffh_ready"), 1)
                yield
                act.wait_ge(sig("ffo_ready"), h + 1)
                s.activation(g2, g2, ACT.Gelu).then_inc(sig("g2_ready"), 1)
                yield

            act.wait_ge(sig("early_in"), 16)
            normT(lnT[:, :], X[:, :])
            local(0, iter(()), pace_local)
            stages = small_stages(0)
            local(1, stages, pace_local)
            finish(stages)
            stages = small_stages(1)
            full(0, stages, pace_full)
            finish(stages)
            stages = linear_stages(0)
            full(1, stages, pace_last)
            finish(stages)
            finish(linear_stages(1))
            normT(lnT[:, :], X[:, :])
            act.wait_ge(sig("gate_arg"), 1)
            s.activation(mr[2], mr[1], ACT.Exp).then_inc(sig("gate_exp"), 1)
            for g in range(4):
                act.wait_ge(sig("hmT_ps"), g + 1)
                s.activation(hmoeT[:, 512 * g:512 * (g + 1)], bank[g][:, :], ACT.Relu).then_inc(sig("hmT_ready"), 1)

        @block.vector
        def _(dve):
            v = nc.vector
            ch = Chain(dve, sig("dve_step"))
            norms, ready, xver = [0], [0], [0]

            def statistics(src3, tiles, eps, extra=None):
                for t in tiles:
                    ch.add(v.bn_stats(st3[:, t, :], src3[:, t, :]))
                ch.join()
                for t in tiles:
                    ch.add(v.bn_aggr(ag3[:, t, :], st3[:, t, :]))
                ch.join()
                ts = slice(tiles.start, tiles.stop)
                if extra is None:
                    v.tensor_scalar(veps[:, ts], ag3[:, ts, 1], eps, None, ALU.add).then_inc(sig("ln_var"), 1)
                else:
                    second = slice(TT + tiles.start, TT + tiles.stop)
                    ch.link(v.tensor_scalar(veps[:, ts], ag3[:, ts, 1], eps, None, ALU.add))
                    ch.link(v.reciprocal(veps[:, second], veps[:, ts]))
                    ch.link(v.tensor_tensor(veps[:, second], veps[:, second], ag3[:, ts, 1], ALU.mult))
                    v.tensor_scalar(veps[:, second], veps[:, second], extra, None, ALU.add).then_inc(sig("ln_var"), 1)
                norms[0] += 1

            def normalize(src3, tiles, dst3=None):
                if dst3 is None:
                    dst3 = xn3
                    dve.wait_ge(sig("ln_rstd"), norms[0])
                    for t in tiles:
                        v.tensor_scalar(dst3[:, t, :], src3[:, t, :], ag3[:, t, 0:1], rstd[:, t:t + 1],
                                        ALU.subtract, ALU.mult).then_inc(sig("xn_ready"), 1)
                    ready[0] += len(tiles)
                else:
                    dve.wait_ge(sig("ln_rstd"), norms[0])
                    for t in tiles:
                        ch.add(v.tensor_scalar(dst3[:, t, :], src3[:, t, :], ag3[:, t, 0:1], rstd[:, t:t + 1],
                                               ALU.subtract, ALU.mult))
                    ch.join()
                    for t in tiles:
                        v.tensor_scalar(xn3[:, t, :], dst3[:, t, :], rstd[:, TT + t:TT + t + 1], None,
                                        ALU.mult).then_inc(sig("xn_ready"), 1)
                    ready[0] += len(tiles)

            def residual(src, base, c):
                v.tensor_tensor(x_tok[:, c], src, base, ALU.add).then_inc(sig("x_new"), 1)
                xver[0] += 1
                dve.wait_ge(sig("x_new"), xver[0])

            def local(h, stages, pace):
                step = 0
                for c in range(HB * h, HB * (h + 1)):
                    dve.wait_ge(sig("k0_ps"), c + 1)
                    qb = q0T[:, SEQ * c:SEQ * (c + 1)].unsqueeze(2).broadcast_to([P, SEQ, LOCAL])
                    v.scalar_tensor_tensor(prod[c % HB].rearrange("p (q j) -> p q j", j=LOCAL),
                                           bank[c % 2][:, :].rearrange("p (q j) -> p q j", j=LOCAL), wt("bk0"), qb,
                                           ALU.add, ALU.mult).then_inc(sig("prod_ready"), 1)
                    advance(stages, pace(step))
                    step += 1
                dve.wait_ge(sig("s0_ps"), 2 * h + 2)
                sv = bank[2][:, :].rearrange("p (q j) -> p q j", j=LOCAL)
                e = e0.rearrange("p (q j) -> p q j", j=LOCAL)
                wide = lambda a: a.unsqueeze(2).broadcast_to([P, SEQ, LOCAL])
                ch.link(v.tensor_reduce(mx0, sv, AX_X, ALU.max))
                if h:
                    dve.wait_ge(sig("p0_spread"), HB)
                v.tensor_tensor(e, sv, wide(mx0), ALU.subtract).then_inc(sig("e0_arg"), 1)
                dve.wait_ge(sig("e0_exp"), h + 1)
                ch.link(v.tensor_reduce(sm0, e, AX_X, ALU.add))
                ch.link(v.reciprocal(rs0, sm0))
                v.tensor_tensor(e, e, wide(rs0), ALU.mult).then_inc(sig("p0_ready"), 1)
                advance(stages, pace(step))
                step += 1
                for c in range(HB * h, HB * (h + 1)):
                    dve.wait_ge(sig("p0_spread"), c + 1)
                    dve.wait_ge(sig("v0_ready"), c + 1)
                    v.tensor_tensor(vp[c % 2], bank[3 + c % 2][:, :], v0s[c % 2], ALU.mult).then_inc(sig("vp_ready"), 1)
                    dve.wait_ge(sig("vp_ready"), c + 1)
                    v.tensor_reduce(o0T[:, SEQ * c:SEQ * (c + 1)], vp[c % 2].rearrange("p (q j) -> p q j", j=LOCAL),
                                    AX_X, ALU.add).then_inc(sig("o0_ready"), 1)
                    advance(stages, pace(step))
                    step += 1
                if h:
                    for _ in range(len(PROJ) - 2 * GAP):
                        advance(stages, pace(step))
                        step += 1

            def small_stages(h):
                tiles, c = tiles_of(h), cols(h)
                yield
                dve.wait_ge(sig("xo_ps"), 3 * h + 1)
                dve.wait_ge(sig("xb_ready"), (1, 3)[h])
                residual(Z[:, 0:HTOK], xb_tok[:, c], c)
                statistics(x3, tiles, EPS_OUTER)
                yield
                normalize(x3, tiles)
                yield
                dve.wait_ge(sig("late_in"), 16)
                dve.wait_ge(sig("edges_ready"), 6 * h + 6)
                if h == 0:
                    dve.wait_ge(sig("wexp_raw"), 1)
                    ch.link(v.tensor_scalar(wexp, wexp, -1.0, None, ALU.mult))
                ch.link(v.memset(now(dec33), 0.0))
                ch.link(v.tensor_scalar(now(dec33), now(dec33), wexp, None, ALU.add))
                yield
                dve.wait_ge(sig("lnT_ready"), (2, 5)[h])
                ch.link(v.tensor_tensor(bs(dx), now(ln33), prev(ln33), ALU.subtract))
                for dst, mix in ((xk, "mk"), (xv, "mv"), (xr, "mr")):
                    v.scalar_tensor_tensor(bs(dst), bs(dx), wt(mix), prev(ln33), ALU.mult, ALU.add).then_inc(sig("mix_ready"), 1)
                yield
                yield
                dve.wait_ge(sig("k_out"), h + 1)
                ch.link(v.tensor_tensor_scan(o33, dec33, k33, NEG_STATE, ALU.add, ALU.max))
                dve.wait_ge(sig("rkvr_ps"), 3 * h + 3)
                dve.wait_ge(sig("mix_ready"), 3 * h + 3)
                ch.link(v.scalar_tensor_tensor(bs(top), now(k33), wt("u"), prev(o33), ALU.add, ALU.max))
                v.tensor_tensor(bs(ab[:, 0:HTOK]), prev(o33), bs(top), ALU.subtract).then_inc(sig("ab_arg"), 1)
                v.scalar_tensor_tensor(bs(ab[:, HTOK:2 * HTOK]), now(k33), wt("u"), bs(top), ALU.add, ALU.subtract)\
                    .then_inc(sig("ab_arg"), 1)
                v.scalar_tensor_tensor(now(A33), prev(o33), wexp, now(o33), ALU.add, ALU.subtract).then_inc(sig("AB_arg"), 1)
                v.tensor_tensor(now(B33), now(k33), now(o33), ALU.subtract).then_inc(sig("AB_arg"), 1)
                yield
                dve.wait_ge(sig("AB_exp"), 2 * h + 2)
                dve.wait_ge(sig("ab_arg"), 2 * h + 2)
                dve.wait_ge(sig("v_out"), h + 1)
                ch.add(v.tensor_tensor(now(Bv33), now(B33), bs(v_sb), ALU.mult))
                ch.link(v.tensor_tensor_scan(q33, A33, B33, 0.0, ALU.mult, ALU.add))
                dve.wait_ge(sig("ab_exp"), h + 1)
                ch.add(v.tensor_tensor(bs(den), bs(ab[:, 0:HTOK]), prev(q33), ALU.mult))
                ch.link(v.tensor_tensor_scan(p33, A33, Bv33, 0.0, ALU.mult, ALU.add))
                yield
                ch.add(v.tensor_tensor(den, den, ab[:, HTOK:2 * HTOK], ALU.add))
                ch.link(v.tensor_tensor(bs(num), bs(ab[:, 0:HTOK]), prev(p33), ALU.mult))
                dve.wait_ge(sig("er_ready"), h + 1)
                dve.wait_ge(sig("bonus_ready"), h + 1)
                ch.add(v.scalar_tensor_tensor(den, er, 1.0, den, ALU.add, ALU.mult))
                ch.link(v.tensor_tensor(num, num, t_bv, ALU.add))
                ch.link(v.reciprocal(den, den))
                v.tensor_tensor(num, num, den, ALU.mult).then_inc(sig("rw_ready"), 1)
                yield
                yield
                yield
                yield
                dve.wait_ge(sig("xo_ps"), 3 * h + 2)
                residual(Z[:, 0:HTOK], x_tok[:, c], c)
                statistics(x3, tiles, EPS_OUTER)
                yield
                normalize(x3, tiles)
                yield
                yield
                e3 = lambda a: a.rearrange("p (t e) -> p t e", e=E0)
                logit, mag, ex, wl, lw, sp, av, t0, t1, cf = fr
                dve.wait_ge(sig("route_ps"), h + 1)
                eb = wt("eb").unsqueeze(1).broadcast_to([P, HT, E0])
                ch.link(v.tensor_tensor(e3(logit), e3(Z[:, 0:HT * E0]), eb, ALU.add))
                v.scalar_tensor_tensor(mag, logit, -1.0, logit, ALU.mult, ALU.max).then_inc(sig("abs_ready"), 1)
                dve.wait_ge(sig("e_ready"), h + 1)
                v.tensor_scalar(wl, ex, 1.0, None, ALU.add).then_inc(sig("w_ready"), 1)
                dve.wait_ge(sig("w_ready"), h + 1)
                ch.link(v.tensor_scalar(t0, wl, -1.0, 1e-30, ALU.add, ALU.max))
                ch.link(v.reciprocal(t0, t0))
                ch.add(v.scalar_tensor_tensor(t1, wl, 1.0, ex, ALU.is_equal, ALU.mult))
                ch.link(v.tensor_tensor(t0, t0, ex, ALU.mult))
                yield
                dve.wait_ge(sig("ln_ready"), h + 1)
                ch.link(v.tensor_tensor(t0, t0, lw, ALU.mult))
                ch.link(v.tensor_tensor(t0, t0, t1, ALU.add))
                v.scalar_tensor_tensor(sp, logit, 0.0, t0, ALU.max, ALU.add).then_inc(sig("softplus_ready"), 1)
                dve.wait_ge(sig("act_ready"), h + 1)
                pair = [P, HT, E0, E0]
                f4 = [a.rearrange("p (t e j) -> p t e j", t=HT, e=E0) for a in (fc0, fc1)]
                a_j, a_e = e3(av).unsqueeze(2).broadcast_to(pair), e3(av).unsqueeze(3).broadcast_to(pair)
                ch.add(v.tensor_tensor(f4[0], a_j, a_e, ALU.is_gt))
                ch.link(v.tensor_tensor(f4[1], a_j, a_e, ALU.is_equal))
                before = wt("before").unsqueeze(1).broadcast_to([P, HT, E0 * E0])
                f3 = fc1.rearrange("p (t k) -> p t k", t=HT)
                ch.link(v.tensor_tensor(f3, f3, before, ALU.mult))
                ch.link(v.tensor_tensor(fc0, fc0, fc1, ALU.add))
                ch.link(v.tensor_reduce(t1, fc0.rearrange("p (k j) -> p k j", j=E0), AX_X, ALU.add))
                v.scalar_tensor_tensor(cf, t1, 1.5, av, ALU.is_lt, ALU.mult).then_inc(sig("cf_ready"), 1)
                yield
                yield
                yield
                dve.wait_ge(sig("cfT_ps"), h + 1)
                v.tensor_copy(cfT, Z[0:E0, 0:HTOK]).then_inc(sig("cfT_ready"), 1)
                yield
                for n in range(4):
                    dve.wait_ge(sig("spread_ps"), 2 * h + n // 2 + 1)
                    dve.wait_ge(sig("hid_ready"), 5 * h + n + 1)
                    v.tensor_tensor(hid[n], hid[n], (X, Y)[n // 2][:, HTOK * (n % 2):HTOK * (n % 2 + 1)],
                                    ALU.mult).then_inc(sig("hsc_ready"), 1)
                yield
                yield
                dve.wait_ge(sig("xo_ps"), 3 * h + 3)
                dve.wait_ge(sig("xb_ready"), (2, 4)[h])
                residual(Z[:, 0:HTOK], xb_tok[:, c], c)
                statistics(x3, tiles, EPS_OUTER)
                yield
                normalize(x3, tiles)
                yield
                yield
                dve.wait_ge(sig("q1_ps"), h + 1)
                ch.link(v.tensor_scalar(q1T[:, c], Y[:, 0:HTOK], wt("bq1"), -QSCALE, ALU.add, ALU.mult))
                v.tensor_scalar(q1T[:, c], q1T[:, c], 1.0 / MASK_BIG, None, ALU.mult).then_inc(sig("q1_ready"), 1)
                yield

            def take_heads(n):
                dve.wait_ge(sig("o1_ready"), 4 * n + 4)
                o = bank[4][:, :].rearrange("p (b j q) -> p b j q", b=4, j=4)
                t = otmp[:, :].rearrange("p (b j q) -> p b j q", b=4, j=4)
                own_b = wt("own4").unsqueeze(1).unsqueeze(3).broadcast_to([P, 4, 4, SEQ])
                v.tensor_tensor(t, o, own_b, ALU.mult).then_inc(sig("o1_taken"), 1)
                dve.wait_ge(sig("o1_taken"), n + 1)
                ch.link(v.tensor_reduce(oT[:, P * n:P * (n + 1)].rearrange("p (b q) -> p b q", b=4),
                                        t.rearrange("p b j q -> p b q j"), AX_X, ALU.add))

            def full(h, stages, pace):
                dve.wait_ge(sig(f"mask_in{h}"), 64)
                for i in range(UNITS + 2):
                    u = UNITS * h + i
                    if i < UNITS:
                        dve.wait_ge(sig("s1_ready"), u + 1)
                        if u >= NSC:
                            dve.wait_ge(sig("pT_ps"), u - NSC + 1)
                        b = u // GROUPS
                        v.tensor_tensor_reduce(sc[u % NSC], bank[u % NS][:, :], mask[:, KEYS * b:KEYS * (b + 1)], MASK_BIG, 3e38,
                                               ALU.add, ALU.min, smin[:, u:u + 1]).then_inc(sig("s1_min"), 1)
                    j = u - 2
                    if i >= 2 and j % 2 == 1:
                        dve.wait_ge(sig("pT_ps"), j + 1)
                        if j >= NPT:
                            dve.wait_ge(sig("o1_ready"), (j - NPT) // GROUPS + 1)
                        v.tensor_copy(pt[j % NPT], bank[2 + j % NT][:, :]).then_inc(sig("pT_odd"), 1)
                    if i == TAKE:
                        take_heads(2 * h)
                    advance(stages, pace(i))

            def linear_stages(h):
                tiles, c = tiles_of(h), cols(h)
                dve.wait_ge(sig("p1_ready"), UNITS * (h + 1))
                if h:
                    dve.wait_ge(sig("ffo_ps"), 1)
                rs = slice(UNITS * h, UNITS * (h + 1))
                ch.link(v.reciprocal(rinv[:, rs], rsum[:, rs]))
                mg4 = mg.rearrange("p (g b q) -> p g b q", g=4, b=HB)
                ri = rinv[:, rs].rearrange("p (b g) -> p g b", g=GROUPS)
                rows = wt("rows32").unsqueeze(1).broadcast_to([P, HB, SEQ])
                for g in range(GROUPS):
                    v.tensor_tensor(mg4[:, g, :, :], rows, ri[:, g, :].unsqueeze(2).broadcast_to([P, HB, SEQ]),
                                    ALU.mult).then_inc(sig("mg_ready"), 1)
                take_heads(2 * h + 1)
                yield
                yield
                dve.wait_ge(sig("rinv_ps"), h + 1)
                ch.link(v.tensor_tensor(oT[:, c], oT[:, c], X[:, 0:HTOK], ALU.mult))
                v.tensor_scalar(oT[:, c], oT[:, c], wt("bv1"), None, ALU.add).then_inc(sig("o1T_ready"), 1)
                yield
                dve.wait_ge(sig("xo_ps"), 7 + h)
                dve.wait_ge(sig("xb_ready"), 5)
                residual(Y[:, 0:HTOK], xb_tok[:, c], c)
                statistics(x3, tiles, EPS_OUTER, EPS_INNER)
                yield
                normalize(x3, tiles, xb3)
                yield
                yield
                dve.wait_ge(sig("qk_ps"), h + 1)
                ch.add(v.tensor_scalar(qp, X[:, 0:HTOK], 0.0, STAB, ALU.max, ALU.add))
                v.tensor_scalar(kp_tok, X[:, HTOK:2 * HTOK], 0.0, STAB, ALU.max, ALU.add).then_inc(sig("kp_ready"), 1)
                ch.join()
                dve.wait_ge(sig("vtok_ps"), h + 1)
                for t in range(HT):
                    v.tensor_tensor(vb[:, 512 * t:512 * (t + 1)].rearrange("p (b d) -> p b d", b=4),
                                    Y[:, P * t:P * (t + 1)].unsqueeze(1).broadcast_to([P, 4, P]),
                                    wt("batchof").unsqueeze(2).broadcast_to([P, 4, P]), ALU.mult).then_inc(sig("vb_ready"), 1)
                yield
                dve.wait_ge(sig("ksum_ps"), h + 1)
                ch.link(v.tensor_copy(ksum, Y[:, 0:HB]))
                v.tensor_tensor(bs(qk), bs(qp), ksum.unsqueeze(2).broadcast_to([P, HB, SEQ]), ALU.mult).then_inc(sig("qksum_ready"), 1)
                yield
                same4 = wt("samehead").unsqueeze(1).broadcast_to([P, 4, D])
                for t in range(HT):
                    dve.wait_ge(sig("kvs_ps"), HT * h + t + 1)
                    v.tensor_tensor(kvs[:, 512 * t:512 * (t + 1)].rearrange("p (b d) -> p b d", b=4),
                                    (X, Z)[t][:, :].rearrange("p (b d) -> p b d", b=4), same4, ALU.mult).then_inc(sig("kvs_ready"), 1)
                yield
                dve.wait_ge(sig("den_ps"), h + 1)
                ch.link(v.reciprocal(rden, Y[:, 0:HTOK]))
                dve.wait_ge(sig("num_ps"), h + 1)
                v.tensor_tensor(att, rden, X[:, 0:HTOK], ALU.mult).then_inc(sig("att_ready"), 1)
                yield
                dve.wait_ge(sig("ao_ps"), h + 1)
                v.tensor_tensor(add1, Z[:, 0:HTOK], xb_tok[:, c], ALU.add).then_inc(sig("add1_ready"), 1)
                dve.wait_ge(sig("add1_ready"), h + 1)
                a3 = add1.rearrange("p (t d) -> p t d", d=D)
                a3 = {t: a3[:, t - tiles.start, :] for t in tiles}
                view = Shifted(a3)
                statistics(view, tiles, EPS_INNER)
                yield
                normalize(view, tiles)
                yield
                yield
                yield
                dve.wait_ge(sig("ffo_ps"), h + 1)
                v.tensor_tensor(g2.rearrange("p (t d) -> p t d", d=D), X[:, 0:HTOK].rearrange("p (t d) -> p t d", d=D),
                                over_tiles(wt("b2"))[:, 0:HT, :], ALU.add).then_inc(sig("ffo_ready"), 1)
                dve.wait_ge(sig("g2_ready"), h + 1)
                dve.wait_ge(sig("res_ready"), h + 1)
                residual(g2, res4, c)
                yield

            dve.wait_ge(sig("x_in"), 16)
            statistics(x3, range(TT), EPS_OUTER)
            normalize(x3, range(TT))
            dve.wait_ge(sig("early_in"), 16)
            dve.wait_ge(sig("q0_ps"), 1)
            ch.link(v.tensor_scalar(q0T, Y[:, :], wt("bq0"), QSCALE, ALU.add, ALU.mult))
            local(0, iter(()), pace_local)
            stages = small_stages(0)
            local(1, stages, pace_local)
            finish(stages)
            stages = small_stages(1)
            full(0, stages, pace_full)
            finish(stages)
            stages = linear_stages(0)
            full(1, stages, pace_last)
            finish(stages)
            finish(linear_stages(1))

            statistics(x3, range(TT), EPS_OUTER)
            normalize(x3, range(TT))
            ge = lambda a: a.rearrange("p (t e) -> p t e", e=E1)
            wide = lambda a: a.unsqueeze(2).broadcast_to([P, TT, E1])
            flat = lambda name: wt(name).unsqueeze(1).broadcast_to([P, TT, E1])
            dve.wait_ge(sig("gate_ps"), 1)
            ch.link(v.tensor_tensor(ge(mr[0]), ge(bank[7][:, 0:64]), flat("bg"), ALU.add))
            ch.link(v.tensor_reduce(m4[0], ge(mr[0]), AX_X, ALU.max))
            v.tensor_tensor(ge(mr[1]), ge(mr[0]), wide(m4[0]), ALU.subtract).then_inc(sig("gate_arg"), 1)
            dve.wait_ge(sig("gate_exp"), 1)
            ch.link(v.tensor_reduce(m4[1], ge(mr[2]), AX_X, ALU.add))
            ch.link(v.reciprocal(m4[2], m4[1]))
            ch.link(v.tensor_tensor(ge(mr[3]), ge(mr[2]), wide(m4[2]), ALU.mult))
            ch.link(v.tensor_reduce(m4[3], ge(mr[3]), AX_X, ALU.max))
            ch.link(v.tensor_tensor(ge(mr[4]), ge(mr[3]), wide(m4[3]), ALU.not_equal))
            ch.link(v.scalar_tensor_tensor(ge(mr[4]), ge(mr[4]), float(E1), flat("iota_e"), ALU.mult, ALU.add))
            ch.link(v.tensor_reduce(m4[4], ge(mr[4]), AX_X, ALU.min))
            v.tensor_tensor(ge(mr[5]), flat("iota_e"), wide(m4[4]), ALU.is_equal).then_inc(sig("onehot_ready"), 1)
            dve.wait_ge(sig("onehot_ready"), 1)
            dve.wait_ge(sig("count_ps"), 1)
            ch.link(v.scalar_tensor_tensor(ge(mr[6]), ge(bank[7][:, 64:128]), -1.0, ge(mr[5]), ALU.add, ALU.mult))
            ch.link(v.tensor_reduce(m4[5], ge(mr[6]), AX_X, ALU.add))
            ch.add(v.tensor_scalar(m4[6], m4[5], CAP - 0.5, float(4 * SLOTS), ALU.is_gt, ALU.mult))
            ch.link(v.scalar_tensor_tensor(m4[7], m4[4], float(CAP), m4[5], ALU.mult, ALU.add))
            ch.link(v.tensor_tensor(m4[7], m4[7], m4[6], ALU.add))
            for t in range(TT):
                v.tensor_scalar(disp[:, 512 * t:512 * (t + 1)], wt("iota_slot"), m4[7][:, t:t + 1], None,
                                ALU.is_equal).then_inc(sig("disp_ready"), 1)
            v.tensor_copy(tok3(slotbc), m4[7].unsqueeze(2).broadcast_to([P, TT, P])).then_inc(sig("slotbc_ready"), 1)
            dve.wait_ge(sig("buf_ps"), 1)
            v.tensor_copy(bufT, bank[4][:, :]).then_inc(sig("buf_ready"), 1)
            dve.wait_ge(sig("moeb_in"), 16)
            for g in range(4):
                dve.wait_ge(sig("hm_ps"), g + 1)
                v.tensor_tensor(hmoe[:, 512 * g:512 * (g + 1)], bank[g][:, :], b1e[:, 512 * g:512 * (g + 1)],
                                ALU.add).then_inc(sig("hm_ready"), 1)
            dve.wait_ge(sig("slotT_ps"), 1)
            for g in range(4):
                v.tensor_scalar(comb[:, 512 * g:512 * (g + 1)], bank[5][:, :], wt("slot_row")[:, g:g + 1], None,
                                ALU.is_equal).then_inc(sig("comb_ready"), 1)
            dve.wait_ge(sig("y_ps"), 4)
            v.tensor_tensor(ymoe, bank[6][:, :], b2e, ALU.add).then_inc(sig("y_ready"), 1)
            for t in range(TT):
                dve.wait_ge(sig("comb_ps"), t + 1)
                v.scalar_tensor_tensor(tok3(outt)[:, t, :], bank[t][:, 0:P], m4[3][:, t:t + 1], x3[:, t, :],
                                       ALU.mult, ALU.add).then_inc(sig("out_ready"), 1)

        @block.tensor
        def _(pe):
            mm = nc.tensor.matmul
            ready, turned = [0], [0]

            def turn_norm(dst, tiles, *waits):
                for name, n in waits:
                    pe.wait_ge(sig(name), n)
                for i, t in enumerate(tiles):
                    ready[0] += 1
                    pe.wait_ge(sig("xn_ready"), ready[0])
                    last = nc.tensor.transpose(dst[:, P * i:P * (i + 1)], xn3[:, t, :], wt("ident"))
                last.then_inc(sig("lnT_ps"), 1)
                turned[0] += 1

            def wait_norm():
                pe.wait_ge(sig("lnT_ready"), turned[0])

            def project_tokens(dst, srcT, w, tiles=HT):
                for t in range(tiles):
                    last = mm(dst[:, P * t:P * (t + 1)], srcT[:, P * t:P * (t + 1)], w, start=True, stop=True)
                return last

            nproj = [0]

            def projection():
                i = nproj[0]
                nproj[0] += 1
                kind, b = PROJ[i]
                if i == 0:
                    pe.wait_ge(sig("late_in"), 16)
                if i >= 2:
                    pe.wait_ge(sig("proj_out"), i - 1)
                dst = bank[3 + i % 2]
                if kind == "k":
                    last = mm(dst[:, :], wt("wk1"), ctx[:, KEYS * b:KEYS * (b + 1)], start=True, stop=True)
                else:
                    for k in range(KT):
                        at = KEYS * b + P * k
                        last = mm(dst[:, P * k:P * (k + 1)], ctx[:, at:at + P], wt("wv1"), start=True, stop=True)
                last.then_inc(sig("proj_done"), 1)

            def local(h, stages, pace):
                step = 0

                def headsum(n):
                    for c in range(4 * n, 4 * n + 4):
                        pe.wait_ge(sig("prod_ready"), c + 1)
                        r = 32 * (c % 4)
                        last = mm(bank[2][r:r + 32, :], wt("headsum")[:, 32 * (n % 2):32 * (n % 2) + 32], prod[c % HB],
                                  start=(n % 2 == 0), stop=(n % 2 == 1), skip_group_check=True)
                    last.then_inc(sig("s0_ps"), 1)

                def values(c):
                    if c % HB < 2:
                        pe.wait_ge(sig("prod_ready"), HB * (h + 1))
                    else:
                        pe.wait_ge(sig("v0_ready"), c - 1)
                    mm(bank[c % 2][:, :], wt("wv0"), ctx[:, KEYS * c:KEYS * (c + 1)], start=True, stop=True).then_inc(sig("v0_ps"), 1)

                def spread(c):
                    if c % HB < 2:
                        pe.wait_ge(sig("p0_ready"), h + 1)
                        pe.wait_ge(sig("proj_out"), GAP * (h + 1))
                    else:
                        pe.wait_ge(sig("vp_ready"), c - 1)
                    if c == 0:
                        pe.wait_ge(sig("hspread_ready"), 4)
                    k = (c // 4) % 2
                    mm(bank[3 + c % 2][:, :], hspread[c % 4][:, P * k:P * (k + 1)], e0,
                       start=True, stop=True).then_inc(sig("p0_spread"), 1)

                for c in range(HB * h, HB * (h + 1)):
                    pe.wait_ge(sig(f"ctx_in{c // 4}"), 16)
                    if c % HB >= 2:
                        pe.wait_ge(sig("prod_ready"), c - 1)
                    elif h:
                        pe.wait_ge(sig("v0_ready"), HB)
                    mm(bank[c % 2][:, :], wt("wk0"), ctx[:, KEYS * c:KEYS * (c + 1)], start=True, stop=True).then_inc(sig("k0_ps"), 1)
                    if c % HB == 5:
                        headsum(2 * h)
                    advance(stages, pace(step))
                    step += 1
                headsum(2 * h + 1)
                values(HB * h)
                values(HB * h + 1)
                if h:
                    pe.wait_ge(sig("vp_ready"), HB)
                for _ in range(GAP):
                    projection()
                advance(stages, pace(step))
                step += 1
                for c in range(HB * h, HB * (h + 1)):
                    spread(c)
                    if c + 2 < HB * (h + 1):
                        values(c + 2)
                    advance(stages, pace(step))
                    step += 1
                if h:
                    pe.wait_ge(sig("vp_ready"), BATCH)
                    while nproj[0] < len(PROJ):
                        projection()
                        advance(stages, pace(step))
                        step += 1

            def small_stages(h):
                tiles, c = tiles_of(h), cols(h)
                pe.wait_ge(sig("o0_ready"), HB * (h + 1))
                project_tokens(Z, o0T[:, c], wt("wo0")).then_inc(sig("xo_ps"), 1)
                yield
                yield
                yield
                turn_norm(X, tiles)
                yield
                yield
                for n, src in enumerate((xk, xv, xr)):
                    pe.wait_ge(sig("mix_ready"), 3 * h + n + 1)
                    if n == 0:
                        wait_norm()
                    dst = (X[:, 0:HTOK], X[:, HTOK:], Y[:, 0:HTOK])[n]
                    mm(dst, wt(("rk", "rv", "rr")[n]), src, start=True, stop=True).then_inc(sig("rkvr_ps"), 1)
                yield
                yield
                yield
                yield
                yield
                yield
                pe.wait_ge(sig("rw_ready"), h + 1)
                project_tokens(Z, num, wt("ro")).then_inc(sig("xo_ps"), 1)
                yield
                yield
                yield
                turn_norm(X, tiles, ("v_out", h + 1))
                yield
                wait_norm()
                for t in range(HT):
                    last = mm(Z[:, E0 * t:E0 * (t + 1)], lnT[:, c][:, P * t:P * (t + 1)], wt("route"), start=True, stop=True)
                last.then_inc(sig("route_ps"), 1)
                for n in range(4):
                    last = mm((X, Y)[n // 2][:, HTOK * (n % 2):HTOK * (n % 2 + 1)], wt("rw1")[:, P * n:P * (n + 1)], lnT[:, c],
                              start=True, stop=True)
                    if n % 2:
                        last.then_inc(sig("hid_ps"), 1)
                yield
                pe.wait_ge(sig("abs_ready"), h + 1)
                mm(Z[0:H0, 0:HTOK], wt("sw1"), lnT[:, c], start=True, stop=True).then_inc(sig("hid_ps"), 1)
                yield
                yield
                yield
                pe.wait_ge(sig("cf_ready"), h + 1)
                pe.wait_ge(sig("hid_ready"), 5 * h + 5)
                cf3 = fr[9].rearrange("p (t e) -> p t e", e=E0)
                for t in range(HT):
                    last = nc.tensor.transpose(Z[0:E0, P * t:P * (t + 1)], cf3[:, t, :], wt("ident"))
                last.then_inc(sig("cfT_ps"), 1)
                yield
                pe.wait_ge(sig("cfT_ready"), h + 1)
                for n in range(4):
                    last = mm((X, Y)[n // 2][:, HTOK * (n % 2):HTOK * (n % 2 + 1)], wt("spread", E0)[:, P * n:P * (n + 1)], cfT,
                              start=True, stop=True)
                    if n % 2:
                        last.then_inc(sig("spread_ps"), 1)
                yield
                pe.wait_ge(sig("hsc_ready"), 4 * h + 4)
                for t in range(HT):
                    k = slice(P * t, P * (t + 1))
                    mm(Z[:, k], cfT[:, k], wt("rb2", E0), start=True, stop=False)
                    mm(Z[:, k], hid[4][0:H0, k], wt("sw2", H0), start=False, stop=False)
                    for n in range(4):
                        last = mm(Z[:, k], hid[n][:, k], wt("rw2")[:, P * n:P * (n + 1)], start=False, stop=(n == 3))
                last.then_inc(sig("xo_ps"), 1)
                yield
                yield
                yield
                turn_norm(X, tiles)
                yield
                wait_norm()
                mm(Y[:, 0:HTOK], wt("wq1"), lnT[:, c], start=True, stop=True).then_inc(sig("q1_ps"), 1)
                yield

            def scores(u):
                b, g = divmod(u, GROUPS)
                if u < NS:
                    pe.wait_ge(sig("vp_ready"), BATCH)
                else:
                    pe.wait_ge(sig("s1_min"), u - NS + 1)
                if g == 0:
                    pe.wait_ge(sig("qbd_ready"), b + 1)
                mm(bank[u % NS][:, :], qbd[b % NQ][:, P * g:P * (g + 1)], k1[:, KEYS * b:KEYS * (b + 1)],
                   start=True, stop=True).then_inc(sig("s1_ready"), 1)

            def turn(u):
                pe.wait_ge(sig("p1_ready"), u + 1)
                if u >= NT:
                    j = u - NT
                    pe.wait_ge(sig("pT_odd" if j % 2 else "pT_even"), j // 2 + 1)
                for k in range(KT):
                    last = nc.tensor.transpose(bank[2 + u % NT][:, P * k:P * (k + 1)], sc[u % NSC][:, P * k:P * (k + 1)], wt("ident"))
                last.then_inc(sig("pT_ps"), 1)

            def outputs(b):
                pe.wait_ge(sig("pT_even"), 2 * b + 2)
                pe.wait_ge(sig("pT_odd"), 2 * b + 2)
                if b % 4 == 0 and b >= 4:
                    pe.wait_ge(sig("o1_taken"), b // 4)
                for k in range(KT):
                    for g in range(GROUPS):
                        r = slice(32 * g, 32 * g + 32)
                        last = mm(bank[4][r, P * (b % 4):P * (b % 4 + 1)], vkey[:, b, k, r],
                                  pt[(GROUPS * b + g) % NPT][:, P * k:P * (k + 1)], start=(k == 0), stop=(k == KT - 1),
                                  skip_group_check=True)
                last.then_inc(sig("o1_ready"), 1)

            def full(h, stages, pace):
                for i in range(UNITS + 2):
                    u = UNITS * h + i
                    if i < UNITS:
                        scores(u)
                    if i >= 2:
                        turn(u - 2)
                    if i >= OUT and (i - OUT) % GROUPS == 0:
                        outputs((u - OUT) // GROUPS)
                    if i == UNITS + 1:
                        outputs(HB * (h + 1) - 1)
                    advance(stages, pace(i))

            def linear_stages(h):
                tiles, c = tiles_of(h), cols(h)
                yield
                for g in range(GROUPS):
                    pe.wait_ge(sig("mg_ready"), GROUPS * h + g + 1)
                    last = mm(X[32 * g:32 * g + 32, 0:HTOK], wt("heads32"), mg[:, HTOK * g:HTOK * (g + 1)], start=True, stop=True,
                              skip_group_check=True)
                last.then_inc(sig("rinv_ps"), 1)
                yield
                yield
                keep_warm(2)
                pe.wait_ge(sig("o1T_ready"), h + 1)
                project_tokens(Y, oT[:, c], wt("wo1")).then_inc(sig("xo_ps"), 1)
                keep_warm(8)
                yield
                yield
                turn_norm(X, tiles)
                yield
                wait_norm()
                mm(X[:, 0:HTOK], wt("lq"), lnT[:, c], start=True, stop=True)
                project_tokens(X[:, HTOK:], lnT[:, c], wt("lk")).then_inc(sig("qk_ps"), 1)
                project_tokens(Y, lnT[:, c], wt("lv")).then_inc(sig("vtok_ps"), 1)
                keep_warm(3)
                yield
                pe.wait_ge(sig("kp_ready"), h + 1)
                pe.wait_ge(sig("vb_ready"), HT * (h + 1))
                for t in range(HT):
                    last = mm(Y[:, 4 * t:4 * t + 4], kp_tok[:, P * t:P * (t + 1)], wt("batchof"), start=True, stop=True)
                last.then_inc(sig("ksum_ps"), 1)
                for t in range(HT):
                    mm((X, Z)[t][:, :], kp_tok[:, P * t:P * (t + 1)], vb[:, 512 * t:512 * (t + 1)],
                       start=True, stop=True).then_inc(sig("kvs_ps"), 1)
                yield
                yield
                pe.wait_ge(sig("qksum_ready"), h + 1)
                mm(Y[:, 0:HTOK], wt("samehead"), qk, start=True, stop=True).then_inc(sig("den_ps"), 1)
                pe.wait_ge(sig("kvs_ready"), HT * (h + 1))
                for b in range(HB):
                    last = mm(X[:, SEQ * b:SEQ * (b + 1)], kvs[:, P * b:P * (b + 1)], qp[:, SEQ * b:SEQ * (b + 1)],
                              start=True, stop=True)
                last.then_inc(sig("num_ps"), 1)
                yield
                pe.wait_ge(sig("att_ready"), h + 1)
                project_tokens(Z, att, wt("lo")).then_inc(sig("ao_ps"), 1)
                keep_warm(5)
                yield
                yield
                turn_norm(X, tiles)
                yield
                wait_norm()
                for n in range(4):
                    last = mm((Y, Z)[n // 2][:, HTOK * (n % 2):HTOK * (n % 2 + 1)], wt("w1")[:, P * n:P * (n + 1)], lnT[:, c],
                              start=True, stop=True)
                    if n % 2:
                        last.then_inc(sig("ffh_ps"), 1)
                yield
                keep_warm(2)
                pe.wait_ge(sig("ffh_ready"), 4 * h + 4)
                for t in range(HT):
                    for n in range(4):
                        last = mm(X[:, P * t:P * (t + 1)], hT[:, HTOK * n + P * t:HTOK * n + P * (t + 1)],
                                  wt("w2")[:, P * n:P * (n + 1)], start=(n == 0), stop=(n == 3))
                last.then_inc(sig("ffo_ps"), 1)
                yield

            def keep_warm(n):
                for _ in range(n if tail[0] else 0):
                    mm(bank[3][:, 0:256], wt("ident"), late[:, 0:256], start=True, stop=True)

            tail = [False]

            pe.wait_ge(sig("early_in"), 16)
            turn_norm(X, range(TT))
            wait_norm()
            mm(Y[:, :], wt("wq0"), lnT[:, :], start=True, stop=True).then_inc(sig("q0_ps"), 1)
            local(0, iter(()), pace_local)
            stages = small_stages(0)
            local(1, stages, pace_local)
            finish(stages)
            stages = small_stages(1)
            full(0, stages, pace_full)
            finish(stages)
            stages = linear_stages(0)
            full(1, stages, pace_last)
            finish(stages)
            tail[0] = True
            finish(linear_stages(1))

            keep_warm(8)
            turn_norm(X, range(TT))
            wait_norm()
            for t in range(TT):
                last = mm(bank[7][:, E1 * t:E1 * (t + 1)], lnT[:, P * t:P * (t + 1)], wt("wg"), start=True, stop=True)
            last.then_inc(sig("gate_ps"), 1)
            keep_warm(7)
            pe.wait_ge(sig("onehot_ready"), 1)
            mm(bank[7][:, 64:128], wt("upto"), mr[5], start=True, stop=False)
            for t in range(1, TT):
                last = mm(bank[7][:, 64 + E1 * t:128], wt("ones"), mr[5][:, 0:E1 * (TT - t)], start=False, stop=(t == TT - 1))
            last.then_inc(sig("count_ps"), 1)
            keep_warm(2)
            for t in range(TT):
                pe.wait_ge(sig("disp_ready"), t + 1)
                last = mm(bank[4][:, :], xn3[:, t, :], disp[:, 512 * t:512 * (t + 1)], start=(t == 0), stop=(t == TT - 1))
            last.then_inc(sig("buf_ps"), 1)
            pe.wait_ge(sig("slotbc_ready"), 1)
            for t in range(TT):
                last = nc.tensor.transpose(bank[5][:, P * t:P * (t + 1)], tok3(slotbc)[:, t, :], wt("ident"))
            last.then_inc(sig("slotT_ps"), 1)
            pe.wait_ge(sig("w1_in"), 16)
            pe.wait_ge(sig("buf_ready"), 1)
            for g in range(4):
                for j in range(4):
                    e = 4 * g + j
                    last = mm(bank[g][32 * j:32 * j + 32, :], bufT[:, CAP * e:CAP * (e + 1)], w1e[:, e, :], start=True, stop=True,
                              skip_group_check=True)
                last.then_inc(sig("hm_ps"), 1)
            for g in range(4):
                pe.wait_ge(sig("hm_ready"), g + 1)
                for k in range(4):
                    last = nc.tensor.transpose(bank[g][:, P * k:P * (k + 1)], hmoe[:, 512 * g + P * k:512 * g + P * (k + 1)], wt("ident"))
                last.then_inc(sig("hmT_ps"), 1)
            pe.wait_ge(sig("w2_in"), 16)
            for g in range(4):
                pe.wait_ge(sig("hmT_ready"), g + 1)
                for k in range(4):
                    for j in range(4):
                        at = 512 * g + P * k + CAP * j
                        last = mm(bank[6][32 * j:32 * j + 32, P * g:P * (g + 1)], hmoeT[:, at:at + CAP], w2e[:, 4 * g + j, k, :],
                                  start=(k == 0), stop=(k == 3), skip_group_check=True)
                last.then_inc(sig("y_ps"), 1)
            pe.wait_ge(sig("y_ready"), 1)
            pe.wait_ge(sig("comb_ready"), 4)
            for t in range(TT):
                for g in range(4):
                    last = mm(bank[t][:, 0:P], comb[:, 512 * g + P * t:512 * g + P * (t + 1)], ymoe[:, P * g:P * (g + 1)],
                              start=(g == 0), stop=(g == 3))
                last.then_inc(sig("comb_ps"), 1)


def constants():
    p, one = np.arange(P), np.float32
    r = p[:, None]
    f = np.arange(P)[None, :]
    out = {
        "ident": r == f,
        "headsum": np.concatenate([(np.arange(32) // 16 == h) & (np.arange(32) % 16 == r // HD) for h in range(2)], 1),
        "headspread": np.concatenate([(r % 32 // 16 == h) & (r % 16 == f // HD) for h in range(2)], 1),
        "spread": np.concatenate([r == 2 * n + f // H0 for n in range(4)], 1),
        "before": np.broadcast_to(np.tril(np.ones((E0, E0)), -1).reshape(1, -1), (P, E0 * E0)),
        "rowblock": r // 32 == np.arange(4)[None, :],
        "own16": r // HD == np.arange(HEADS)[None, :],
        "own4": r // HD % 4 == np.arange(4)[None, :],
        "rows32": r % 32 == np.arange(32)[None, :],
        "heads32": r // 32 == np.arange(32)[None, :] // HD,
        "samehead": r // HD == f // HD,
        "batchof": r // SEQ == np.arange(4)[None, :],
        "iota_e": np.broadcast_to(np.arange(E1)[None, :], (P, E1)),
        "iota_slot": np.broadcast_to(np.arange(SLOTS)[None, :], (P, SLOTS)),
        "slot_row": P * np.arange(4)[None, :] + r,
        "upto": r <= f,
        "ones": np.ones((P, P)),
    }
    return {k: np.ascontiguousarray(v).astype(one) for k, v in out.items()}


def kernel(**inputs):
    import concourse.bacc as bacc
    from concourse.bass_utils import run_bass_kernel_spmd

    a = {k: np.asarray(v) for k, v in inputs.items()}

    def col(name):
        return a[name].reshape(-1, 1)

    def rows(name):
        return np.broadcast_to(a[name].reshape(1, -1), (P, a[name].size))

    def tiles(m):
        return m.reshape(-1, P, m.shape[-1]).transpose(1, 0, 2).reshape(P, -1)

    parts = dict(constants())
    parts.update(
        wq0=a["L0_xattn_Wq"].T, wk0=a["L0_xattn_Wk"].T, wv0=a["L0_xattn_Wv"].T, wo0=a["L0_xattn_Wo"].T,
        bq0=col("L0_xattn_bq"), bk0=col("L0_xattn_bk"), bv0=col("L0_xattn_bv"), bo0=rows("L0_xattn_bo"),
        rk=a["L0_attn_Wk"].T, rv=a["L0_attn_Wv"].T, rr=a["L0_attn_Wr"].T, ro=a["L0_attn_Wo"].T,
        w=col("L0_attn_w"), u=col("L0_attn_u"), mk=col("L0_attn_mix_k"), mv=col("L0_attn_mix_v"), mr=col("L0_attn_mix_r"),
        route=a["L0_ffn_routing_W"].T, eb=rows("L0_ffn_expert_bias"), sw1=a["L0_ffn_sW1"], sb1=col("L0_ffn_sb1"),
        rw1=a["L0_ffn_rW1"].transpose(1, 0, 2).reshape(P, -1), rb1=a["L0_ffn_rb1"].reshape(4, P).T,
        rw2=tiles(a["L0_ffn_rW2"].reshape(E0 * H0, D)), sw2=a["L0_ffn_sW2"], rb2=a["L0_ffn_rb2"], sb2=rows("L0_ffn_sb2"),
        wq1=a["L1_xattn_Wq"], wk1=a["L1_xattn_Wk"], wv1=a["L1_xattn_Wv"], wo1=a["L1_xattn_Wo"],
        bq1=col("L1_xattn_bq"), bk1=col("L1_xattn_bk"), bv1=col("L1_xattn_bv"), bo1=rows("L1_xattn_bo"),
        gamma=col("L1_attn_gamma1"), beta=col("L1_attn_beta1"), lq=a["L1_attn_wq"].reshape(D, D), lk=a["L1_attn_wk"].reshape(D, D),
        lv=a["L1_attn_wv"].reshape(D, D), lo=a["L1_attn_wo"].reshape(D, D), w1=a["L1_attn_w1"],
        b1=a["L1_attn_b1"].reshape(4, P).T, w2=tiles(a["L1_attn_w2"]), b2=rows("L1_attn_b2"),
        wg=a["L1_ffn_Wg"], bg=rows("L1_ffn_bg"),
    )

    def pack(layout):
        out = np.zeros((P, width(layout)), np.float32)
        for name, (lo, hi) in columns(layout).items():
            out[:parts[name].shape[0], lo:hi] = parts[name]
        return out

    def slots(b):
        n = b.shape[1]
        return np.broadcast_to(b.reshape(4, 4, 1, n).transpose(1, 2, 0, 3), (4, CAP, 4, n)).reshape(P, 4 * n)

    arrays = {
        "x": a["x"].reshape(TOK, D),
        "early": pack(EARLY),
        "late": pack(LATE),
        "ctx": a["ctx_1024"].reshape(CTX, D).T,
        "mask": a["mask_Bx1xSxS2_fk0"].transpose(2, 0, 1, 3).reshape(SEQ, CTX),
        "moe_w1": a["L1_ffn_W1"].transpose(1, 0, 2).reshape(D, E1 * H1),
        "moe_w2": a["L1_ffn_W2"].reshape(E1, 4, P, D).transpose(2, 0, 1, 3).reshape(P, E1 * H1),
        "moe_b": np.concatenate([slots(a["L1_ffn_b1"]), slots(a["L1_ffn_b2"])], axis=1),
    }
    arrays = {k: np.ascontiguousarray(v) for k, v in arrays.items()}
    nc = bacc.Bacc("TRN2", target_bir_lowering=False, num_devices=1)
    args = [nc.dram_tensor(k, v.shape, F32, kind="ExternalInput").ap() for k, v in arrays.items()]
    args.append(nc.dram_tensor("out", (TOK, D), F32, kind="ExternalOutput").ap())
    program(nc, *args)
    done = run_bass_kernel_spmd(nc, [arrays], core_ids=[0])
    return done.results[0]["out"].reshape(BATCH, SEQ, D)
```

```python
from contextlib import ExitStack

import numpy as np
import concourse.bass as bass
from concourse import mybir

F32 = mybir.dt.float32
ALU = mybir.AluOpType
ACT = mybir.ActivationFunctionType
AX_X = mybir.AxisListType.X

P = 128
BATCH, SEQ, D = 16, 32, 128
TOK = BATCH * SEQ
TT = TOK // P
KEYS = 512
CTX = BATCH * KEYS
HEADS, HD = 16, 8
GROUPS = 4
LOCAL = KEYS // SEQ
KT = KEYS // P
HB, HT, HTOK = BATCH // 2, TT // 2, TOK // 2
UNITS = HB * GROUPS
E0, H0 = 8, 64
E1, H1 = 16, 512
CAP = TOK // E1
SLOTS = E1 * CAP
FF = 512
QSCALE = float(1.0 / np.sqrt(np.float32(HD)))
MASK_BIG = 1e15
NEG_STATE = -1e30
STAB = 0.001
EPS_OUTER, EPS_INNER = 1e-5, 1e-6

EARLY = [("ident", 128), ("bq0", 1), ("bk0", 1), ("bv0", 1), ("wq0", 128), ("wk0", 128), ("wv0", 128),
         ("wk1", 128), ("bk1", 1), ("wo0", 128), ("headsum", 64), ("headspread", 256), ("rowblock", 4), ("bo0", 128)]
LATE = [("rk", 128), ("rv", 128), ("rr", 128), ("ro", 128), ("w", 1), ("u", 1), ("mk", 1), ("mv", 1), ("mr", 1),
        ("route", E0), ("eb", E0), ("sw1", H0), ("sb1", 1), ("rw1", 512), ("rb1", 4), ("rw2", 512), ("sw2", 128),
        ("rb2", 128), ("sb2", 128), ("spread", 512), ("before", E0 * E0),
        ("wq1", 128), ("wv1", 128), ("wo1", 128), ("bq1", 1), ("bv1", 1), ("bo1", 128),
        ("own4", 4), ("own16", HEADS), ("rows32", 32), ("heads32", 32),
        ("gamma", 1), ("beta", 1), ("lq", 128), ("lk", 128), ("lv", 128), ("lo", 128), ("w1", FF), ("b1", 4),
        ("w2", FF), ("b2", 128), ("samehead", 128), ("batchof", 4),
        ("wg", E1), ("bg", E1), ("iota_e", E1), ("iota_slot", SLOTS), ("slot_row", 4), ("upto", 128), ("ones", 128)]


def width(pack):
    return sum(n for _, n in pack)


def columns(pack):
    at, out = 0, {}
    for name, n in pack:
        out[name] = (at, at + n)
        at += n
    return out


LAG = 2
OUT = LAG + 5
TAKE = 3 * GROUPS + OUT + 2


class Shifted:

    def __init__(self, tiles):
        self.tiles = tiles

    def __getitem__(self, at):
        return self.tiles[at[1]]


class Chain:

    def __init__(self, eng, sem):
        self.eng, self.sem, self.n = eng, sem, 0

    def add(self, ins):
        self.n += 1
        ins.then_inc(self.sem, 1)

    def join(self):
        self.eng.wait_ge(self.sem, self.n)

    def link(self, ins):
        self.add(ins)
        self.join()


def program(nc, x_d, early_d, late_d, ctx_d, mask_d, w1_d, w2_d, moeb_d, out_d):
    with ExitStack() as stack:
        def sb(name, cols, rows=P):
            return stack.enter_context(nc.sbuf_tensor(name + "_sb", [rows, cols], F32))

        sems = {}

        def sig(name):
            if name not in sems:
                sems[name] = stack.enter_context(nc.semaphore(name))
            return sems[name]

        bank = [stack.enter_context(nc.psum_tensor(f"bank{i}", [P, 512], F32)) for i in range(8)]

        early, late = sb("early", width(EARLY)), sb("late", width(LATE))
        ce, cl = columns(EARLY), columns(LATE)

        def wt(name, rows=P):
            if name in ce:
                return early[0:rows, ce[name][0]:ce[name][1]]
            return late[0:rows, cl[name][0]:cl[name][1]]

        ctx = sb("ctx", CTX)
        k1 = sb("k1", CTX)
        v1 = sb("v1", CTX)
        mask = sb("mask", CTX)
        x_tok = sb("x_tok", TOK)
        xb_tok = sb("xb_tok", TOK)
        xn_tok = sb("xn_tok", TOK)
        lnT = sb("lnT", TOK)
        work = sb("work", 16 * 512)
        otmp = sb("otmp", 512)
        o0 = sb("o0", TOK)
        spare = sb("spare", 512)
        stats, aggr = sb("stats", TT * 6), sb("aggr", TT * 2)
        veps, rstd, minus_half, half = sb("veps", 2 * TT), sb("rstd", 2 * TT), sb("minus_half", 2 * TT), sb("half", TT * E0)
        small = sb("small", 1024)

        def tile(i, n=1, of=work):
            return of[:, 512 * i:512 * (i + n)]

        def tok3(a):
            return a.rearrange("p (t d) -> p t d", t=TT)

        x3, xb3, xn3 = tok3(x_tok[:, :]), tok3(xb_tok[:, :]), tok3(xn_tok[:, :])
        st3, ag3 = stats[:, :].rearrange("p (t k) -> p t k", t=TT), aggr[:, :].rearrange("p (t k) -> p t k", t=TT)

        def over_tiles(row):
            return row.unsqueeze(1).broadcast_to([P, TT, D])


        def cols(h):
            return slice(HTOK * h, HTOK * (h + 1))

        def tiles_of(h):
            return range(HT * h, HT * (h + 1))

        def part(region, sizes, at):
            out = []
            for n in sizes:
                out.append(region[:, at:at + n])
                at += n
            return out, at

        X, Y, Z = bank[5], bank[6], bank[7]

        q0T, e0 = tile(0), tile(2)
        o0T = o0[:, :]
        v0s, vp = [tile(3), tile(4)], [tile(5), tile(6)]
        prod = [tile(7 + i) for i in range(HB)]
        mx0, sm0, rs0 = small[:, 0:32], small[:, 32:64], small[:, 64:96]
        wexp = small[:, 96:97]
        hspread = [tile(1)[:, 0:256], tile(1)[:, 256:512], otmp[:, 0:256], otmp[:, 256:512]]

        S33 = SEQ + 1
        N33 = HB * S33

        def b33(a):
            return a.rearrange("p (b s) -> p b s", s=S33)

        def now(a):
            return b33(a)[:, :, 1:S33]

        def prev(a):
            return b33(a)[:, :, 0:SEQ]

        def bs(a):
            return a.rearrange("p (b s) -> p b s", s=SEQ)

        MH = CTX // 2
        (ln33, dec33, k33, o33, A33, B33, Bv33), at = part(mask, [N33] * 7, MH)
        q33, p33 = o33, B33
        (dx, xk, xv, xr, ab, er, v_sb), at = part(mask, [HTOK] * 4 + [2 * HTOK] + [HTOK] * 2, at)
        top, t_bv, num, den = xk, dx, xv, xr
        assert at <= CTX

        hid, at = part(mask, [HTOK] * 5, MH + MH // 2)
        (cfT, fc0, fc1), at = part(mask, [HTOK, HT * E0 * E0, HT * E0 * E0], at)
        cfT = cfT[0:E0, :]
        fr = [small[:, 100 + HT * E0 * i:100 + HT * E0 * (i + 1)] for i in range(10)]

        NQ = 4
        qbd = [tile(i) for i in range(NQ)]
        NS, NT, NSC, NPT = 2, 2, 4, 8
        q1T = tile(15)
        sc = [tile(4 + i) for i in range(NSC - 1)] + [spare[:, :]]
        pt = [tile(7 + i) for i in range(NPT)]
        rsum, rinv, smin = small[:, 640:704], small[:, 704:768], small[:, 768:832]
        oT = q1T
        vkey = v1[:, :].rearrange("p (b k f) -> p b k f", b=BATCH, k=KT)

        (qp, att, qk, rden, kp_tok, add1, res4, g2), at = part(mask, [HTOK] * 8, 0)
        (vb, kvs), at = part(mask, [2 * HT * 256, 2 * HT * 256], at)
        assert at <= MH
        hT, mg = kvs, kvs
        ksum = small[:, 832:832 + HB]

        w1e = ctx[:, :].rearrange("p (e h) -> p e h", e=E1)
        w2e = k1[:, :].rearrange("p (e k d) -> p e k d", e=E1, k=4)
        moeb = v1[:, 0:2560]
        b1e, b2e = moeb[:, 0:2048], moeb[:, 2048:2560]
        (disp4, comb, slotbc), at = part(v1, [TT * SLOTS, 2048, 512], 2560)
        disp = [tile(t, of=disp4) for t in range(TT)]
        HS = SLOTS // 2
        YB = (6, 4, 7, 3)
        OB = (0, 1, 2, 5)
        RE = HT * E1
        (bufT, hmoe, hmoeT, ymoe, outt), at = part(mask, [512, 2048, 2048, 512, 512], 0)
        mr = [small[:, 64 * i:64 * (i + 1)] for i in range(8)]
        m4 = [small[:, 512 + 4 * i:516 + 4 * i] for i in range(8)]

        PIECES = (0, 2, 4, 8, 12, BATCH)
        PRE = 2
        PROJ = [(kind, b) for h in range(2) for kind in "kv" for b in range(HB * h, HB * (h + 1))]
        GAP = 2

        LAST = PRE + 2 * GAP + HB

        def taker(i):
            if i < LAST:
                return "proj_out", i + 1
            n = (i - LAST) // 2 + 1
            return ("proj_out_dve", n) if (i - LAST) % 2 else ("proj_out", LAST + n)

        def pace_local(step):
            return 1 if step <= 2 * HB or step % 4 != 0 else 0

        def beside(u, second, first):
            if u < UNITS:
                advance(second, 1)
            if u == UNITS - 1:
                finish(second)
            if u >= UNITS + OUT - GROUPS + 1:
                advance(first, 1 if u % 3 != 2 else 0)

        def last_stages(first, second):
            for k in range(STAGES):
                advance(second, 1)
                if k in (4, 8, 11):
                    advance(first, 1)
            finish(second)

        def advance(stages, n):
            for _ in range(n):
                next(stages, None)

        STAGES = 15

        def finish(stages):
            for _ in stages:
                pass

        block = stack.enter_context(nc.Block())

        @block.sync
        def _(sp):
            sp.dma_start(x3, x_d.rearrange("(t p) d -> p t d", p=P)).then_inc(sig("x_in"), 16)
            sp.dma_start(early[:, :], early_d).then_inc(sig("early_in"), 16)
            for c in range(len(PIECES) - 1):
                k = slice(KEYS * PIECES[c], KEYS * PIECES[c + 1])
                sp.dma_start(ctx[:, k], ctx_d[:, k]).then_inc(sig(f"ctx_in{c}"), 16)
                if c == 2:
                    sp.dma_start(late[:, :], late_d).then_inc(sig("late_in"), 16)
            for j in range(4):
                sp.dma_start(mask[32 * j:32 * j + 32, 0:MH], mask_d[:, 0:MH]).then_inc(sig("mask_in0"), 16)
            sp.wait_ge(sig("proj_done"), len(PROJ))
            sp.dma_start(ctx[:, :], w1_d).then_inc(sig("w1_in"), 16)
            for part, count in ((0, 5), (1, 6)):
                sp.wait_ge(sig("x_new"), count)
                lo = MH + part * (MH // 2)
                for j in range(4):
                    sp.dma_start(mask[32 * j:32 * j + 32, lo:lo + MH // 2], mask_d[:, lo:lo + MH // 2])\
                        .then_inc(sig(f"mask_in{1 + part}"), 16)
            sp.wait_ge(sig("s1_ready"), 2 * UNITS)
            sp.dma_start(k1[:, :], w2_d).then_inc(sig("w2_in"), 16)
            sp.wait_ge(sig("o1_ready"), BATCH)
            sp.dma_start(moeb, moeb_d).then_inc(sig("moeb_in"), 16)
            for h in range(2):
                sp.wait_ge(sig("out_ready"), HT * (h + 1))
                t = slice(HT * h, HT * (h + 1))
                sp.dma_start(out_d.rearrange("(t p) d -> p t d", p=P)[:, t, :], tok3(outt)[:, t, :]).then_inc(sig("stored"), 16)
            sp.wait_ge(sig("stored"), 32)

        @block.gpsimd
        def _(pool):
            g = nc.gpsimd
            pool.memset(q1T, 0.0).then_inc(sig("blank_ready"), 1)
            pool.memset(minus_half[:, :], -0.5).then_inc(sig("half_ready"), 1)
            pool.memset(half[:, :], 0.5).then_inc(sig("half_ready"), 1)
            pool.wait_ge(sig("half_ready"), 2)
            norms = [0]

            def inverse_std(tiles, extra=False):
                norms[0] += 1
                pool.wait_ge(sig("ln_var"), norms[0])
                views = [a[:, :].rearrange("p (k t) -> p k t", k=2)[:, 0:2 if extra else 1, tiles.start:tiles.stop]
                         for a in (rstd, veps, minus_half)]
                g.tensor_tensor(*views, ALU.pow).then_inc(sig("ln_rstd"), 1)

            def residual_bias(name, tiles, count):
                if count:
                    pool.wait_ge(sig("x_new"), count)
                t = slice(tiles.start, tiles.stop)
                g.tensor_tensor(xb3[:, t, :], x3[:, t, :], over_tiles(wt(name))[:, 0:len(tiles), :],
                                ALU.add).then_inc(sig("xb_ready"), 1)

            def edges():
                for a, v in ((ln33, 0.0), (k33, NEG_STATE), (A33, 0.0), (B33, 0.0), (Bv33, 0.0), (dec33, NEG_STATE)):
                    pool.memset(b33(a)[:, :, 0:1], v).then_inc(sig("edges_ready"), 1)

            def queries(h, lo, hi):
                own = wt("own16").unsqueeze(2).broadcast_to([P, HEADS, SEQ])
                if lo == 0:
                    pool.wait_ge(sig("q1_ready"), h + 1)
                    pool.wait_ge(sig("p0_spread"), BATCH)
                    pool.wait_ge(sig("vp_ready"), BATCH)
                    pool.wait_ge(sig("prod_ready"), BATCH)
                for b in range(HB * h + lo, HB * h + hi):
                    if b >= NQ:
                        pool.wait_ge(sig("s1_ready"), GROUPS * (b - NQ + 1))
                    qv = q1T[:, SEQ * b:SEQ * (b + 1)].unsqueeze(1).broadcast_to([P, HEADS, SEQ])
                    g.tensor_tensor(qbd[b % NQ].rearrange("p (j q) -> p j q", j=HEADS), qv, own, ALU.mult)\
                        .then_inc(sig("qbd_ready"), 1)

            def full(second, first):
                for u in range(2 * UNITS + LAG):
                    h, b = divmod(u // GROUPS, HB)
                    if u % UNITS == 0 and h < 2:
                        queries(h, 0, NQ)
                    if u % GROUPS == 0 and h < 2 and 0 < b <= HB - NQ:
                        queries(h, b + NQ - 1, b + NQ)
                    beside(u, second, first)

            def small_stages(h):
                tiles = tiles_of(h)
                yield
                if h:
                    pool.wait_ge(sig("x_new"), 3)
                edges()
                inverse_std(tiles)
                yield
                yield
                yield
                yield
                yield
                pool.wait_ge(sig("ab_exp"), h + 1)
                pool.wait_ge(sig("v_out"), h + 1)
                g.tensor_tensor(t_bv, ab[:, HTOK:2 * HTOK], v_sb, ALU.mult).then_inc(sig("bonus_ready"), 1)
                yield
                yield
                yield
                yield
                yield
                yield
                yield
                inverse_std(tiles)
                residual_bias("sb2", tiles, 3 * h + 2)
                yield
                yield
                yield
                yield
                pool.wait_ge(sig("softplus_ready"), h + 1)
                g.tensor_tensor(fr[6], fr[5], half[:, 0:HT * E0], ALU.pow).then_inc(sig("act_ready"), 1)
                yield
                yield
                yield
                yield
                yield
                yield
                inverse_std(tiles)
                residual_bias("bo1", tiles, 3 * h + 3)
                yield
                yield
                yield

            def linear_stages(h):
                yield
                yield
                yield
                inverse_std(tiles_of(h), extra=True)
                yield
                for _ in range(6):
                    yield
                inverse_std(tiles_of(h))
                g.tensor_tensor(res4, x_tok[:, cols(h)], add1, ALU.add).then_inc(sig("res_ready"), 1)
                yield
                for _ in range(3):
                    yield
                inverse_std(tiles_of(h))
                yield

            inverse_std(range(TT))
            pool.wait_ge(sig("x_in"), 16)
            pool.wait_ge(sig("early_in"), 16)
            for j in range(4):
                g.tensor_tensor(hspread[j], wt("headspread"), wt("rowblock")[:, j:j + 1].broadcast_to([P, 256]),
                                ALU.mult).then_inc(sig("hspread_ready"), 1)
            residual_bias("bo0", range(TT), 0)
            finish(small_stages(0))
            first = linear_stages(0)
            full(small_stages(1), first)
            last_stages(first, linear_stages(1))

        @block.scalar
        def _(act):
            s = nc.scalar
            turned = [0]

            def normT(dst, src, **affine):
                turned[0] += 1
                act.wait_ge(sig("lnT_ps"), turned[0])
                s.activation(dst, src, ACT.Identity, **affine).then_inc(sig("lnT_ready"), 1)

            nproj = [0]

            def projection():
                i = nproj[0]
                nproj[0] += 1
                if taker(i)[0] != "proj_out":
                    return
                kind, b = PROJ[i]
                act.wait_ge(sig("proj_done"), i + 1)
                src = bank[3 + i % 2][:, :]
                dst = (k1 if kind == "k" else v1)[:, KEYS * b:KEYS * (b + 1)]
                if kind == "k":
                    s.activation(dst, src, ACT.Identity, bias=wt("bk1")).then_inc(sig("proj_out"), 1)
                else:
                    s.copy(dst, src).then_inc(sig("proj_out"), 1)

            def local(h, stages, pace):
                step = 0
                for c in range(HB):
                    if h:
                        projection()
                    advance(stages, pace(step))
                    step += 1
                act.wait_ge(sig("e0_arg"), h + 1)
                s.activation(e0, e0, ACT.Exp).then_inc(sig("e0_exp"), 1)

                def values(c):
                    act.wait_ge(sig("v0_ps"), c + 1)
                    if c >= 2:
                        act.wait_ge(sig("vp_ready"), c - 1)
                    s.activation(v0s[c % 2], bank[c % 2][:, :], ACT.Identity, bias=wt("bv0")).then_inc(sig("v0_ready"), 1)

                values(HB * h)
                values(HB * h + 1)
                for _ in range(GAP):
                    projection()
                advance(stages, pace(step))
                step += 1
                for c in range(HB * h, HB * (h + 1)):
                    if c + 2 < HB * (h + 1):
                        values(c + 2)
                    advance(stages, pace(step))
                    step += 1
                if h:
                    while nproj[0] < len(PROJ):
                        projection()
                        advance(stages, pace(step))
                        step += 1

            def small_stages(h):
                yield
                yield
                yield
                if h == 0:
                    s.activation(wexp, wt("w"), ACT.Exp).then_inc(sig("wexp_raw"), 1)
                act.wait_ge(sig("edges_ready"), 6 * h + 6)
                normT(now(ln33), bs(X[:, 0:HTOK]))
                yield
                yield
                act.wait_ge(sig("rkvr_ps"), 3 * h + 2)
                s.copy(now(k33), bs(X[:, 0:HTOK])).then_inc(sig("k_out"), 1)
                s.copy(v_sb, X[:, HTOK:2 * HTOK]).then_inc(sig("v_out"), 1)
                act.wait_ge(sig("rkvr_ps"), 3 * h + 3)
                s.activation(er, Y[:, 0:HTOK], ACT.Exp, scale=-1.0).then_inc(sig("er_ready"), 1)
                yield
                act.wait_ge(sig("ab_arg"), 2 * h + 2)
                s.activation(ab, ab, ACT.Exp).then_inc(sig("ab_exp"), 1)
                for n, a in enumerate((A33, B33)):
                    act.wait_ge(sig("AB_arg"), 2 * h + n + 1)
                    s.activation(now(a), now(a), ACT.Exp).then_inc(sig("AB_exp"), 1)
                yield
                yield
                yield
                yield
                yield
                yield
                yield
                yield
                yield
                normT(lnT[:, cols(h)], X[:, 0:HTOK])
                yield
                act.wait_ge(sig("abs_ready"), h + 1)
                s.activation(fr[2], fr[1], ACT.Exp, scale=-1.0).then_inc(sig("e_ready"), 1)
                act.wait_ge(sig("w_ready"), h + 1)
                s.activation(fr[4], fr[3], ACT.Ln).then_inc(sig("ln_ready"), 1)
                yield
                for n in range(5):
                    act.wait_ge(sig("hid_ps"), 3 * h + (1, 1, 2, 2, 3)[n])
                    rows = P if n < 4 else H0
                    src = (X[:, 0:HTOK], X[:, HTOK:], Y[:, 0:HTOK], Y[:, HTOK:], Z[0:H0, 0:HTOK])[n]
                    bias = wt("rb1")[:, n:n + 1] if n < 4 else wt("sb1", H0)
                    s.activation(hid[n][0:rows, :], src, ACT.Silu, bias=bias).then_inc(sig("hid_ready"), 1)
                yield
                yield
                yield
                yield
                yield
                yield
                yield
                yield
                normT(lnT[:, cols(h)], X[:, 0:HTOK])
                yield
                yield

            def full(second, first):
                for u in range(2 * UNITS + LAG):
                    if u < 2 * UNITS:
                        act.wait_ge(sig("s1_min"), u + 1)
                        s.activation(sc[u % NSC], sc[u % NSC], ACT.Exp, bias=smin[:, u:u + 1], scale=-1.0,
                                     accum_out=rsum[:, u:u + 1]).then_inc(sig("p1_ready"), 1)
                    j = u - LAG
                    if j >= 0 and j % 2 == 0:
                        act.wait_ge(sig("pT_ps"), j + 1)
                        if j >= NPT:
                            act.wait_ge(sig("o1_ready"), (j - NPT) // GROUPS + 1)
                        s.copy(pt[j % NPT], bank[2 + j % NT][:, :]).then_inc(sig("pT_even"), 1)
                    beside(u, second, first)

            def linear_stages(h):
                yield
                yield
                yield
                yield
                yield
                normT(lnT[:, cols(h)], X[:, 0:HTOK], scale=wt("gamma"), bias=wt("beta"))
                yield
                act.wait_ge(sig("vtok_ps"), h + 1)
                for b in range(4):
                    at = 512 + P * b
                    s.activation(vb[:, at:at + P], Z[:, 0:P], ACT.Identity, scale=wt("batchof")[:, b:b + 1])\
                        .then_inc(sig("vb2_ready"), 1)
                yield
                yield
                yield
                yield
                yield
                yield
                normT(lnT[:, cols(h)], X[:, 0:HTOK], scale=wt("gamma"), bias=wt("beta"))
                yield
                for n in range(4):
                    act.wait_ge(sig("ffh_ps"), 2 * h + n // 2 + 1)
                    s.activation(hT[:, HTOK * n:HTOK * (n + 1)], (Y, Z)[n // 2][:, HTOK * (n % 2):HTOK * (n % 2 + 1)], ACT.Gelu,
                                 bias=wt("b1")[:, n:n + 1]).then_inc(sig("ffh_ready"), 1)
                yield
                act.wait_ge(sig("ffo_ready"), h + 1)
                s.activation(g2, g2, ACT.Gelu).then_inc(sig("g2_ready"), 1)
                yield
                yield
                yield
                normT(lnT[:, cols(h)], X[:, 0:HTOK])
                yield
                yield
                yield
                act.wait_ge(sig("gate_arg"), h + 1)
                e = slice(RE * h, RE * (h + 1))
                s.activation(mr[2][:, e], mr[1][:, e], ACT.Exp).then_inc(sig("gate_exp"), 1)
                yield
                yield
                yield

            act.wait_ge(sig("blank_ready"), 1)
            s.activation(wexp, q1T[:, 0:1], ACT.Exp).then_inc(sig("table_in"), 1)
            act.wait_ge(sig("early_in"), 16)
            act.wait_ge(sig("table_in"), 1)
            projection()
            normT(lnT[:, :], X[:, :])
            for _ in range(1, PRE):
                projection()
            local(0, iter(()), pace_local)
            stages = small_stages(0)
            local(1, stages, pace_local)
            finish(stages)
            first = linear_stages(0)
            full(small_stages(1), first)
            last_stages(first, linear_stages(1))
            act.wait_ge(sig("buf_ps"), 2)
            s.copy(bufT[:, HS:SLOTS], bank[3][:, 0:HS]).then_inc(sig("buf_b_ready"), 1)
            for g in range(4):
                act.wait_ge(sig("hmT_ps"), g + 1)
                s.activation(hmoeT[:, 512 * g:512 * (g + 1)], bank[g][:, :], ACT.Relu).then_inc(sig("hmT_ready"), 1)

        @block.vector
        def _(dve):
            v = nc.vector
            ch = Chain(dve, sig("dve_step"))
            norms, ready, xver = [0], [0], [0]

            def statistics(src3, tiles, eps, extra=None):
                for t in tiles:
                    ch.add(v.bn_stats(st3[:, t, :], src3[:, t, :]))
                ch.join()
                for t in tiles:
                    ch.add(v.bn_aggr(ag3[:, t, :], st3[:, t, :]))
                ch.join()
                ts = slice(tiles.start, tiles.stop)
                if extra is None:
                    v.tensor_scalar(veps[:, ts], ag3[:, ts, 1], eps, None, ALU.add).then_inc(sig("ln_var"), 1)
                else:
                    second = slice(TT + tiles.start, TT + tiles.stop)
                    ch.link(v.tensor_scalar(veps[:, ts], ag3[:, ts, 1], eps, None, ALU.add))
                    ch.link(v.reciprocal(veps[:, second], veps[:, ts]))
                    ch.link(v.tensor_tensor(veps[:, second], veps[:, second], ag3[:, ts, 1], ALU.mult))
                    v.tensor_scalar(veps[:, second], veps[:, second], extra, None, ALU.add).then_inc(sig("ln_var"), 1)
                norms[0] += 1

            def normalize(src3, tiles, dst3=None):
                if dst3 is None:
                    dst3 = xn3
                    dve.wait_ge(sig("ln_rstd"), norms[0])
                    for t in tiles:
                        v.tensor_scalar(dst3[:, t, :], src3[:, t, :], ag3[:, t, 0:1], rstd[:, t:t + 1],
                                        ALU.subtract, ALU.mult).then_inc(sig("xn_ready"), 1)
                    ready[0] += len(tiles)
                else:
                    dve.wait_ge(sig("ln_rstd"), norms[0])
                    first, second = (rstd[:, k + tiles.start:k + tiles.stop] for k in (0, TT))
                    ch.link(v.tensor_tensor(second, second, first, ALU.mult))
                    for t in tiles:
                        v.tensor_scalar(xn3[:, t, :], src3[:, t, :], ag3[:, t, 0:1], rstd[:, TT + t:TT + t + 1],
                                        ALU.subtract, ALU.mult).then_inc(sig("xn_ready"), 1)
                    ready[0] += len(tiles)
                    for t in tiles:
                        ch.add(v.tensor_scalar(dst3[:, t, :], src3[:, t, :], ag3[:, t, 0:1], rstd[:, t:t + 1],
                                               ALU.subtract, ALU.mult))
                    ch.join()

            def residual(src, base, c):
                v.tensor_tensor(x_tok[:, c], src, base, ALU.add).then_inc(sig("x_new"), 1)
                xver[0] += 1
                dve.wait_ge(sig("x_new"), xver[0])

            def local(h, stages, pace):
                step = 0
                for c in range(HB * h, HB * (h + 1)):
                    dve.wait_ge(sig("k0_ps"), c + 1)
                    qb = q0T[:, SEQ * c:SEQ * (c + 1)].unsqueeze(2).broadcast_to([P, SEQ, LOCAL])
                    v.scalar_tensor_tensor(prod[c % HB].rearrange("p (q j) -> p q j", j=LOCAL),
                                           bank[c % 2][:, :].rearrange("p (q j) -> p q j", j=LOCAL), wt("bk0"), qb,
                                           ALU.add, ALU.mult).then_inc(sig("prod_ready"), 1)
                    advance(stages, pace(step))
                    step += 1
                dve.wait_ge(sig("s0_ps"), 2 * h + 2)
                sv = bank[2][:, :].rearrange("p (q j) -> p q j", j=LOCAL)
                e = e0.rearrange("p (q j) -> p q j", j=LOCAL)
                wide = lambda a: a.unsqueeze(2).broadcast_to([P, SEQ, LOCAL])
                ch.link(v.tensor_reduce(mx0, sv, AX_X, ALU.max))
                if h:
                    dve.wait_ge(sig("p0_spread"), HB)
                v.tensor_tensor(e, sv, wide(mx0), ALU.subtract).then_inc(sig("e0_arg"), 1)
                dve.wait_ge(sig("e0_exp"), h + 1)
                ch.link(v.tensor_reduce(sm0, e, AX_X, ALU.add))
                ch.link(v.reciprocal(rs0, sm0))
                v.tensor_tensor(e, e, wide(rs0), ALU.mult).then_inc(sig("p0_ready"), 1)
                advance(stages, pace(step))
                step += 1
                for c in range(HB * h, HB * (h + 1)):
                    dve.wait_ge(sig("p0_spread"), c + 1)
                    dve.wait_ge(sig("v0_ready"), c + 1)
                    v.tensor_tensor(vp[c % 2], bank[3 + c % 2][:, :], v0s[c % 2], ALU.mult).then_inc(sig("vp_ready"), 1)
                    dve.wait_ge(sig("vp_ready"), c + 1)
                    v.tensor_reduce(o0T[:, SEQ * c:SEQ * (c + 1)], vp[c % 2].rearrange("p (q j) -> p q j", j=LOCAL),
                                    AX_X, ALU.add).then_inc(sig("o0_ready"), 1)
                    advance(stages, pace(step))
                    step += 1
                if h:
                    for i in range(LAST, len(PROJ)):
                        if taker(i)[0] == "proj_out_dve":
                            kind, b = PROJ[i]
                            dve.wait_ge(sig("proj_done"), i + 1)
                            src, k = bank[3 + i % 2][:, :], slice(KEYS * b, KEYS * (b + 1))
                            if kind == "k":
                                v.tensor_scalar(k1[:, k], src, wt("bk1"), None, ALU.add).then_inc(sig("proj_out_dve"), 1)
                            else:
                                v.tensor_copy(v1[:, k], src).then_inc(sig("proj_out_dve"), 1)
                        advance(stages, pace(step))
                        step += 1

            def small_stages(h):
                tiles, c = tiles_of(h), cols(h)
                yield
                dve.wait_ge(sig("xo_ps"), 3 * h + 1)
                dve.wait_ge(sig("xb_ready"), (1, 3)[h])
                residual(Z[:, 0:HTOK], xb_tok[:, c], c)
                statistics(x3, tiles, EPS_OUTER)
                yield
                normalize(x3, tiles)
                yield
                dve.wait_ge(sig("late_in"), 16)
                dve.wait_ge(sig("edges_ready"), 6 * h + 6)
                if h == 0:
                    dve.wait_ge(sig("wexp_raw"), 1)
                    ch.link(v.tensor_scalar(wexp, wexp, -1.0, None, ALU.mult))
                ch.link(v.memset(now(dec33), 0.0))
                ch.link(v.tensor_scalar(now(dec33), now(dec33), wexp, None, ALU.add))
                yield
                dve.wait_ge(sig("lnT_ready"), (2, 5)[h])
                ch.link(v.tensor_tensor(bs(dx), now(ln33), prev(ln33), ALU.subtract))
                for dst, mix in ((xk, "mk"), (xv, "mv"), (xr, "mr")):
                    v.scalar_tensor_tensor(bs(dst), bs(dx), wt(mix), prev(ln33), ALU.mult, ALU.add).then_inc(sig("mix_ready"), 1)
                yield
                yield
                dve.wait_ge(sig("k_out"), h + 1)
                ch.link(v.tensor_tensor_scan(o33, dec33, k33, NEG_STATE, ALU.add, ALU.max))
                dve.wait_ge(sig("rkvr_ps"), 3 * h + 3)
                dve.wait_ge(sig("mix_ready"), 3 * h + 3)
                ch.link(v.scalar_tensor_tensor(bs(top), now(k33), wt("u"), prev(o33), ALU.add, ALU.max))
                v.tensor_tensor(bs(ab[:, 0:HTOK]), prev(o33), bs(top), ALU.subtract).then_inc(sig("ab_arg"), 1)
                v.scalar_tensor_tensor(bs(ab[:, HTOK:2 * HTOK]), now(k33), wt("u"), bs(top), ALU.add, ALU.subtract)\
                    .then_inc(sig("ab_arg"), 1)
                v.scalar_tensor_tensor(now(A33), prev(o33), wexp, now(o33), ALU.add, ALU.subtract).then_inc(sig("AB_arg"), 1)
                v.tensor_tensor(now(B33), now(k33), now(o33), ALU.subtract).then_inc(sig("AB_arg"), 1)
                yield
                dve.wait_ge(sig("AB_exp"), 2 * h + 2)
                dve.wait_ge(sig("ab_arg"), 2 * h + 2)
                dve.wait_ge(sig("v_out"), h + 1)
                ch.add(v.tensor_tensor(now(Bv33), now(B33), bs(v_sb), ALU.mult))
                ch.link(v.tensor_tensor_scan(q33, A33, B33, 0.0, ALU.mult, ALU.add))
                yield
                dve.wait_ge(sig("ab_exp"), h + 1)
                ch.add(v.tensor_tensor(bs(den), bs(ab[:, 0:HTOK]), prev(q33), ALU.mult))
                ch.link(v.tensor_tensor_scan(p33, A33, Bv33, 0.0, ALU.mult, ALU.add))
                yield
                ch.add(v.tensor_tensor(den, den, ab[:, HTOK:2 * HTOK], ALU.add))
                ch.link(v.tensor_tensor(bs(num), bs(ab[:, 0:HTOK]), prev(p33), ALU.mult))
                dve.wait_ge(sig("er_ready"), h + 1)
                dve.wait_ge(sig("bonus_ready"), h + 1)
                ch.add(v.scalar_tensor_tensor(den, er, 1.0, den, ALU.add, ALU.mult))
                ch.link(v.tensor_tensor(num, num, t_bv, ALU.add))
                yield
                ch.link(v.reciprocal(den, den))
                v.tensor_tensor(num, num, den, ALU.mult).then_inc(sig("rw_ready"), 1)
                yield
                yield
                yield
                dve.wait_ge(sig("xo_ps"), 3 * h + 2)
                residual(Z[:, 0:HTOK], x_tok[:, c], c)
                statistics(x3, tiles, EPS_OUTER)
                yield
                normalize(x3, tiles)
                yield
                yield
                e3 = lambda a: a.rearrange("p (t e) -> p t e", e=E0)
                logit, mag, ex, wl, lw, sp, av, t0, t1, cf = fr
                dve.wait_ge(sig("route_ps"), h + 1)
                eb = wt("eb").unsqueeze(1).broadcast_to([P, HT, E0])
                ch.link(v.tensor_tensor(e3(logit), e3(Z[:, 0:HT * E0]), eb, ALU.add))
                v.scalar_tensor_tensor(mag, logit, -1.0, logit, ALU.mult, ALU.max).then_inc(sig("abs_ready"), 1)
                dve.wait_ge(sig("e_ready"), h + 1)
                v.tensor_scalar(wl, ex, 1.0, None, ALU.add).then_inc(sig("w_ready"), 1)
                dve.wait_ge(sig("w_ready"), h + 1)
                ch.link(v.tensor_scalar(t0, wl, -1.0, 1e-30, ALU.add, ALU.max))
                ch.link(v.reciprocal(t0, t0))
                ch.add(v.scalar_tensor_tensor(t1, wl, 1.0, ex, ALU.is_equal, ALU.mult))
                ch.link(v.tensor_tensor(t0, t0, ex, ALU.mult))
                yield
                dve.wait_ge(sig("ln_ready"), h + 1)
                ch.link(v.tensor_tensor(t0, t0, lw, ALU.mult))
                ch.link(v.tensor_tensor(t0, t0, t1, ALU.add))
                v.scalar_tensor_tensor(sp, logit, 0.0, t0, ALU.max, ALU.add).then_inc(sig("softplus_ready"), 1)
                yield
                dve.wait_ge(sig("act_ready"), h + 1)
                pair = [P, HT, E0, E0]
                f4 = [a.rearrange("p (t e j) -> p t e j", t=HT, e=E0) for a in (fc0, fc1)]
                a_j, a_e = e3(av).unsqueeze(2).broadcast_to(pair), e3(av).unsqueeze(3).broadcast_to(pair)
                ch.add(v.tensor_tensor(f4[0], a_j, a_e, ALU.is_gt))
                ch.link(v.tensor_tensor(f4[1], a_j, a_e, ALU.is_equal))
                before = wt("before").unsqueeze(1).broadcast_to([P, HT, E0 * E0])
                f3 = fc1.rearrange("p (t k) -> p t k", t=HT)
                yield
                ch.link(v.tensor_tensor(f3, f3, before, ALU.mult))
                ch.link(v.tensor_tensor(fc0, fc0, fc1, ALU.add))
                ch.link(v.tensor_reduce(t1, fc0.rearrange("p (k j) -> p k j", j=E0), AX_X, ALU.add))
                v.scalar_tensor_tensor(cf, t1, 1.5, av, ALU.is_lt, ALU.mult).then_inc(sig("cf_ready"), 1)
                yield
                dve.wait_ge(sig("cfT_ps"), h + 1)
                v.tensor_copy(cfT, Z[0:E0, 0:HTOK]).then_inc(sig("cfT_ready"), 1)
                yield
                for n in range(4):
                    dve.wait_ge(sig("spread_ps"), 2 * h + n // 2 + 1)
                    dve.wait_ge(sig("hid_ready"), 5 * h + n + 1)
                    v.tensor_tensor(hid[n], hid[n], (X, Y)[n // 2][:, HTOK * (n % 2):HTOK * (n % 2 + 1)],
                                    ALU.mult).then_inc(sig("hsc_ready"), 1)
                yield
                yield
                dve.wait_ge(sig("xo_ps"), 3 * h + 3)
                dve.wait_ge(sig("xb_ready"), (2, 4)[h])
                residual(Z[:, 0:HTOK], xb_tok[:, c], c)
                statistics(x3, tiles, EPS_OUTER)
                yield
                normalize(x3, tiles)
                yield
                yield
                dve.wait_ge(sig("q1_ps"), h + 1)
                ch.link(v.tensor_scalar(q1T[:, c], Y[:, 0:HTOK], wt("bq1"), -QSCALE, ALU.add, ALU.mult))
                v.tensor_scalar(q1T[:, c], q1T[:, c], 1.0 / MASK_BIG, None, ALU.mult).then_inc(sig("q1_ready"), 1)
                yield

            def take_heads(n):
                dve.wait_ge(sig("o1_ready"), 4 * n + 4)
                o = bank[4][:, :].rearrange("p (b j q) -> p b j q", b=4, j=4)
                t = otmp[:, :].rearrange("p (b j q) -> p b j q", b=4, j=4)
                own_b = wt("own4").unsqueeze(1).unsqueeze(3).broadcast_to([P, 4, 4, SEQ])
                v.tensor_tensor(t, o, own_b, ALU.mult).then_inc(sig("o1_taken"), 1)
                dve.wait_ge(sig("o1_taken"), n + 1)
                ch.link(v.tensor_reduce(oT[:, P * n:P * (n + 1)].rearrange("p (b q) -> p b q", b=4),
                                        t.rearrange("p b j q -> p b q j"), AX_X, ALU.add))

            def full(second, first):
                for u in range(2 * UNITS + LAG):
                    if u < 2 * UNITS:
                        dve.wait_ge(sig("s1_ready"), u + 1)
                        if u >= NSC:
                            dve.wait_ge(sig("pT_ps"), u - NSC + 1)
                        b = u // GROUPS
                        if u in (0, UNITS, UNITS + UNITS // 2):
                            dve.wait_ge(sig(f"mask_in{u * 2 // UNITS - u // UNITS}"), 64)
                        v.tensor_tensor_reduce(sc[u % NSC], bank[u % NS][:, :], mask[:, KEYS * b:KEYS * (b + 1)], MASK_BIG, 3e38,
                                               ALU.add, ALU.min, smin[:, u:u + 1]).then_inc(sig("s1_min"), 1)
                    j = u - LAG
                    if j >= 0 and j % 2 == 1:
                        dve.wait_ge(sig("pT_ps"), j + 1)
                        if j >= NPT:
                            dve.wait_ge(sig("o1_ready"), (j - NPT) // GROUPS + 1)
                        v.tensor_copy(pt[j % NPT], bank[2 + j % NT][:, :]).then_inc(sig("pT_odd"), 1)
                    if u % UNITS == TAKE:
                        take_heads(2 * (u // UNITS))
                    beside(u, second, first)

            def linear_stages(h):
                tiles, c = tiles_of(h), cols(h)
                dve.wait_ge(sig("p1_ready"), UNITS * (h + 1))
                if h:
                    dve.wait_ge(sig("ffo_ps"), 1)
                rs = slice(UNITS * h, UNITS * (h + 1))
                ch.link(v.reciprocal(rinv[:, rs], rsum[:, rs]))
                mg4 = mg.rearrange("p (g b q) -> p g b q", g=4, b=HB)
                ri = rinv[:, rs].rearrange("p (b g) -> p g b", g=GROUPS)
                rows = wt("rows32").unsqueeze(1).broadcast_to([P, HB, SEQ])
                for g in range(GROUPS):
                    v.tensor_tensor(mg4[:, g, :, :], rows, ri[:, g, :].unsqueeze(2).broadcast_to([P, HB, SEQ]),
                                    ALU.mult).then_inc(sig("mg_ready"), 1)
                take_heads(2 * h + 1)
                yield
                yield
                dve.wait_ge(sig("rinv_ps"), h + 1)
                ch.link(v.tensor_tensor(oT[:, c], oT[:, c], X[:, 0:HTOK], ALU.mult))
                v.tensor_scalar(oT[:, c], oT[:, c], wt("bv1"), None, ALU.add).then_inc(sig("o1T_ready"), 1)
                yield
                dve.wait_ge(sig("xo_ps"), 7 + h)
                dve.wait_ge(sig("xb_ready"), 5)
                residual(Y[:, 0:HTOK], xb_tok[:, c], c)
                statistics(x3, tiles, EPS_OUTER, EPS_INNER)
                yield
                normalize(x3, tiles, xb3)
                yield
                yield
                dve.wait_ge(sig("qk_ps"), h + 1)
                ch.add(v.tensor_scalar(qp, X[:, 0:HTOK], 0.0, STAB, ALU.max, ALU.add))
                v.tensor_scalar(kp_tok, X[:, HTOK:2 * HTOK], 0.0, STAB, ALU.max, ALU.add).then_inc(sig("kp_ready"), 1)
                ch.join()
                dve.wait_ge(sig("vtok_ps"), h + 1)
                v.tensor_tensor(vb[:, 0:512].rearrange("p (b d) -> p b d", b=4),
                                Y[:, 0:P].unsqueeze(1).broadcast_to([P, 4, P]),
                                wt("batchof").unsqueeze(2).broadcast_to([P, 4, P]), ALU.mult).then_inc(sig("vb_ready"), 1)
                yield
                dve.wait_ge(sig("ksum_ps"), h + 1)
                ch.link(v.tensor_copy(ksum, Y[:, 0:HB]))
                v.tensor_tensor(bs(qk), bs(qp), ksum.unsqueeze(2).broadcast_to([P, HB, SEQ]), ALU.mult).then_inc(sig("qksum_ready"), 1)
                yield
                same4 = wt("samehead").unsqueeze(1).broadcast_to([P, 4, D])
                for t in range(HT):
                    dve.wait_ge(sig("kvs_ps"), HT * h + t + 1)
                    v.tensor_tensor(kvs[:, 512 * t:512 * (t + 1)].rearrange("p (b d) -> p b d", b=4),
                                    (X, Z)[t][:, :].rearrange("p (b d) -> p b d", b=4), same4, ALU.mult).then_inc(sig("kvs_ready"), 1)
                yield
                dve.wait_ge(sig("den_ps"), h + 1)
                ch.link(v.reciprocal(rden, Y[:, 0:HTOK]))
                dve.wait_ge(sig("num_ps"), h + 1)
                v.tensor_tensor(att, rden, X[:, 0:HTOK], ALU.mult).then_inc(sig("att_ready"), 1)
                yield
                dve.wait_ge(sig("ao_ps"), h + 1)
                v.tensor_tensor(add1, Z[:, 0:HTOK], xb_tok[:, c], ALU.add).then_inc(sig("add1_ready"), 1)
                dve.wait_ge(sig("add1_ready"), h + 1)
                a3 = add1.rearrange("p (t d) -> p t d", d=D)
                a3 = {t: a3[:, t - tiles.start, :] for t in tiles}
                view = Shifted(a3)
                statistics(view, tiles, EPS_INNER)
                yield
                normalize(view, tiles)
                yield
                yield
                yield
                dve.wait_ge(sig("ffo_ps"), h + 1)
                v.tensor_tensor(g2.rearrange("p (t d) -> p t d", d=D), X[:, 0:HTOK].rearrange("p (t d) -> p t d", d=D),
                                over_tiles(wt("b2"))[:, 0:HT, :], ALU.add).then_inc(sig("ffo_ready"), 1)
                dve.wait_ge(sig("g2_ready"), h + 1)
                dve.wait_ge(sig("res_ready"), h + 1)
                residual(g2, res4, c)
                yield
                statistics(x3, tiles, EPS_OUTER)
                yield
                normalize(x3, tiles)
                yield
                yield
                yield
                e = slice(RE * h, RE * (h + 1))
                ge = lambda a: a[:, e].rearrange("p (t e) -> p t e", e=E1)
                one = lambda k: m4[k][:, HT * h:HT * (h + 1)]
                wide = lambda a: a.unsqueeze(2).broadcast_to([P, HT, E1])
                flat = lambda name: wt(name).unsqueeze(1).broadcast_to([P, HT, E1])
                dve.wait_ge(sig("gate_ps"), h + 1)
                ch.link(v.tensor_tensor(ge(mr[0]), ge(Z[:, 0:64]), flat("bg"), ALU.add))
                ch.link(v.tensor_reduce(one(0), ge(mr[0]), AX_X, ALU.max))
                v.tensor_tensor(ge(mr[1]), ge(mr[0]), wide(one(0)), ALU.subtract).then_inc(sig("gate_arg"), 1)
                yield
                dve.wait_ge(sig("gate_exp"), h + 1)
                ch.link(v.tensor_reduce(one(1), ge(mr[2]), AX_X, ALU.add))
                ch.link(v.reciprocal(one(2), one(1)))
                ch.link(v.tensor_tensor(ge(mr[3]), ge(mr[2]), wide(one(2)), ALU.mult))
                ch.link(v.tensor_reduce(one(3), ge(mr[3]), AX_X, ALU.max))
                ch.link(v.tensor_tensor(ge(mr[4]), ge(mr[3]), wide(one(3)), ALU.not_equal))
                ch.link(v.scalar_tensor_tensor(ge(mr[4]), ge(mr[4]), float(E1), flat("iota_e"), ALU.mult, ALU.add))
                ch.link(v.tensor_reduce(one(4), ge(mr[4]), AX_X, ALU.min))
                v.tensor_tensor(ge(mr[5]), flat("iota_e"), wide(one(4)), ALU.is_equal).then_inc(sig("onehot_ready"), 1)
                dve.wait_ge(sig("onehot_ready"), h + 1)
                yield
                yield
                dve.wait_ge(sig("count_ps"), h + 1)
                ch.link(v.scalar_tensor_tensor(ge(mr[6]), ge(bank[0][:, 0:64]), -1.0, ge(mr[5]), ALU.add, ALU.mult))
                ch.link(v.tensor_reduce(one(5), ge(mr[6]), AX_X, ALU.add))
                ch.add(v.tensor_scalar(one(6), one(5), CAP - 0.5, float(4 * SLOTS), ALU.is_gt, ALU.mult))
                ch.link(v.scalar_tensor_tensor(one(7), one(4), float(CAP), one(5), ALU.mult, ALU.add))
                ch.link(v.tensor_tensor(one(7), one(7), one(6), ALU.add))
                for t in tiles:
                    v.tensor_scalar(disp[t], wt("iota_slot"), m4[7][:, t:t + 1], None, ALU.is_equal).then_inc(sig("disp_ready"), 1)
                yield

            dve.wait_ge(sig("x_in"), 16)
            statistics(x3, range(TT), EPS_OUTER)
            normalize(x3, range(TT))
            dve.wait_ge(sig("early_in"), 16)
            dve.wait_ge(sig("q0_ps"), 1)
            ch.link(v.tensor_scalar(q0T, Y[:, :], wt("bq0"), QSCALE, ALU.add, ALU.mult))
            local(0, iter(()), pace_local)
            stages = small_stages(0)
            local(1, stages, pace_local)
            finish(stages)
            first = linear_stages(0)
            full(small_stages(1), first)
            last_stages(first, linear_stages(1))

            v.tensor_copy(tok3(slotbc), m4[7].unsqueeze(2).broadcast_to([P, TT, P])).then_inc(sig("slotbc_ready"), 1)
            dve.wait_ge(sig("buf_ps"), 1)
            v.tensor_copy(bufT[:, 0:HS], bank[4][:, 0:HS]).then_inc(sig("buf_a_ready"), 1)
            dve.wait_ge(sig("moeb_in"), 16)
            for g in range(4):
                dve.wait_ge(sig("hm_ps"), g + 1)
                v.tensor_tensor(hmoe[:, 512 * g:512 * (g + 1)], bank[g][:, :], b1e[:, 512 * g:512 * (g + 1)],
                                ALU.add).then_inc(sig("hm_ready"), 1)
            dve.wait_ge(sig("slotT_ps"), 1)
            for g in range(4):
                v.tensor_scalar(comb[:, 512 * g:512 * (g + 1)], bank[5][:, :], wt("slot_row")[:, g:g + 1], None,
                                ALU.is_equal).then_inc(sig("comb_ready"), 1)
            for g in range(4):
                k = slice(P * g, P * (g + 1))
                dve.wait_ge(sig("y_ps"), g + 1)
                v.tensor_tensor(ymoe[:, k], bank[YB[g]][:, 0:P], b2e[:, k], ALU.add).then_inc(sig("y_ready"), 1)
            for t in range(TT):
                dve.wait_ge(sig("comb_ps"), t + 1)
                v.scalar_tensor_tensor(tok3(outt)[:, t, :], bank[OB[t]][:, 0:P], m4[3][:, t:t + 1], x3[:, t, :],
                                       ALU.mult, ALU.add).then_inc(sig("out_ready"), 1)

        @block.tensor
        def _(pe):
            mm = nc.tensor.matmul
            ready, turned = [0], [0]

            def turn_norm(dst, tiles, *waits):
                for name, n in waits:
                    pe.wait_ge(sig(name), n)
                for i, t in enumerate(tiles):
                    ready[0] += 1
                    pe.wait_ge(sig("xn_ready"), ready[0])
                    last = nc.tensor.transpose(dst[:, P * i:P * (i + 1)], xn3[:, t, :], wt("ident"))
                last.then_inc(sig("lnT_ps"), 1)
                turned[0] += 1

            def wait_norm():
                pe.wait_ge(sig("lnT_ready"), turned[0])

            def project_tokens(dst, srcT, w, tiles=HT):
                for t in range(tiles):
                    last = mm(dst[:, P * t:P * (t + 1)], srcT[:, P * t:P * (t + 1)], w, start=True, stop=True)
                return last

            nproj = [0]

            def projection():
                i = nproj[0]
                nproj[0] += 1
                kind, b = PROJ[i]
                if i == 0:
                    pe.wait_ge(sig("ctx_in0"), 16)
                if kind == "v":
                    pe.wait_ge(sig("late_in"), 16)
                if i >= 2:
                    name, n = taker(i - 2)
                    pe.wait_ge(sig(name), n)
                dst = bank[3 + i % 2]
                if kind == "k":
                    last = mm(dst[:, :], wt("wk1"), ctx[:, KEYS * b:KEYS * (b + 1)], start=True, stop=True)
                else:
                    for k in range(KT):
                        at = KEYS * b + P * k
                        last = mm(dst[:, P * k:P * (k + 1)], ctx[:, at:at + P], wt("wv1"), start=True, stop=True)
                last.then_inc(sig("proj_done"), 1)

            def local(h, stages, pace):
                step = 0

                def headsum(n):
                    for c in range(4 * n, 4 * n + 4):
                        pe.wait_ge(sig("prod_ready"), c + 1)
                        r = 32 * (c % 4)
                        last = mm(bank[2][r:r + 32, :], wt("headsum")[:, 32 * (n % 2):32 * (n % 2) + 32], prod[c % HB],
                                  start=(n % 2 == 0), stop=(n % 2 == 1), skip_group_check=True)
                    last.then_inc(sig("s0_ps"), 1)

                def values(c):
                    if c % HB < 2:
                        pe.wait_ge(sig("prod_ready"), HB * (h + 1))
                    else:
                        pe.wait_ge(sig("v0_ready"), c - 1)
                    mm(bank[c % 2][:, :], wt("wv0"), ctx[:, KEYS * c:KEYS * (c + 1)], start=True, stop=True).then_inc(sig("v0_ps"), 1)

                def spread(c):
                    if c % HB < 2:
                        pe.wait_ge(sig("p0_ready"), h + 1)
                        pe.wait_ge(sig("proj_out"), nproj[0])
                    else:
                        pe.wait_ge(sig("vp_ready"), c - 1)
                    if c == 0:
                        pe.wait_ge(sig("hspread_ready"), 4)
                    k = (c // 4) % 2
                    mm(bank[3 + c % 2][:, :], hspread[c % 4][:, P * k:P * (k + 1)], e0,
                       start=True, stop=True).then_inc(sig("p0_spread"), 1)

                for c in range(HB * h, HB * (h + 1)):
                    if h:
                        if c == HB:
                            pe.wait_ge(sig("vp_ready"), HB)
                        projection()
                    if c in PIECES:
                        pe.wait_ge(sig(f"ctx_in{PIECES.index(c)}"), 16)
                    if c % HB >= 2:
                        pe.wait_ge(sig("prod_ready"), c - 1)
                    elif h:
                        pe.wait_ge(sig("v0_ready"), HB)
                    mm(bank[c % 2][:, :], wt("wk0"), ctx[:, KEYS * c:KEYS * (c + 1)], start=True, stop=True).then_inc(sig("k0_ps"), 1)
                    if c % HB == 5:
                        headsum(2 * h)
                    advance(stages, pace(step))
                    step += 1
                headsum(2 * h + 1)
                values(HB * h)
                values(HB * h + 1)
                for _ in range(GAP):
                    projection()
                advance(stages, pace(step))
                step += 1
                for c in range(HB * h, HB * (h + 1)):
                    spread(c)
                    if c + 2 < HB * (h + 1):
                        values(c + 2)
                    advance(stages, pace(step))
                    step += 1
                if h:
                    pe.wait_ge(sig("vp_ready"), BATCH)
                    while nproj[0] < len(PROJ):
                        projection()
                        advance(stages, pace(step))
                        step += 1

            def small_stages(h):
                tiles, c = tiles_of(h), cols(h)
                pe.wait_ge(sig("o0_ready"), HB * (h + 1))
                project_tokens(Z, o0T[:, c], wt("wo0")).then_inc(sig("xo_ps"), 1)
                yield
                yield
                yield
                turn_norm(X, tiles)
                yield
                yield
                for n, src in enumerate((xk, xv, xr)):
                    pe.wait_ge(sig("mix_ready"), 3 * h + n + 1)
                    if n == 0:
                        wait_norm()
                    dst = (X[:, 0:HTOK], X[:, HTOK:], Y[:, 0:HTOK])[n]
                    mm(dst, wt(("rk", "rv", "rr")[n]), src, start=True, stop=True).then_inc(sig("rkvr_ps"), 1)
                yield
                yield
                yield
                yield
                yield
                yield
                yield
                pe.wait_ge(sig("rw_ready"), h + 1)
                project_tokens(Z, num, wt("ro")).then_inc(sig("xo_ps"), 1)
                yield
                yield
                yield
                turn_norm(X, tiles, ("v_out", h + 1))
                yield
                wait_norm()
                for t in range(HT):
                    last = mm(Z[:, E0 * t:E0 * (t + 1)], lnT[:, c][:, P * t:P * (t + 1)], wt("route"), start=True, stop=True)
                last.then_inc(sig("route_ps"), 1)
                for n in range(4):
                    last = mm((X, Y)[n // 2][:, HTOK * (n % 2):HTOK * (n % 2 + 1)], wt("rw1")[:, P * n:P * (n + 1)], lnT[:, c],
                              start=True, stop=True)
                    if n % 2:
                        last.then_inc(sig("hid_ps"), 1)
                yield
                pe.wait_ge(sig("abs_ready"), h + 1)
                mm(Z[0:H0, 0:HTOK], wt("sw1"), lnT[:, c], start=True, stop=True).then_inc(sig("hid_ps"), 1)
                yield
                yield
                yield
                pe.wait_ge(sig("cf_ready"), h + 1)
                pe.wait_ge(sig("hid_ready"), 5 * h + 5)
                cf3 = fr[9].rearrange("p (t e) -> p t e", e=E0)
                for t in range(HT):
                    last = nc.tensor.transpose(Z[0:E0, P * t:P * (t + 1)], cf3[:, t, :], wt("ident"))
                last.then_inc(sig("cfT_ps"), 1)
                yield
                pe.wait_ge(sig("cfT_ready"), h + 1)
                for n in range(4):
                    last = mm((X, Y)[n // 2][:, HTOK * (n % 2):HTOK * (n % 2 + 1)], wt("spread", E0)[:, P * n:P * (n + 1)], cfT,
                              start=True, stop=True)
                    if n % 2:
                        last.then_inc(sig("spread_ps"), 1)
                yield
                pe.wait_ge(sig("hsc_ready"), 4 * h + 4)
                for t in range(HT):
                    k = slice(P * t, P * (t + 1))
                    mm(Z[:, k], cfT[:, k], wt("rb2", E0), start=True, stop=False)
                    mm(Z[:, k], hid[4][0:H0, k], wt("sw2", H0), start=False, stop=False)
                    for n in range(4):
                        last = mm(Z[:, k], hid[n][:, k], wt("rw2")[:, P * n:P * (n + 1)], start=False, stop=(n == 3))
                last.then_inc(sig("xo_ps"), 1)
                yield
                yield
                yield
                turn_norm(X, tiles)
                yield
                wait_norm()
                mm(Y[:, 0:HTOK], wt("wq1"), lnT[:, c], start=True, stop=True).then_inc(sig("q1_ps"), 1)
                yield

            def scores(u):
                b, g = divmod(u, GROUPS)
                if u < NS:
                    pe.wait_ge(sig("vp_ready"), BATCH)
                    for i in (len(PROJ) - 2, len(PROJ) - 1):
                        name, n = taker(i)
                        pe.wait_ge(sig(name), n)
                else:
                    pe.wait_ge(sig("s1_min"), u - NS + 1)
                if g == 0:
                    pe.wait_ge(sig("qbd_ready"), b + 1)
                mm(bank[u % NS][:, :], qbd[b % NQ][:, P * g:P * (g + 1)], k1[:, KEYS * b:KEYS * (b + 1)],
                   start=True, stop=True).then_inc(sig("s1_ready"), 1)

            def turn(u):
                pe.wait_ge(sig("p1_ready"), u + 1)
                if u >= NT:
                    j = u - NT
                    pe.wait_ge(sig("pT_odd" if j % 2 else "pT_even"), j // 2 + 1)
                for k in range(KT):
                    last = nc.tensor.transpose(bank[2 + u % NT][:, P * k:P * (k + 1)], sc[u % NSC][:, P * k:P * (k + 1)], wt("ident"))
                last.then_inc(sig("pT_ps"), 1)

            def outputs(b):
                pe.wait_ge(sig("pT_even"), 2 * b + 2)
                pe.wait_ge(sig("pT_odd"), 2 * b + 2)
                if b % 4 == 0 and b >= 4:
                    pe.wait_ge(sig("o1_taken"), b // 4)
                for k in range(KT):
                    for g in range(GROUPS):
                        r = slice(32 * g, 32 * g + 32)
                        last = mm(bank[4][r, P * (b % 4):P * (b % 4 + 1)], vkey[:, b, k, r],
                                  pt[(GROUPS * b + g) % NPT][:, P * k:P * (k + 1)], start=(k == 0), stop=(k == KT - 1),
                                  skip_group_check=True)
                last.then_inc(sig("o1_ready"), 1)

            def full(second, first):
                for u in range(2 * UNITS + LAG):
                    if u < 2 * UNITS:
                        scores(u)
                    if u >= LAG:
                        turn(u - LAG)
                    if u >= OUT and (u - OUT) % GROUPS == 0:
                        outputs((u - OUT) // GROUPS)
                    beside(u, second, first)
                outputs(BATCH - 1)

            def linear_stages(h):
                tiles, c = tiles_of(h), cols(h)
                yield
                for g in range(GROUPS):
                    pe.wait_ge(sig("mg_ready"), GROUPS * h + g + 1)
                    last = mm(X[32 * g:32 * g + 32, 0:HTOK], wt("heads32"), mg[:, HTOK * g:HTOK * (g + 1)], start=True, stop=True,
                              skip_group_check=True)
                last.then_inc(sig("rinv_ps"), 1)
                yield
                yield
                keep_warm(2)
                pe.wait_ge(sig("o1T_ready"), h + 1)
                project_tokens(Y, oT[:, c], wt("wo1")).then_inc(sig("xo_ps"), 1)
                keep_warm(8)
                yield
                yield
                turn_norm(X, tiles)
                keep_warm(2)
                yield
                wait_norm()
                mm(X[:, 0:HTOK], wt("lq"), lnT[:, c], start=True, stop=True)
                project_tokens(X[:, HTOK:], lnT[:, c], wt("lk")).then_inc(sig("qk_ps"), 1)
                for t, dst in enumerate((Y, Z)):
                    last = mm(dst[:, 0:P], lnT[:, c][:, P * t:P * (t + 1)], wt("lv"), start=True, stop=True)
                last.then_inc(sig("vtok_ps"), 1)
                keep_warm(3)
                yield
                pe.wait_ge(sig("kp_ready"), h + 1)
                pe.wait_ge(sig("vb_ready"), h + 1)
                for t in range(HT):
                    last = mm(Y[:, 4 * t:4 * t + 4], kp_tok[:, P * t:P * (t + 1)], wt("batchof"), start=True, stop=True)
                last.then_inc(sig("ksum_ps"), 1)
                for t in range(HT):
                    if t:
                        pe.wait_ge(sig("vb2_ready"), 4 * (h + 1))
                    mm((X, Z)[t][:, :], kp_tok[:, P * t:P * (t + 1)], vb[:, 512 * t:512 * (t + 1)],
                       start=True, stop=True).then_inc(sig("kvs_ps"), 1)
                yield
                yield
                pe.wait_ge(sig("qksum_ready"), h + 1)
                mm(Y[:, 0:HTOK], wt("samehead"), qk, start=True, stop=True).then_inc(sig("den_ps"), 1)
                pe.wait_ge(sig("kvs_ready"), HT * (h + 1))
                for b in range(HB):
                    last = mm(X[:, SEQ * b:SEQ * (b + 1)], kvs[:, P * b:P * (b + 1)], qp[:, SEQ * b:SEQ * (b + 1)],
                              start=True, stop=True)
                last.then_inc(sig("num_ps"), 1)
                keep_warm(2)
                yield
                pe.wait_ge(sig("att_ready"), h + 1)
                project_tokens(Z, att, wt("lo")).then_inc(sig("ao_ps"), 1)
                keep_warm(5)
                yield
                yield
                turn_norm(X, tiles)
                keep_warm(2)
                yield
                wait_norm()
                for n in range(4):
                    last = mm((Y, Z)[n // 2][:, HTOK * (n % 2):HTOK * (n % 2 + 1)], wt("w1")[:, P * n:P * (n + 1)], lnT[:, c],
                              start=True, stop=True)
                    if n % 2:
                        last.then_inc(sig("ffh_ps"), 1)
                yield
                keep_warm(2)
                pe.wait_ge(sig("ffh_ready"), 4 * h + 4)
                for t in range(HT):
                    for n in range(4):
                        last = mm(X[:, P * t:P * (t + 1)], hT[:, HTOK * n + P * t:HTOK * n + P * (t + 1)],
                                  wt("w2")[:, P * n:P * (n + 1)], start=(n == 0), stop=(n == 3))
                last.then_inc(sig("ffo_ps"), 1)
                if h:
                    for j in range(2):
                        dispatch(0, j)
                keep_warm(4)
                yield
                yield
                yield
                turn_norm(X, tiles)
                keep_warm(1)
                yield
                wait_norm()
                for t in tiles:
                    last = mm(Z[:, E1 * t:E1 * (t + 1)], lnT[:, P * t:P * (t + 1)], wt("wg"), start=True, stop=True)
                last.then_inc(sig("gate_ps"), 1)
                keep_warm(7)
                yield
                yield
                yield
                pe.wait_ge(sig("onehot_ready"), h + 1)
                dst = bank[0][:, RE * h:RE * (h + 1)]
                mm(dst, wt("upto"), mr[5][:, RE * h:RE * (h + 1)], start=True, stop=False)
                for back in range(1, HT * (h + 1)):
                    lo = max(RE * h, E1 * back)
                    last = mm(bank[0][:, lo:RE * (h + 1)], wt("ones"), mr[5][:, lo - E1 * back:RE * (h + 1) - E1 * back],
                              start=False, stop=(back == HT * (h + 1) - 1))
                last.then_inc(sig("count_ps"), 1)
                if h:
                    keep_warm(2)
                yield
                yield

            def dispatch(h, j):
                for t in tiles_of(h):
                    pe.wait_ge(sig("disp_ready"), t + 1)
                    last = mm(bank[(4, 3)[j]][:, 0:HS], xn3[:, t, :], disp[t][:, HS * j:HS * (j + 1)],
                              start=(t == 0), stop=(t == TT - 1), skip_group_check=True)
                return last

            def keep_warm(n):
                for _ in range(n if alone[0] else 0):
                    mm(bank[2][:, 0:256], q1T[:, 0:P], q1T[:, 0:256], start=True, stop=True)

            alone = [True]

            pe.wait_ge(sig("blank_ready"), 1)
            keep_warm(7)
            pe.wait_ge(sig("early_in"), 16)
            alone[0] = False
            projection()
            turn_norm(X, range(TT))
            for _ in range(1, PRE):
                projection()
            wait_norm()
            mm(Y[:, :], wt("wq0"), lnT[:, :], start=True, stop=True).then_inc(sig("q0_ps"), 1)
            local(0, iter(()), pace_local)
            stages = small_stages(0)
            local(1, stages, pace_local)
            finish(stages)
            first = linear_stages(0)
            full(small_stages(1), first)
            alone[0] = True
            last_stages(first, linear_stages(1))

            for j in range(2):
                dispatch(1, j).then_inc(sig("buf_ps"), 1)
            pe.wait_ge(sig("w1_in"), 16)
            for g in range(4):
                if g % 2 == 0:
                    pe.wait_ge(sig(("buf_a_ready", "buf_b_ready")[g // 2]), 1)
                for j in range(4):
                    e = 4 * g + j
                    last = mm(bank[g][32 * j:32 * j + 32, :], bufT[:, CAP * e:CAP * (e + 1)], w1e[:, e, :], start=True, stop=True,
                              skip_group_check=True)
                last.then_inc(sig("hm_ps"), 1)
            pe.wait_ge(sig("slotbc_ready"), 1)
            for t in range(TT):
                last = nc.tensor.transpose(X[:, P * t:P * (t + 1)], tok3(slotbc)[:, t, :], wt("ident"))
            last.then_inc(sig("slotT_ps"), 1)
            for g in range(4):
                pe.wait_ge(sig("hm_ready"), g + 1)
                for k in range(4):
                    last = nc.tensor.transpose(bank[g][:, P * k:P * (k + 1)], hmoe[:, 512 * g + P * k:512 * g + P * (k + 1)], wt("ident"))
                last.then_inc(sig("hmT_ps"), 1)
            pe.wait_ge(sig("w2_in"), 16)
            for g in range(4):
                pe.wait_ge(sig("hmT_ready"), g + 1)
                for k in range(4):
                    for j in range(4):
                        at = 512 * g + P * k + CAP * j
                        last = mm(bank[YB[g]][32 * j:32 * j + 32, 0:P], hmoeT[:, at:at + CAP], w2e[:, 4 * g + j, k, :],
                                  start=(k == 0), stop=(k == 3), skip_group_check=True)
                last.then_inc(sig("y_ps"), 1)
            for t in range(TT):
                for g in range(4):
                    if t == 0:
                        pe.wait_ge(sig("comb_ready"), 4)
                        pe.wait_ge(sig("y_ready"), g + 1)
                    last = mm(bank[OB[t]][:, 0:P], comb[:, 512 * g + P * t:512 * g + P * (t + 1)], ymoe[:, P * g:P * (g + 1)],
                              start=(g == 0), stop=(g == 3))
                last.then_inc(sig("comb_ps"), 1)


def constants():
    p, one = np.arange(P), np.float32
    r = p[:, None]
    f = np.arange(P)[None, :]
    out = {
        "ident": r == f,
        "headsum": np.concatenate([(np.arange(32) // 16 == h) & (np.arange(32) % 16 == r // HD) for h in range(2)], 1),
        "headspread": np.concatenate([(r % 32 // 16 == h) & (r % 16 == f // HD) for h in range(2)], 1),
        "spread": np.concatenate([r == 2 * n + f // H0 for n in range(4)], 1),
        "before": np.broadcast_to(np.tril(np.ones((E0, E0)), -1).reshape(1, -1), (P, E0 * E0)),
        "rowblock": r // 32 == np.arange(4)[None, :],
        "own16": r // HD == np.arange(HEADS)[None, :],
        "own4": r // HD % 4 == np.arange(4)[None, :],
        "rows32": r % 32 == np.arange(32)[None, :],
        "heads32": r // 32 == np.arange(32)[None, :] // HD,
        "samehead": r // HD == f // HD,
        "batchof": r // SEQ == np.arange(4)[None, :],
        "iota_e": np.broadcast_to(np.arange(E1)[None, :], (P, E1)),
        "iota_slot": np.broadcast_to(np.arange(SLOTS)[None, :], (P, SLOTS)),
        "slot_row": P * np.arange(4)[None, :] + r,
        "upto": r <= f,
        "ones": np.ones((P, P)),
    }
    return {k: np.ascontiguousarray(v).astype(one) for k, v in out.items()}


def kernel(**inputs):
    import concourse.bacc as bacc
    from concourse.bass_utils import run_bass_kernel_spmd

    a = {k: np.asarray(v) for k, v in inputs.items()}

    def col(name):
        return a[name].reshape(-1, 1)

    def rows(name):
        return np.broadcast_to(a[name].reshape(1, -1), (P, a[name].size))

    def tiles(m):
        return m.reshape(-1, P, m.shape[-1]).transpose(1, 0, 2).reshape(P, -1)

    parts = dict(constants())
    parts.update(
        wq0=a["L0_xattn_Wq"].T, wk0=a["L0_xattn_Wk"].T, wv0=a["L0_xattn_Wv"].T, wo0=a["L0_xattn_Wo"].T,
        bq0=col("L0_xattn_bq"), bk0=col("L0_xattn_bk"), bv0=col("L0_xattn_bv"), bo0=rows("L0_xattn_bo"),
        rk=a["L0_attn_Wk"].T, rv=a["L0_attn_Wv"].T, rr=a["L0_attn_Wr"].T, ro=a["L0_attn_Wo"].T,
        w=col("L0_attn_w"), u=col("L0_attn_u"), mk=col("L0_attn_mix_k"), mv=col("L0_attn_mix_v"), mr=col("L0_attn_mix_r"),
        route=a["L0_ffn_routing_W"].T, eb=rows("L0_ffn_expert_bias"), sw1=a["L0_ffn_sW1"], sb1=col("L0_ffn_sb1"),
        rw1=a["L0_ffn_rW1"].transpose(1, 0, 2).reshape(P, -1), rb1=a["L0_ffn_rb1"].reshape(4, P).T,
        rw2=tiles(a["L0_ffn_rW2"].reshape(E0 * H0, D)), sw2=a["L0_ffn_sW2"], rb2=a["L0_ffn_rb2"], sb2=rows("L0_ffn_sb2"),
        wq1=a["L1_xattn_Wq"], wk1=a["L1_xattn_Wk"], wv1=a["L1_xattn_Wv"], wo1=a["L1_xattn_Wo"],
        bq1=col("L1_xattn_bq"), bk1=col("L1_xattn_bk"), bv1=col("L1_xattn_bv"), bo1=rows("L1_xattn_bo"),
        gamma=col("L1_attn_gamma1"), beta=col("L1_attn_beta1"), lq=a["L1_attn_wq"].reshape(D, D), lk=a["L1_attn_wk"].reshape(D, D),
        lv=a["L1_attn_wv"].reshape(D, D), lo=a["L1_attn_wo"].reshape(D, D), w1=a["L1_attn_w1"],
        b1=a["L1_attn_b1"].reshape(4, P).T, w2=tiles(a["L1_attn_w2"]), b2=rows("L1_attn_b2"),
        wg=a["L1_ffn_Wg"], bg=rows("L1_ffn_bg"),
    )

    def pack(layout):
        out = np.zeros((P, width(layout)), np.float32)
        for name, (lo, hi) in columns(layout).items():
            out[:parts[name].shape[0], lo:hi] = parts[name]
        return out

    def slots(b):
        n = b.shape[1]
        return np.broadcast_to(b.reshape(4, 4, 1, n).transpose(1, 2, 0, 3), (4, CAP, 4, n)).reshape(P, 4 * n)

    arrays = {
        "x": a["x"].reshape(TOK, D),
        "early": pack(EARLY),
        "late": pack(LATE),
        "ctx": a["ctx_1024"].reshape(CTX, D).T,
        "mask": a["mask_Bx1xSxS2_fk0"].transpose(2, 0, 1, 3).reshape(SEQ, CTX),
        "moe_w1": a["L1_ffn_W1"].transpose(1, 0, 2).reshape(D, E1 * H1),
        "moe_w2": a["L1_ffn_W2"].reshape(E1, 4, P, D).transpose(2, 0, 1, 3).reshape(P, E1 * H1),
        "moe_b": np.concatenate([slots(a["L1_ffn_b1"]), slots(a["L1_ffn_b2"])], axis=1),
    }
    arrays = {k: np.ascontiguousarray(v) for k, v in arrays.items()}
    nc = bacc.Bacc("TRN2", target_bir_lowering=False, num_devices=1)
    args = [nc.dram_tensor(k, v.shape, F32, kind="ExternalInput").ap() for k, v in arrays.items()]
    args.append(nc.dram_tensor("out", (TOK, D), F32, kind="ExternalOutput").ap())
    program(nc, *args)
    done = run_bass_kernel_spmd(nc, [arrays], core_ids=[0])
    return done.results[0]["out"].reshape(BATCH, SEQ, D)
```
